# Optimizing a Trainium2 kernel written in Bass

```python
import numpy as np
import jax
import jax.numpy as jnp

def _softmax(x, axis=-1):
    return jax.nn.softmax(x, axis=axis)

def _gelu(x):
    return jax.nn.gelu(x, approximate=True)

def _silu(x):
    return jax.nn.silu(x)

def _sigmoid(x):
    return jax.nn.sigmoid(x)

def _layernorm(x, axis=-1, eps=1e-05):
    m = jnp.mean(x, axis=axis, keepdims=True)
    v = jnp.var(x, axis=axis, keepdims=True)
    return (x - m) / jnp.sqrt(v + eps)

def _scatter_add(tgt, idx, src, axis=0):
    return tgt.at[idx].add(src)

def _segment_sum(src, seg, n):
    return jax.ops.segment_sum(src, seg, n)
kernel_name = 'mk_adaln_ffn_d4_seqx_r8_b45e89'

def setup_inputs(seed: int=0):
    np.random.seed(seed)
    _w = jnp.asarray

    def _rec_inputs():
        import jax
        import jax.numpy as jnp
        _rk = jax.random.key(seed)
        x = -0.000125 + 0.9999 * jax.random.normal(jax.random.fold_in(_rk, 1), (4, 256, 256), jnp.float32)
        _lenS = 256 - jax.random.randint(jax.random.fold_in(_rk, 7), (4,), 0, max(1, 256 // 4) + 1, jnp.int32)
        _lenS2 = 256 - jax.random.randint(jax.random.fold_in(_rk, 8), (4,), 0, max(1, 256 // 4) + 1, jnp.int32)
        fside_BxSxS_0 = -1.52775e-05 + 0.999936 * jax.random.normal(jax.random.fold_in(_rk, 11), (4, 256, 256), jnp.float32)
        cond_512 = -5.03954e-05 + 1.00559 * jax.random.normal(jax.random.fold_in(_rk, 12), (4, 64), jnp.float32)
        return (x, fside_BxSxS_0, cond_512)
    x, fside_BxSxS_0, cond_512 = _rec_inputs()

    def _L0_cond_setup():
        import jax, jax.numpy as jnp
        from jax import lax
        import numpy as np
        B, T, C, TD = (8, 256, 256, 64)

        def _bi_wkv(r, k, v, w, u, time_emb):
            tf = jax.nn.sigmoid(jnp.sum(time_emb, axis=-1))[:, None, None]
            decay = jnp.exp(-jnp.exp(w.astype(jnp.float32)))[None, :] * (0.5 + 0.5 * tf[:, :, 0])
            kf = k.astype(jnp.float32)
            vf = v.astype(jnp.float32)
            ek = jnp.exp(jnp.minimum(kf, 30.0))
            ekv = ek * vf

            def step(carry, x):
                a, b = carry
                ekv_t, ek_t = x
                a = a * decay + ekv_t
                b = b * decay + ek_t
                return ((a, b), (a, b))
            ekv_t = jnp.swapaxes(ekv, 0, 1)
            ek_t = jnp.swapaxes(ek, 0, 1)
            init = (jnp.zeros_like(decay), jnp.zeros_like(decay))
            _, (nf, df) = lax.scan(step, init, (ekv_t, ek_t))
            _, (nb, db) = lax.scan(step, init, (ekv_t, ek_t), reverse=True)
            nf = jnp.swapaxes(nf, 0, 1)
            df = jnp.swapaxes(df, 0, 1)
            nb = jnp.swapaxes(nb, 0, 1)
            db = jnp.swapaxes(db, 0, 1)
            euk = jnp.exp(jnp.minimum(u.astype(jnp.float32)[None, None, :] + kf, 30.0))
            num = nf + nb - ekv + euk * vf
            den = df + db - ek + euk
            base = jax.nn.sigmoid(r.astype(jnp.float32)) * (num / jnp.maximum(den, 1e-08))
            out = base * (0.8 + 0.2 * tf)
            return out.astype(r.dtype)
        key = jax.random.key(seed)
        ks = jax.random.split(key, 6)
        return {'r': jax.random.normal(ks[0], (B, T, C), dtype=jnp.float32), 'k': jax.random.normal(ks[1], (B, T, C), dtype=jnp.float32), 'v': jax.random.normal(ks[2], (B, T, C), dtype=jnp.float32), 'w': jax.random.normal(ks[3], (C,), dtype=jnp.float32), 'u': jax.random.normal(ks[4], (C,), dtype=jnp.float32), 'time_emb': jax.random.normal(ks[5], (B, TD), dtype=jnp.float32)}
    _L0_cond_all = _L0_cond_setup()
    _L0_cond_in = {k: v for k, v in _L0_cond_all.items() if k in ('w', 'u')}
    del _L0_cond_all

    def _L0_ffn_setup():
        import jax, jax.numpy as jnp
        import numpy as np
        H, LAT, INTER, E, G, TOPK_G, TOP_K = (256, 128, 128, 32, 4, 2, 8)
        SHARED_INTER = 512
        ROUTED_SCALE = 2.5
        B, S = (2, 128)

        def relu2(x):
            return jnp.square(jax.nn.relu(x))
        key = jax.random.key(seed)
        ks = jax.random.split(key, 9)
        w = 0.02
        return {'hidden_states': jax.random.normal(ks[0], (B, S, H), jnp.float32), 'gate_w': jax.random.normal(ks[1], (E, H), jnp.float32) * w, 'gate_bias': jax.random.normal(ks[2], (E,), jnp.float32) * w, 'fc1_w': jax.random.normal(ks[3], (LAT, H), jnp.float32) * w, 'fc2_w': jax.random.normal(ks[4], (H, LAT), jnp.float32) * w, 'w1': jax.random.normal(ks[5], (E, INTER, LAT), jnp.float32) * w, 'w2': jax.random.normal(ks[6], (E, LAT, INTER), jnp.float32) * w, 'shared_up_w': jax.random.normal(ks[7], (SHARED_INTER, H), jnp.float32) * w, 'shared_down_w': jax.random.normal(ks[8], (H, SHARED_INTER), jnp.float32) * w}
    _L0_ffn_all = _L0_ffn_setup()
    _L0_ffn_in = {k: v for k, v in _L0_ffn_all.items() if k in ('gate_w', 'gate_bias', 'fc1_w', 'fc2_w', 'w1', 'w2', 'shared_up_w', 'shared_down_w')}
    del _L0_ffn_all

    def _L1_cond_setup():
        import jax, jax.numpy as jnp
        from jax import lax
        import numpy as np
        B, T, C, TD = (8, 256, 256, 64)

        def _bi_wkv(r, k, v, w, u, time_emb):
            tf = jax.nn.sigmoid(jnp.sum(time_emb, axis=-1))[:, None, None]
            decay = jnp.exp(-jnp.exp(w.astype(jnp.float32)))[None, :] * (0.5 + 0.5 * tf[:, :, 0])
            kf = k.astype(jnp.float32)
            vf = v.astype(jnp.float32)
            ek = jnp.exp(jnp.minimum(kf, 30.0))
            ekv = ek * vf

            def step(carry, x):
                a, b = carry
                ekv_t, ek_t = x
                a = a * decay + ekv_t
                b = b * decay + ek_t
                return ((a, b), (a, b))
            ekv_t = jnp.swapaxes(ekv, 0, 1)
            ek_t = jnp.swapaxes(ek, 0, 1)
            init = (jnp.zeros_like(decay), jnp.zeros_like(decay))
            _, (nf, df) = lax.scan(step, init, (ekv_t, ek_t))
            _, (nb, db) = lax.scan(step, init, (ekv_t, ek_t), reverse=True)
            nf = jnp.swapaxes(nf, 0, 1)
            df = jnp.swapaxes(df, 0, 1)
            nb = jnp.swapaxes(nb, 0, 1)
            db = jnp.swapaxes(db, 0, 1)
            euk = jnp.exp(jnp.minimum(u.astype(jnp.float32)[None, None, :] + kf, 30.0))
            num = nf + nb - ekv + euk * vf
            den = df + db - ek + euk
            base = jax.nn.sigmoid(r.astype(jnp.float32)) * (num / jnp.maximum(den, 1e-08))
            out = base * (0.8 + 0.2 * tf)
            return out.astype(r.dtype)
        key = jax.random.key(seed)
        ks = jax.random.split(key, 6)
        return {'r': jax.random.normal(ks[0], (B, T, C), dtype=jnp.float32), 'k': jax.random.normal(ks[1], (B, T, C), dtype=jnp.float32), 'v': jax.random.normal(ks[2], (B, T, C), dtype=jnp.float32), 'w': jax.random.normal(ks[3], (C,), dtype=jnp.float32), 'u': jax.random.normal(ks[4], (C,), dtype=jnp.float32), 'time_emb': jax.random.normal(ks[5], (B, TD), dtype=jnp.float32)}
    _L1_cond_all = _L1_cond_setup()
    _L1_cond_in = {k: v for k, v in _L1_cond_all.items() if k in ('w', 'u')}
    del _L1_cond_all

    def _L1_ffn_setup():
        import jax, jax.numpy as jnp
        import numpy as np
        Q = 127.0

        def _round_ste(v):
            return v + jax.lax.stop_gradient(jnp.round(v) - v)

        def quantize_rowwise(x):
            absmax = jnp.max(jnp.abs(x), axis=1, keepdims=True)
            q = jnp.clip(_round_ste(x * (Q / absmax)), -Q, Q)
            return (q, absmax)

        def quantize_global(w):
            absmax = jnp.max(jnp.abs(w))
            q = jnp.clip(_round_ste(w * (Q / absmax)), -Q, Q)
            return (q, absmax)

        def int8_matmul_dequant_bias(a_q, b_q_t, state_a, state_b, bias):
            acc = jnp.matmul(a_q, b_q_t)
            return acc * (state_a * state_b / (Q * Q)) + bias
        key = jax.random.key(seed)
        k1, k2, k3, k4, k5 = jax.random.split(key, 5)
        B, S, D, H = (4, 256, 256, 1024)
        x = jax.random.normal(k1, (B, S, D), dtype=jnp.float32)
        W1 = jax.random.normal(k2, (H, D), dtype=jnp.float32) * (1.0 / np.sqrt(D))
        B1 = jax.random.normal(k3, (H,), dtype=jnp.float32) * 0.02
        W2 = jax.random.normal(k4, (D, H), dtype=jnp.float32) * (1.0 / np.sqrt(H))
        B2 = jax.random.normal(k5, (D,), dtype=jnp.float32) * 0.02
        return {'x': x, 'W1': W1, 'B1': B1, 'W2': W2, 'B2': B2}
    _L1_ffn_all = _L1_ffn_setup()
    _L1_ffn_in = {k: v for k, v in _L1_ffn_all.items() if k in ('W1', 'B1', 'W2', 'B2')}
    del _L1_ffn_all

    def _L2_cond_setup():
        import jax, jax.numpy as jnp
        from jax import lax
        import numpy as np
        B, T, C, TD = (8, 256, 256, 64)

        def _bi_wkv(r, k, v, w, u, time_emb):
            tf = jax.nn.sigmoid(jnp.sum(time_emb, axis=-1))[:, None, None]
            decay = jnp.exp(-jnp.exp(w.astype(jnp.float32)))[None, :] * (0.5 + 0.5 * tf[:, :, 0])
            kf = k.astype(jnp.float32)
            vf = v.astype(jnp.float32)
            ek = jnp.exp(jnp.minimum(kf, 30.0))
            ekv = ek * vf

            def step(carry, x):
                a, b = carry
                ekv_t, ek_t = x
                a = a * decay + ekv_t
                b = b * decay + ek_t
                return ((a, b), (a, b))
            ekv_t = jnp.swapaxes(ekv, 0, 1)
            ek_t = jnp.swapaxes(ek, 0, 1)
            init = (jnp.zeros_like(decay), jnp.zeros_like(decay))
            _, (nf, df) = lax.scan(step, init, (ekv_t, ek_t))
            _, (nb, db) = lax.scan(step, init, (ekv_t, ek_t), reverse=True)
            nf = jnp.swapaxes(nf, 0, 1)
            df = jnp.swapaxes(df, 0, 1)
            nb = jnp.swapaxes(nb, 0, 1)
            db = jnp.swapaxes(db, 0, 1)
            euk = jnp.exp(jnp.minimum(u.astype(jnp.float32)[None, None, :] + kf, 30.0))
            num = nf + nb - ekv + euk * vf
            den = df + db - ek + euk
            base = jax.nn.sigmoid(r.astype(jnp.float32)) * (num / jnp.maximum(den, 1e-08))
            out = base * (0.8 + 0.2 * tf)
            return out.astype(r.dtype)
        key = jax.random.key(seed)
        ks = jax.random.split(key, 6)
        return {'r': jax.random.normal(ks[0], (B, T, C), dtype=jnp.float32), 'k': jax.random.normal(ks[1], (B, T, C), dtype=jnp.float32), 'v': jax.random.normal(ks[2], (B, T, C), dtype=jnp.float32), 'w': jax.random.normal(ks[3], (C,), dtype=jnp.float32), 'u': jax.random.normal(ks[4], (C,), dtype=jnp.float32), 'time_emb': jax.random.normal(ks[5], (B, TD), dtype=jnp.float32)}
    _L2_cond_all = _L2_cond_setup()
    _L2_cond_in = {k: v for k, v in _L2_cond_all.items() if k in ('w', 'u')}
    del _L2_cond_all

    def _L2_ffn_setup():
        import jax, jax.numpy as jnp
        import numpy as np
        B, S, H, I, E, K = (4, 256, 256, 512, 8, 2)
        key = jax.random.key(seed)
        k1, k2, k3, k4 = jax.random.split(key, 4)
        return {'hidden_states': jax.random.normal(k1, (B, S, H), dtype=jnp.float32), 'gate_weight': jax.random.normal(k2, (E, H), dtype=jnp.float32) * 0.02, 'gate_up_proj': jax.random.normal(k3, (E, 2 * I, H), dtype=jnp.float32) * 0.02, 'down_proj': jax.random.normal(k4, (E, H, I), dtype=jnp.float32) * 0.02}
    _L2_ffn_all = _L2_ffn_setup()
    _L2_ffn_in = {k: v for k, v in _L2_ffn_all.items() if k in ('gate_weight', 'gate_up_proj', 'down_proj')}
    del _L2_ffn_all

    def _L3_cond_setup():
        import jax, jax.numpy as jnp
        from jax import lax
        import numpy as np
        B, T, C, TD = (8, 256, 256, 64)

        def _bi_wkv(r, k, v, w, u, time_emb):
            tf = jax.nn.sigmoid(jnp.sum(time_emb, axis=-1))[:, None, None]
            decay = jnp.exp(-jnp.exp(w.astype(jnp.float32)))[None, :] * (0.5 + 0.5 * tf[:, :, 0])
            kf = k.astype(jnp.float32)
            vf = v.astype(jnp.float32)
            ek = jnp.exp(jnp.minimum(kf, 30.0))
            ekv = ek * vf

            def step(carry, x):
                a, b = carry
                ekv_t, ek_t = x
                a = a * decay + ekv_t
                b = b * decay + ek_t
                return ((a, b), (a, b))
            ekv_t = jnp.swapaxes(ekv, 0, 1)
            ek_t = jnp.swapaxes(ek, 0, 1)
            init = (jnp.zeros_like(decay), jnp.zeros_like(decay))
            _, (nf, df) = lax.scan(step, init, (ekv_t, ek_t))
            _, (nb, db) = lax.scan(step, init, (ekv_t, ek_t), reverse=True)
            nf = jnp.swapaxes(nf, 0, 1)
            df = jnp.swapaxes(df, 0, 1)
            nb = jnp.swapaxes(nb, 0, 1)
            db = jnp.swapaxes(db, 0, 1)
            euk = jnp.exp(jnp.minimum(u.astype(jnp.float32)[None, None, :] + kf, 30.0))
            num = nf + nb - ekv + euk * vf
            den = df + db - ek + euk
            base = jax.nn.sigmoid(r.astype(jnp.float32)) * (num / jnp.maximum(den, 1e-08))
            out = base * (0.8 + 0.2 * tf)
            return out.astype(r.dtype)
        key = jax.random.key(seed)
        ks = jax.random.split(key, 6)
        return {'r': jax.random.normal(ks[0], (B, T, C), dtype=jnp.float32), 'k': jax.random.normal(ks[1], (B, T, C), dtype=jnp.float32), 'v': jax.random.normal(ks[2], (B, T, C), dtype=jnp.float32), 'w': jax.random.normal(ks[3], (C,), dtype=jnp.float32), 'u': jax.random.normal(ks[4], (C,), dtype=jnp.float32), 'time_emb': jax.random.normal(ks[5], (B, TD), dtype=jnp.float32)}
    _L3_cond_all = _L3_cond_setup()
    _L3_cond_in = {k: v for k, v in _L3_cond_all.items() if k in ('w', 'u')}
    del _L3_cond_all

    def _L3_ffn_setup():
        import jax, jax.numpy as jnp
        import numpy as np
        N_EMBD = 256
        D_FF = 4 * N_EMBD
        BATCH, SEQ = (4, 256)
        EPS = 1e-05

        def rmsnorm(x):
            return x * jax.lax.rsqrt(jnp.mean(x * x, axis=-1, keepdims=True) + 1e-06)

        def activation_quant(x):
            scale = 127.0 / jnp.clip(jnp.max(jnp.abs(x), axis=-1, keepdims=True), EPS, None)
            return jnp.clip(jnp.round(x * scale), -128, 127) / scale

        def weight_quant(w):
            scale = 1.0 / jnp.clip(jnp.mean(jnp.abs(w)), EPS, None)
            return jnp.clip(jnp.round(w * scale), -1, 1) / scale

        def bitlinear(x, w):
            xn = rmsnorm(x)
            xq = xn + jax.lax.stop_gradient(activation_quant(xn) - xn)
            wq = w + jax.lax.stop_gradient(weight_quant(w) - w)
            return jnp.einsum('bsi,oi->bso', xq, wq)
        key = jax.random.key(seed)
        k0, k1, k2, k3 = jax.random.split(key, 4)
        x = jax.random.normal(k0, (BATCH, SEQ, N_EMBD), dtype=jnp.float32)
        s_in = 1.0 / np.sqrt(N_EMBD)
        s_ff = 1.0 / np.sqrt(D_FF)
        w1 = jax.random.normal(k1, (D_FF, N_EMBD), dtype=jnp.float32) * s_in
        w2 = jax.random.normal(k2, (D_FF, N_EMBD), dtype=jnp.float32) * s_in
        w3 = jax.random.normal(k3, (N_EMBD, D_FF), dtype=jnp.float32) * s_ff
        return {'x': x, 'w1': w1, 'w2': w2, 'w3': w3}
    _L3_ffn_all = _L3_ffn_setup()
    _L3_ffn_in = {k: v for k, v in _L3_ffn_all.items() if k in ('w1', 'w2', 'w3')}
    del _L3_ffn_all
    return {'x': x, 'fside_BxSxS_0': fside_BxSxS_0, 'cond_512': cond_512, 'L0_cond_w': _L0_cond_in['w'], 'L0_cond_u': _L0_cond_in['u'], 'L0_ffn_gate_w': _L0_ffn_in['gate_w'], 'L0_ffn_gate_bias': _L0_ffn_in['gate_bias'], 'L0_ffn_fc1_w': _L0_ffn_in['fc1_w'], 'L0_ffn_fc2_w': _L0_ffn_in['fc2_w'], 'L0_ffn_w1': _L0_ffn_in['w1'], 'L0_ffn_w2': _L0_ffn_in['w2'], 'L0_ffn_shared_up_w': _L0_ffn_in['shared_up_w'], 'L0_ffn_shared_down_w': _L0_ffn_in['shared_down_w'], 'L1_cond_w': _L1_cond_in['w'], 'L1_cond_u': _L1_cond_in['u'], 'L1_ffn_W1': _L1_ffn_in['W1'], 'L1_ffn_B1': _L1_ffn_in['B1'], 'L1_ffn_W2': _L1_ffn_in['W2'], 'L1_ffn_B2': _L1_ffn_in['B2'], 'L2_cond_w': _L2_cond_in['w'], 'L2_cond_u': _L2_cond_in['u'], 'L2_ffn_gate_weight': _L2_ffn_in['gate_weight'], 'L2_ffn_gate_up_proj': _L2_ffn_in['gate_up_proj'], 'L2_ffn_down_proj': _L2_ffn_in['down_proj'], 'L3_cond_w': _L3_cond_in['w'], 'L3_cond_u': _L3_cond_in['u'], 'L3_ffn_w1': _L3_ffn_in['w1'], 'L3_ffn_w2': _L3_ffn_in['w2'], 'L3_ffn_w3': _L3_ffn_in['w3']}

def reference(x, fside_BxSxS_0, cond_512, L0_cond_w, L0_cond_u, L0_ffn_gate_w, L0_ffn_gate_bias, L0_ffn_fc1_w, L0_ffn_fc2_w, L0_ffn_w1, L0_ffn_w2, L0_ffn_shared_up_w, L0_ffn_shared_down_w, L1_cond_w, L1_cond_u, L1_ffn_W1, L1_ffn_B1, L1_ffn_W2, L1_ffn_B2, L2_cond_w, L2_cond_u, L2_ffn_gate_weight, L2_ffn_gate_up_proj, L2_ffn_down_proj, L3_cond_w, L3_cond_u, L3_ffn_w1, L3_ffn_w2, L3_ffn_w3):
    import jax
    import jax.numpy as jnp

    def _L0_cond_ref(r, k, v, w, u, time_emb):
        import jax, jax.numpy as jnp
        from jax import lax
        import numpy as np
        B, T, C, TD = (8, 256, 256, 64)

        def _bi_wkv(r, k, v, w, u, time_emb):
            tf = jax.nn.sigmoid(jnp.sum(time_emb, axis=-1))[:, None, None]
            decay = jnp.exp(-jnp.exp(w.astype(jnp.float32)))[None, :] * (0.5 + 0.5 * tf[:, :, 0])
            kf = k.astype(jnp.float32)
            vf = v.astype(jnp.float32)
            ek = jnp.exp(jnp.minimum(kf, 30.0))
            ekv = ek * vf

            def step(carry, x):
                a, b = carry
                ekv_t, ek_t = x
                a = a * decay + ekv_t
                b = b * decay + ek_t
                return ((a, b), (a, b))
            ekv_t = jnp.swapaxes(ekv, 0, 1)
            ek_t = jnp.swapaxes(ek, 0, 1)
            init = (jnp.zeros_like(decay), jnp.zeros_like(decay))
            _, (nf, df) = lax.scan(step, init, (ekv_t, ek_t))
            _, (nb, db) = lax.scan(step, init, (ekv_t, ek_t), reverse=True)
            nf = jnp.swapaxes(nf, 0, 1)
            df = jnp.swapaxes(df, 0, 1)
            nb = jnp.swapaxes(nb, 0, 1)
            db = jnp.swapaxes(db, 0, 1)
            euk = jnp.exp(jnp.minimum(u.astype(jnp.float32)[None, None, :] + kf, 30.0))
            num = nf + nb - ekv + euk * vf
            den = df + db - ek + euk
            base = jax.nn.sigmoid(r.astype(jnp.float32)) * (num / jnp.maximum(den, 1e-08))
            out = base * (0.8 + 0.2 * tf)
            return out.astype(r.dtype)
        return _bi_wkv(r, k, v, w, u, time_emb)

    def _L0_ffn_ref(hidden_states, gate_w, gate_bias, fc1_w, fc2_w, w1, w2, shared_up_w, shared_down_w):
        import jax, jax.numpy as jnp
        import numpy as np
        H, LAT, INTER, E, G, TOPK_G, TOP_K = (256, 128, 128, 32, 4, 2, 8)
        SHARED_INTER = 512
        ROUTED_SCALE = 2.5
        B, S = (2, 128)

        def relu2(x):
            return jnp.square(jax.nn.relu(x))
        orig_shape = hidden_states.shape
        x = hidden_states.reshape(-1, H)
        T = x.shape[0]
        logits = jnp.einsum('th,eh->te', x.astype(jnp.float32), gate_w)
        scores = jax.nn.sigmoid(logits)
        sb = scores + gate_bias
        grp = sb.reshape(T, G, E // G)
        group_scores = jax.lax.top_k(grp, 2)[0].sum(-1)
        _, gidx = jax.lax.top_k(group_scores, TOPK_G)
        gmask = jax.nn.one_hot(gidx, G, dtype=sb.dtype).sum(1)
        masked = jnp.where(gmask[:, :, None] > 0, grp, -jnp.inf).reshape(T, E)
        _, topi = jax.lax.top_k(masked, TOP_K)
        wsel = jnp.take_along_axis(scores, topi, axis=1)
        wsel = wsel / wsel.sum(-1, keepdims=True) * ROUTED_SCALE
        cw = jnp.zeros((T, E), jnp.float32).at[jnp.arange(T)[:, None], topi].add(wsel)
        x_lat = x @ fc1_w.T
        h = relu2(jnp.einsum('tl,eil->eti', x_lat, w1))
        h = h * cw.T[:, :, None]
        y_lat = jnp.einsum('eti,eli->tl', h, w2)
        routed = y_lat @ fc2_w.T
        shared = relu2(x @ shared_up_w.T) @ shared_down_w.T
        return (shared + routed).reshape(orig_shape)

    def _L1_cond_ref(r, k, v, w, u, time_emb):
        import jax, jax.numpy as jnp
        from jax import lax
        import numpy as np
        B, T, C, TD = (8, 256, 256, 64)

        def _bi_wkv(r, k, v, w, u, time_emb):
            tf = jax.nn.sigmoid(jnp.sum(time_emb, axis=-1))[:, None, None]
            decay = jnp.exp(-jnp.exp(w.astype(jnp.float32)))[None, :] * (0.5 + 0.5 * tf[:, :, 0])
            kf = k.astype(jnp.float32)
            vf = v.astype(jnp.float32)
            ek = jnp.exp(jnp.minimum(kf, 30.0))
            ekv = ek * vf

            def step(carry, x):
                a, b = carry
                ekv_t, ek_t = x
                a = a * decay + ekv_t
                b = b * decay + ek_t
                return ((a, b), (a, b))
            ekv_t = jnp.swapaxes(ekv, 0, 1)
            ek_t = jnp.swapaxes(ek, 0, 1)
            init = (jnp.zeros_like(decay), jnp.zeros_like(decay))
            _, (nf, df) = lax.scan(step, init, (ekv_t, ek_t))
            _, (nb, db) = lax.scan(step, init, (ekv_t, ek_t), reverse=True)
            nf = jnp.swapaxes(nf, 0, 1)
            df = jnp.swapaxes(df, 0, 1)
            nb = jnp.swapaxes(nb, 0, 1)
            db = jnp.swapaxes(db, 0, 1)
            euk = jnp.exp(jnp.minimum(u.astype(jnp.float32)[None, None, :] + kf, 30.0))
            num = nf + nb - ekv + euk * vf
            den = df + db - ek + euk
            base = jax.nn.sigmoid(r.astype(jnp.float32)) * (num / jnp.maximum(den, 1e-08))
            out = base * (0.8 + 0.2 * tf)
            return out.astype(r.dtype)
        return _bi_wkv(r, k, v, w, u, time_emb)

    def _L1_ffn_ref(x, W1, B1, W2, B2):
        import jax, jax.numpy as jnp
        import numpy as np
        Q = 127.0

        def _round_ste(v):
            return v + jax.lax.stop_gradient(jnp.round(v) - v)

        def quantize_rowwise(x):
            absmax = jnp.max(jnp.abs(x), axis=1, keepdims=True)
            q = jnp.clip(_round_ste(x * (Q / absmax)), -Q, Q)
            return (q, absmax)

        def quantize_global(w):
            absmax = jnp.max(jnp.abs(w))
            q = jnp.clip(_round_ste(w * (Q / absmax)), -Q, Q)
            return (q, absmax)

        def int8_matmul_dequant_bias(a_q, b_q_t, state_a, state_b, bias):
            acc = jnp.matmul(a_q, b_q_t)
            return acc * (state_a * state_b / (Q * Q)) + bias
        X1 = x.reshape(-1, x.shape[-1])
        X1_q, sX1 = quantize_rowwise(X1)
        W1_q, sW1 = quantize_global(W1)
        X2_pre = int8_matmul_dequant_bias(X1_q, W1_q.T, sX1, sW1, B1)
        X2 = jax.nn.gelu(X2_pre, approximate=True)
        X2_q, sX2 = quantize_rowwise(X2)
        W2_q, sW2 = quantize_global(W2)
        out = int8_matmul_dequant_bias(X2_q, W2_q.T, sX2, sW2, B2)
        return out.reshape(*x.shape[:-1], -1)

    def _L2_cond_ref(r, k, v, w, u, time_emb):
        import jax, jax.numpy as jnp
        from jax import lax
        import numpy as np
        B, T, C, TD = (8, 256, 256, 64)

        def _bi_wkv(r, k, v, w, u, time_emb):
            tf = jax.nn.sigmoid(jnp.sum(time_emb, axis=-1))[:, None, None]
            decay = jnp.exp(-jnp.exp(w.astype(jnp.float32)))[None, :] * (0.5 + 0.5 * tf[:, :, 0])
            kf = k.astype(jnp.float32)
            vf = v.astype(jnp.float32)
            ek = jnp.exp(jnp.minimum(kf, 30.0))
            ekv = ek * vf

            def step(carry, x):
                a, b = carry
                ekv_t, ek_t = x
                a = a * decay + ekv_t
                b = b * decay + ek_t
                return ((a, b), (a, b))
            ekv_t = jnp.swapaxes(ekv, 0, 1)
            ek_t = jnp.swapaxes(ek, 0, 1)
            init = (jnp.zeros_like(decay), jnp.zeros_like(decay))
            _, (nf, df) = lax.scan(step, init, (ekv_t, ek_t))
            _, (nb, db) = lax.scan(step, init, (ekv_t, ek_t), reverse=True)
            nf = jnp.swapaxes(nf, 0, 1)
            df = jnp.swapaxes(df, 0, 1)
            nb = jnp.swapaxes(nb, 0, 1)
            db = jnp.swapaxes(db, 0, 1)
            euk = jnp.exp(jnp.minimum(u.astype(jnp.float32)[None, None, :] + kf, 30.0))
            num = nf + nb - ekv + euk * vf
            den = df + db - ek + euk
            base = jax.nn.sigmoid(r.astype(jnp.float32)) * (num / jnp.maximum(den, 1e-08))
            out = base * (0.8 + 0.2 * tf)
            return out.astype(r.dtype)
        return _bi_wkv(r, k, v, w, u, time_emb)

    def _L2_ffn_ref(hidden_states, gate_weight, gate_up_proj, down_proj):
        import jax, jax.numpy as jnp
        import numpy as np
        B, S, H, I, E, K = (4, 256, 256, 512, 8, 2)
        b, s, h = hidden_states.shape
        num_experts, top_k = (gate_weight.shape[0], K)
        x = hidden_states.reshape(-1, h)
        router_logits = x @ gate_weight.T
        probs = jax.nn.softmax(router_logits.astype(jnp.float32), axis=-1)
        top_v, top_i = jax.lax.top_k(probs, top_k)
        top_v = top_v / top_v.sum(axis=-1, keepdims=True)
        combine_w = jnp.einsum('tke,tk->te', jax.nn.one_hot(top_i, num_experts, dtype=top_v.dtype), top_v).astype(x.dtype)

        def expert_step(acc, inp):
            gu, dp, w = inp
            gate, up = jnp.split(x @ gu.T, 2, axis=-1)
            hidden = jax.nn.silu(gate) * up
            y = hidden @ dp.T
            return (acc + w[:, None] * y, None)
        out, _ = jax.lax.scan(expert_step, jnp.zeros_like(x), (gate_up_proj, down_proj, combine_w.T))
        return out.reshape(b, s, h)

    def _L3_cond_ref(r, k, v, w, u, time_emb):
        import jax, jax.numpy as jnp
        from jax import lax
        import numpy as np
        B, T, C, TD = (8, 256, 256, 64)

        def _bi_wkv(r, k, v, w, u, time_emb):
            tf = jax.nn.sigmoid(jnp.sum(time_emb, axis=-1))[:, None, None]
            decay = jnp.exp(-jnp.exp(w.astype(jnp.float32)))[None, :] * (0.5 + 0.5 * tf[:, :, 0])
            kf = k.astype(jnp.float32)
            vf = v.astype(jnp.float32)
            ek = jnp.exp(jnp.minimum(kf, 30.0))
            ekv = ek * vf

            def step(carry, x):
                a, b = carry
                ekv_t, ek_t = x
                a = a * decay + ekv_t
                b = b * decay + ek_t
                return ((a, b), (a, b))
            ekv_t = jnp.swapaxes(ekv, 0, 1)
            ek_t = jnp.swapaxes(ek, 0, 1)
            init = (jnp.zeros_like(decay), jnp.zeros_like(decay))
            _, (nf, df) = lax.scan(step, init, (ekv_t, ek_t))
            _, (nb, db) = lax.scan(step, init, (ekv_t, ek_t), reverse=True)
            nf = jnp.swapaxes(nf, 0, 1)
            df = jnp.swapaxes(df, 0, 1)
            nb = jnp.swapaxes(nb, 0, 1)
            db = jnp.swapaxes(db, 0, 1)
            euk = jnp.exp(jnp.minimum(u.astype(jnp.float32)[None, None, :] + kf, 30.0))
            num = nf + nb - ekv + euk * vf
            den = df + db - ek + euk
            base = jax.nn.sigmoid(r.astype(jnp.float32)) * (num / jnp.maximum(den, 1e-08))
            out = base * (0.8 + 0.2 * tf)
            return out.astype(r.dtype)
        return _bi_wkv(r, k, v, w, u, time_emb)

    def _L3_ffn_ref(x, w1, w2, w3):
        import jax, jax.numpy as jnp
        import numpy as np
        N_EMBD = 256
        D_FF = 4 * N_EMBD
        BATCH, SEQ = (4, 256)
        EPS = 1e-05

        def rmsnorm(x):
            return x * jax.lax.rsqrt(jnp.mean(x * x, axis=-1, keepdims=True) + 1e-06)

        def activation_quant(x):
            scale = 127.0 / jnp.clip(jnp.max(jnp.abs(x), axis=-1, keepdims=True), EPS, None)
            return jnp.clip(jnp.round(x * scale), -128, 127) / scale

        def weight_quant(w):
            scale = 1.0 / jnp.clip(jnp.mean(jnp.abs(w)), EPS, None)
            return jnp.clip(jnp.round(w * scale), -1, 1) / scale

        def bitlinear(x, w):
            xn = rmsnorm(x)
            xq = xn + jax.lax.stop_gradient(activation_quant(xn) - xn)
            wq = w + jax.lax.stop_gradient(weight_quant(w) - w)
            return jnp.einsum('bsi,oi->bso', xq, wq)
        h = jax.nn.silu(bitlinear(x, w1)) * bitlinear(x, w2)
        return bitlinear(h, w3)
    x = x + _L0_ffn_ref(_L0_cond_ref(x, fside_BxSxS_0, fside_BxSxS_0, L0_cond_w, L0_cond_u, cond_512), L0_ffn_gate_w, L0_ffn_gate_bias, L0_ffn_fc1_w, L0_ffn_fc2_w, L0_ffn_w1, L0_ffn_w2, L0_ffn_shared_up_w, L0_ffn_shared_down_w)
    x = x + _L1_ffn_ref(_L1_cond_ref(x, fside_BxSxS_0, fside_BxSxS_0, L1_cond_w, L1_cond_u, cond_512), L1_ffn_W1, L1_ffn_B1, L1_ffn_W2, L1_ffn_B2)
    x = x + _L2_ffn_ref(_L2_cond_ref(x, fside_BxSxS_0, fside_BxSxS_0, L2_cond_w, L2_cond_u, cond_512), L2_ffn_gate_weight, L2_ffn_gate_up_proj, L2_ffn_down_proj)
    x = x + _L3_ffn_ref(_L3_cond_ref(x, fside_BxSxS_0, fside_BxSxS_0, L3_cond_w, L3_cond_u, cond_512), L3_ffn_w1, L3_ffn_w2, L3_ffn_w3)
    return x

_drawn_inputs = setup_inputs


def setup_inputs(seed=0):
    import zlib

    import numpy as np

    out = dict(_drawn_inputs(seed))
    spreads = {}
    factors = {'L0_cond_w': 5.427,
     'L0_cond_u': 7.404,
     'L0_ffn_gate_w': 8.0,
     'L0_ffn_gate_bias': 8.0,
     'L0_ffn_fc1_w': 8.0,
     'L0_ffn_fc2_w': 8.0,
     'L0_ffn_w1': 8.0,
     'L0_ffn_w2': 8.0,
     'L0_ffn_shared_up_w': 3.978,
     'L0_ffn_shared_down_w': 3.746,
     'L1_ffn_B1': 31.032,
     'L1_ffn_B2': 22.992,
     'L2_cond_w': 7.75,
     'L2_cond_u': 8.0,
     'L2_ffn_gate_weight': 7.085,
     'L2_ffn_gate_up_proj': 6.894,
     'L2_ffn_down_proj': 6.919,
     'L1_cond_w': 4.709,
     'L1_cond_u': 8.0,
     'L1_ffn_W1': 2.834,
     'L3_cond_w': 3.522,
     'L3_cond_u': 8.0}
    for name, (base, spread) in spreads.items():
        noise = np.random.default_rng([zlib.crc32(name.encode()), seed]).standard_normal(out[name].shape)
        drawn = base * np.exp(spread * noise) if base else spread * noise
        out[name] = jnp.asarray(drawn.astype(out[name].dtype))
    for name, factor in factors.items():
        out[name] = (out[name] * factor).astype(out[name].dtype)
    return out
```

```python
from contextlib import ExitStack

import concourse.bass as bass
from concourse import mybir

F32 = mybir.dt.float32
F32R = mybir.dt.float32r
BF16 = mybir.dt.bfloat16
ALU = mybir.AluOpType
ACT = mybir.ActivationFunctionType
AX = mybir.AxisListType

P = 128
B, S, C = 4, 256, 256
TOK = B * S
NT = TOK // P
KC = C // P
NBLK = B * KC
HALF = TOK // 2
TH = NT // 2
LAT = INTER = 128
E0, G0 = 32, 4
EG = E0 // G0
SH = 512
HID = 1024
E2, I2 = 8, 512
ROUND = 12582912.0
Q = 127.0
ROUTED_SCALE = 2.5


def wait(eng, sem, value):
    if not isinstance(value, int) or value > 0:
        eng.wait_ge(sem, value)


def build(nc, x_d, kt_d, te_d, w_d, u_d, sm_d, gbias_d, down_d, fc2_d, w1_d, w2_d,
          q1_d, q1b_d, q2_d, q2b_d, rt_d, gu_d, dn_d, t1_d, t2_d, t3_d, out_d):
    with ExitStack() as ctx:
        sems = {}

        def sem(name):
            if name not in sems:
                sems[name] = ctx.enter_context(nc.semaphore(name))
            return sems[name]

        cursor = [-(-nc.sbuf_base // 32) * 32]

        def sb(name, shape, dt=F32):
            size = 2 if dt == BF16 else 4
            for n in shape[1:]:
                size *= n
            t = nc.alloc_sbuf_tensor_at(name, shape, dt, offset=cursor[0])
            cursor[0] += -(-size // 32) * 32
            return t

        ident = sb("ident", [P, P])
        zeros = sb("zeros", [P, P])
        x = sb("x", [P, NT, C])
        kT = sb("kT", [P, NBLK, S])
        ekk = sb("ekk", [P, NBLK, 2, S])
        GT = sb("GT", [P, 2, NBLK, S])
        eu = sb("eu", [P, 2, 2, S])
        fw = sb("fw", [P, 2, 2, S])
        ekb = sb("ekb", [P, 2, 2, S])
        bw = sb("bw", [P, 2, 2, S])
        cond = sb("cond", [P, NT, C])
        cThi = sb("cThi", [P, KC, TOK], F32R)
        cTlo = sb("cTlo", [P, KC, TOK], F32R)
        b1bc = sb("b1bc", [P, HID])
        b2bc = sb("b2bc", [P, C])
        te = sb("te", [P, B, 64])
        wl = sb("wl", [P, 4, KC])
        ul = sb("ul", [P, 4, KC])
        dec = sb("dec", [P, 4, B, KC])
        ubk = sb("ubk", [P, 4, B, KC])
        gain = sb("gain", [P, B, KC])
        tfb = sb("tfb", [P, 4, B])
        low4 = sb("low4", [P, G0, G0])
        low8 = sb("low8", [P, E2, E2])
        cw0 = sb("cw0", [P, NT, E0])
        cw2 = sb("cw2", [P, NT, E2])
        st = sb("st", [P, 12, NT])
        pt = sb("pt", [P, 8, 2])
        ws = sb("ws", [P, 24])
        region = cursor[0]

        sm_raw = sb("sm_raw", [P, KC, E0 + LAT + SH])
        sm_hi = sb("sm_hi", [P, KC, E0 + LAT + SH], F32R)
        sm_lo = sb("sm_lo", [P, KC, E0 + LAT + SH], F32R)
        downw = sb("downw", [P, SH // P, C])
        fc2w = sb("fc2w", [P, C])
        xlhi = sb("xlhi", [P, TOK], F32R)
        xllo = sb("xllo", [P, TOK], F32R)
        hx = sb("hx", [P, 2, TH, 512])
        hT = sb("hT", [P, 2, 512])
        rl = sb("rl", [P, 2, 512])
        w1raw = sb("w1raw", [P, 2, 512])
        w1hi = sb("w1hi", [P, 2, 512], F32R)
        w1lo = sb("w1lo", [P, 2, 512], F32R)
        w2raw = sb("w2raw", [P, 2, 4, LAT])
        gbias = sb("gbias", [P, E0])
        rt = sb("rt", [P, 12, NT * E0])
        ylat = sb("ylat", [P, 2, HALF])
        top8 = sb("top8", [P, NT, 8])
        ends = [cursor[0]]

        cursor[0] = region
        guraw = sb("guraw", [P, KC, 2 * I2])
        dnraw = sb("dnraw", [P, I2 // P, C])
        guhi = sb("guhi", [P, KC, 2 * I2], F32R)
        gulo = sb("gulo", [P, KC, 2 * I2], F32R)
        dnhi = sb("dnhi", [P, I2 // P, C], F32R)
        dnlo = sb("dnlo", [P, I2 // P, C], F32R)
        rtraw = sb("rtraw", [P, KC, E2])
        rthi = sb("rthi", [P, KC, E2], F32R)
        rtlo = sb("rtlo", [P, KC, E2], F32R)
        region2 = cursor[0]
        hhi = sb("hhi", [P, 2, I2 // P, HALF], F32R)
        hlo = sb("hlo", [P, 2, I2 // P, HALF], F32R)
        sl = sb("sl", [P, 2, HALF])
        hh = sb("hh", [P, 2, HALF])
        r2 = sb("r2", [P, 10, NT, E2])
        r2c = sb("r2c", [P, 2, NT, E2 * E2])
        ends.append(cursor[0])

        cursor[0] = region2
        qf = sb("qf", [P, 2, C])
        qT = sb("qT", [P, 2, KC, P], BF16)
        xp = sb("xp", [P, 2, HID])
        gl = sb("gl", [P, 2, HID])
        q2T = sb("q2T", [P, 2, HID // P, P], BF16)
        junk = sb("junk", [P, HID])
        ends.append(cursor[0])

        cursor[0] = max(ends)
        region3 = cursor[0]
        q1raw = sb("q1raw", [P, KC, HID])
        q2raw = sb("q2raw", [P, HID // P, C])
        q1w = sb("q1w", [P, KC, HID], BF16)
        q2w = sb("q2w", [P, HID // P, C], BF16)
        cursor[0] = region3
        traw = sb("traw", [P, KC * HID])
        tw = sb("tw", [P, 3, KC * HID], BF16)
        assert max(cursor[0], region3 + 24 * 1024) <= nc.sbuf_usable_end

        bank = [ctx.enter_context(nc.psum_tensor(f"bank{i}", [P, 512], F32)) for i in range(8)]

        def one(ap, spec, **kw):
            return ap.rearrange(spec, **kw)

        DONE = [NBLK, 3 * NBLK, 3 * NBLK, 4 * NBLK]

        block = ctx.enter_context(nc.Block())

        @block.sync
        def _(sp):
            for b in range(B):
                sp.dma_start(kT[:, 2 * b:2 * b + 2, :], kt_d[:, 2 * b:2 * b + 2, :]).then_inc(sem(f"kT_in{b}"), 16)
                if b == 0:
                    for dst, src in ((te, te_d), (wl, w_d), (ul, u_d)):
                        sp.dma_start(dst[:], src).then_inc(sem("small_in"), 16)
            for s in range(2):
                sp.dma_start(x[:, TH * s:TH * s + TH, :], x_d[:, TH * s:TH * s + TH, :]).then_inc(sem(f"x_in{s}"), 16)
            sp.dma_start(sm_raw[:], sm_d).then_inc(sem("sm_in"), 16)
            sp.dma_start(gbias[:], gbias_d).then_inc(sem("gbias_in"), 16)
            sp.dma_start(downw[:], down_d).then_inc(sem("down_in"), 16)
            sp.dma_start(fc2w[:], fc2_d).then_inc(sem("fc2_in"), 16)
            for dst, src in ((q1raw, q1_d), (q2raw, q2_d)):
                sp.dma_start(dst[:], src).then_inc(sem("q_in"), 16)
            for dst, src in ((b1bc, q1b_d), (b2bc, q2b_d)):
                sp.dma_start(dst[:], src).then_inc(sem("qb_in"), 16)

            def expert_weights(i, o):
                eg = 2 * i + o
                wait(sp, sem("w1_split"), eg - 1)
                sp.dma_start(w1raw[:, o, :], w1_d[:, eg, :]).then_inc(sem(f"w1_in{o}"), 16)
                wait(sp, sem("y_done"), 8 * eg - 8)
                sp.dma_start(w2raw[:, o, :, :], w2_d[:, eg, :, :]).then_inc(sem(f"w2_in{o}"), 16)

            expert_weights(0, 0)
            expert_weights(0, 1)
            with sp.Fori(1, EG // 2) as i:
                expert_weights(i, 0)
                expert_weights(i, 1)

            sp.wait_ge(sem("x1_ready"), 4)
            sp.dma_start(rtraw[:], rt_d).then_inc(sem("rt_in"), 16)

            def glu_weights(e):
                wait(sp, sem("gu_split"), e)
                sp.dma_start(guraw[:], gu_d[bass.ds(e, 1), :, :, :].rearrange("o p k n -> p (o k) n")
                             ).then_inc(sem("gu_in"), 16)
                wait(sp, sem("dn_split"), e)
                sp.dma_start(dnraw[:], dn_d[bass.ds(e, 1), :, :, :].rearrange("o p k n -> p (o k) n")
                             ).then_inc(sem("dn_in"), 16)

            glu_weights(0)
            sp.wait_ge(sem("x2_ready"), NT)
            for m, src in enumerate((t1_d, t2_d, t3_d)):
                wait(sp, sem("t_quant"), m)
                sp.dma_start(traw[:], src).then_inc(sem("t_in"), 16)
                if m < 2:
                    glu_weights(m + 1)
            with sp.Fori(3, E2) as e:
                glu_weights(e)
            for t in range(NT):
                sp.wait_ge(sem("x4_ready"), t + 1)
                sp.dma_start(out_d[:, t, :], x[:, t, :]).then_inc(sem("out_done"), 16)
            sp.wait_ge(sem("out_done"), 16 * NT)

        @block.gpsimd
        def _(pool):
            def wait_alone(name, value):
                wait(pool, sem(name), value)
                if not isinstance(value, int):
                    pool.sem_inc(sem("pool_waited"), 1)

            pool.memset(ident[:], 0.0).then_inc(sem("consts"), 1)
            pool.memset(zeros[:], 0.0).then_inc(sem("consts"), 1)
            pool.memset(low4[:], 1.0).then_inc(sem("consts"), 1)
            pool.memset(low8[:], 1.0).then_inc(sem("consts"), 1)
            pool.memset(bw[:], 0.0).then_inc(sem("bw_zero"), 1)
            pool.wait_ge(sem("consts"), 4)
            pool.affine_select(out=ident[:], in_=ident[:], compare_op=ALU.not_equal, fill=1.0, base=0,
                               pattern=[[-1, P]], channel_multiplier=1).then_inc(sem("ident_ready"), 1)
            for low, n in ((low4, G0), (low8, E2)):
                pool.affine_select(out=low[:], in_=low[:], compare_op=ALU.is_gt, fill=0.0, base=0,
                                   pattern=[[1, n], [-1, n]], channel_multiplier=0).then_inc(sem("low_ready"), 1)

            def wkv_sums(n, blk, p):
                wait_alone("eu_ready", n + 1)
                pool.tensor_tensor(eu[:, p, 0, :], eu[:, p, 1, :], kT[:, blk, :], ALU.mult).then_inc(sem("euv_ready"), 1)
                wait_alone("scan_ready", n + 1)
                pool.tensor_tensor(fw[:, p, :, :], fw[:, p, :, :], bw[:, p, :, :], ALU.add).then_inc(sem("both_ready"), 1)
                wait_alone("euv_ready", n + 1)
                wait_alone("both_ready", n + 1)
                pool.tensor_tensor(fw[:, p, :, :], fw[:, p, :, :], eu[:, p, :, :], ALU.add).then_inc(sem("sums_ready"), 1)

            for n in range(NBLK):
                wkv_sums(n, n, n % 2)

            def split_w1(i, o):
                eg = 2 * i + o
                wait_alone(f"w1_in{o}", 16 * (i + 1))
                wait_alone("z_ready", 8 * eg - 8)
                pool.tensor_scalar(w1hi[:, o, :], w1raw[:, o, :], 1.0, 0.0, ALU.mult, ALU.add).then_inc(sem("w1_high"), 1)
                wait_alone("w1_high", eg + 1)
                pool.tensor_tensor(w1lo[:, o, :], w1raw[:, o, :], w1hi[:, o, :].bitcast(F32), ALU.subtract
                                   ).then_inc(sem("w1_split"), 1)

            split_w1(0, 0)
            split_w1(0, 1)

            def expert_steps(i, last):
                for o in range(4):
                    q = 4 * i + o
                    wkv_sums(NBLK + q, 2 * i + o // 2, o % 2)
                    if o % 2 and not last:
                        split_w1(i + 1, o // 2)

            expert_steps(0, False)
            with pool.Fori(1, EG // 2 - 1) as i:
                expert_steps(i, False)
            expert_steps(EG // 2 - 1, True)

            pool.wait_ge(sem("wmax_part"), 2)
            pool.partition_all_reduce(ws[:, 2:4], ws[:, 0:2], P, bass.bass_isa.ReduceOp.max).then_inc(sem("wmax_ready"), 1)
            pool.wait_ge(sem("wscale_ready"), 1)
            for m, (raw, w) in enumerate(((q1raw, q1w), (q2raw, q2w))):
                pool.tensor_scalar(raw[:], raw[:], ws[:, 6 + m:7 + m], ROUND, ALU.mult, ALU.add).then_inc(sem("q_round"), 1)
            for m, (raw, w) in enumerate(((q1raw, q1w), (q2raw, q2w))):
                pool.wait_ge(sem("q_round"), m + 1)
                pool.tensor_scalar(w[:], raw[:], -ROUND, 1.0, ALU.add, ALU.mult).then_inc(sem("q_quant"), 1)
            pool.wait_ge(sem("qb_in"), 32)
            for t in range(NT):
                pool.wait_ge(sem("sig_ready"), 2 + t // TH + 1)
                pool.tensor_tensor(x[:, t, :], x[:, t, :], b2bc[:], ALU.add).then_inc(sem("xb_ready"), 1)

            def split_glu(e):
                wait_alone("gu_in", 16 * (e + 1))
                wait_alone("gu_done", 8 * e)
                for k in range(KC):
                    pool.tensor_scalar(guhi[:, k, :], guraw[:, k, :], 1.0, 0.0, ALU.mult, ALU.add).then_inc(sem("gu_high"), 1)
                for k in range(KC):
                    wait_alone("gu_high", 2 * e + k + 1)
                    ins = pool.tensor_tensor(gulo[:, k, :], guraw[:, k, :], guhi[:, k, :].bitcast(F32), ALU.subtract)
                ins.then_inc(sem("gu_split"), 1)
                wait_alone("dn_in", 16 * (e + 1))
                wait_alone("d_done", 8 * e)
                pool.tensor_scalar(dnhi[:], dnraw[:], 1.0, 0.0, ALU.mult, ALU.add).then_inc(sem("dn_high"), 1)
                wait_alone("dn_high", e + 1)
                pool.tensor_tensor(dnlo[:], dnraw[:], dnhi[:].bitcast(F32), ALU.subtract).then_inc(sem("dn_split"), 1)

            split_glu(0)
            def ternary(m):
                pool.wait_ge(sem("tsum_part"), m + 1)
                pool.partition_all_reduce(ws[:, 12 + m:13 + m], ws[:, 9 + m:10 + m], P,
                                          bass.bass_isa.ReduceOp.add).then_inc(sem("tsum_ready"), 1)
                pool.wait_ge(sem("tscale_ready"), m + 1)
                pool.tensor_scalar(traw[:], traw[:], ws[:, 18 + m:19 + m], ROUND, ALU.mult, ALU.add).then_inc(sem("t_step"), 1)
                pool.wait_ge(sem("t_step"), 2 * m + 1)
                pool.tensor_scalar(traw[:], traw[:], ROUND + 1.0, ROUND - 1.0, ALU.min, ALU.max).then_inc(sem("t_step"), 1)
                pool.wait_ge(sem("t_step"), 2 * m + 2)
                pool.tensor_scalar(tw[:, m, :], traw[:], -ROUND, 1.0, ALU.add, ALU.mult).then_inc(sem("t_quant"), 1)

            def glu_step(e, p):
                split_glu(e)
                if isinstance(e, int) and e <= 3:
                    ternary(e - 1)
                wkv_sums(3 * NBLK + e, e, p)

            wkv_sums(3 * NBLK, 0, 0)
            for e in range(1, 4):
                glu_step(e, e % 2)
            with pool.Fori(2, E2 // 2) as i:
                glu_step(2 * i, 0)
                glu_step(2 * i + 1, 1)

            def rms_stats(mean_sq, root, absmax, out, sum_name, max_name, n, out_name):
                pool.wait_ge(sem(sum_name), n)
                pool.tensor_scalar(mean_sq, mean_sq, 1.0, 1e-6, ALU.mult, ALU.add).then_inc(sem("p3"), 1)
                p3[0] += 1
                pool.wait_ge(sem("p3"), p3[0])
                pool.tensor_tensor(root, mean_sq, half, ALU.pow).then_inc(sem("p3"), 1)
                p3[0] += 1
                pool.wait_ge(sem("p3"), p3[0])
                pool.wait_ge(sem(max_name), n)
                pool.tensor_tensor(out, absmax, root, ALU.mult).then_inc(sem(out_name), 1)

            p3 = [0]
            pool.memset(st[:, 11, :], -0.5).then_inc(sem("p3"), 1)
            p3[0] += 1
            pool.wait_ge(sem("p3"), p3[0])
            half = st[:, 11, :]
            rms_stats(st[:, 4, :], st[:, 5, :], st[:, 6, :], st[:, 7, :], "c3_sq", "c3_max", 1, "c3_stat")
            half = st[:, 11, 0:1]
            for t in range(NT):
                p = t % 2
                rms_stats(pt[:, 4, p:p + 1], pt[:, 5, p:p + 1], pt[:, 6, p:p + 1], pt[:, 7, p:p + 1],
                          "h3_sq", "h3_max", t + 1, "h3_stat")

        @block.scalar
        def _(act):
            act.wait_ge(sem("small_in"), 48)
            act.activation(wl[:], wl[:], ACT.Exp).then_inc(sem("a0"), 1)
            act.wait_ge(sem("a0"), 1)
            act.activation(wl[:], wl[:], ACT.Exp, scale=-1.0).then_inc(sem("wl_ready"), 1)
            act.wait_ge(sem("te_sum"), 1)
            act.activation(tfb[:, 1, :], tfb[:, 0, :], ACT.Exp, scale=-1.0).then_inc(sem("te_exp"), 1)

            def wkv_exp(n, p):
                wait(act, sem("kup_ready"), n + 1)
                act.activation(eu[:, p, 1, :], eu[:, p, 1, :], ACT.Exp).then_inc(sem("eu_ready"), 1)

            for b in range(B):
                act.wait_ge(sem("kmin_ready"), b + 1)
                act.activation(ekk[:, 2 * b:2 * b + 2, 1, :], ekk[:, 2 * b:2 * b + 2, 1, :], ACT.Exp).then_inc(sem("ek_ready"), 1)
                wkv_exp(2 * b, 0)
                wkv_exp(2 * b + 1, 1)

            def sigmoid_x(l):
                for s in range(2):
                    if l == 0:
                        act.wait_ge(sem(f"x_in{s}"), 16)
                    elif l == 1:
                        act.wait_ge(sem("x1_ready"), 2 * s + 2)
                    elif l == 2:
                        act.wait_ge(sem("x2_ready"), TH * s + TH)
                    else:
                        act.wait_ge(sem("acc_ready"), 8 * (E2 - 1) + TH * s + TH)
                    act.activation(cond[:, TH * s:TH * s + TH, :], x[:, TH * s:TH * s + TH, :],
                                   ACT.Sigmoid).then_inc(sem("sig_ready"), 1)

            def cond_high(n0):
                for s in range(2):
                    for k in range(KC):
                        n = n0 + 2 * s + k
                        act.wait_ge(sem("cT_ready"), n + 1)
                        act.activation(cThi[:, k, HALF * s:HALF * s + HALF], bank[2 + n % 2][:], ACT.Copy
                                       ).then_inc(sem("cT_high"), 1)

            sigmoid_x(0)
            act.wait_ge(sem("sm_in"), 16)
            act.activation(sm_hi[:], sm_raw[:], ACT.Copy).then_inc(sem("sm_high"), 1)
            cond_high(0)
            act.wait_ge(sem("gate_ready"), 1)
            act.activation(rt[:, 0, :], bank[4][:, 0:NT * E0], ACT.Sigmoid).then_inc(sem("score_ready"), 1)
            for s in range(2):
                act.wait_ge(sem("xl_ready"), s + 1)
                act.activation(xlhi[:, HALF * s:HALF * s + HALF], bank[5 + s][:], ACT.Copy).then_inc(sem("xl_high"), 1)
            for u in range(8):
                act.wait_ge(sem("sz_ready"), u + 1)
                wait(act, sem("sh_ready"), u - 1)
                act.activation(rl[:, u % 2, :], bank[u % 4][:], ACT.Relu).then_inc(sem("sr_ready"), 1)

            def relu_scaled(q, o, j):
                eg = q // 2 if isinstance(q, int) else None
                t = TH * (o % 2) + j
                wait(act, sem("h0_ready"), 4 * q + j - 1)
                wait(act, sem("z_ready"), 4 * q + j + 1)
                act.wait_ge(sem("cw0_ready"), 1)
                for e in range(4):
                    ins = act.activation(rl[:, j % 2, e * P:e * P + P], bank[j][:, e * P:e * P + P], ACT.Relu,
                                         scale=cw0[:, t, bass.ds(4 * relu_scaled.eg + e, 1)])
                ins.then_inc(sem("r_ready"), 1)

            def hT_copy(q, e):
                wait(act, sem("y_done"), 4 * q + e - 1)
                wait(act, sem("t_ready"), 4 * q + e + 1)
                act.activation(hT[:, e % 2, :], bank[6 + e % 2][:], ACT.Copy).then_inc(sem("hT_ready"), 1)

            relu_scaled.eg = 0
            for j in range(4):
                relu_scaled(0, 0, j)

            def expert_steps(i, last):
                for o in range(4):
                    q = 4 * i + o
                    more = not (last and o == 3)
                    relu_scaled.eg = 2 * i + (o + 1) // 2
                    if more:
                        relu_scaled(q + 1, (o + 1) % 4, 0)
                        relu_scaled(q + 1, (o + 1) % 4, 1)
                    hT_copy(q, 0)
                    wkv_exp(NBLK + q, o % 2)
                    if more:
                        relu_scaled(q + 1, (o + 1) % 4, 2)
                    hT_copy(q, 1)
                    if more:
                        relu_scaled(q + 1, (o + 1) % 4, 3)
                    hT_copy(q, 2)
                    hT_copy(q, 3)

            expert_steps(0, False)
            with act.Fori(1, EG // 2 - 1) as i:
                expert_steps(i, False)
            expert_steps(EG // 2 - 1, True)
            act.wait_ge(sem("y_closed"), 1)
            for s in range(2):
                act.activation(ylat[:, s, :], bank[4 + s][:], ACT.Copy).then_inc(sem("ylat_ready"), 1)

            sigmoid_x(1)

            def l1_first(t):
                p = t % 2
                act.wait_ge(sem("q1t_ready"), t + 1)
                wait(act, sem("m1_ready"), t - 1)
                act.activation(qT[:, p, :, :], bank[4][:, 0:C], ACT.Copy, bias=-ROUND).then_inc(sem("q1T_ready"), 1)

            def l1_gelu(t):
                p = t % 2
                wait(act, sem("q2t_ready"), 2 * t - 2)
                act.wait_ge(sem("pre_ready"), t + 1)
                act.activation(gl[:, p, :], xp[:, p, :], ACT.Gelu_apprx_tanh).then_inc(sem("gelu_ready"), 1)

            def l1_second(t, tag=""):
                p = t % 2
                wait(act, sem("m2_ready" + tag), t - 1)
                for h in range(2):
                    act.wait_ge(sem("q2t_ready" + tag), 2 * t + h + 1)
                    act.activation(q2T[:, p, 4 * h:4 * h + 4, :], bank[5 + h][:], ACT.Copy, bias=-ROUND
                                   ).then_inc(sem("q2T_ready" + tag), 1)

            for t in range(-2, NT):
                if t + 2 < NT:
                    l1_first(t + 2)
                if 0 <= t + 1 < NT:
                    l1_gelu(t + 1)
                if t >= 0:
                    l1_second(t)

            sigmoid_x(2)
            cond_high(4)
            act.wait_ge(sem("lsub_ready"), 1)
            act.activation(r2[:, 1, :, :], r2[:, 1, :, :], ACT.Exp).then_inc(sem("lexp_ready"), 1)

            def silu_gate(u, p):
                wait(act, sem("hh_ready"), u - 1)
                wait(act, sem("gu_done"), u + 1)
                act.activation(sl[:, p, :], bank[2 * p][:], ACT.Silu).then_inc(sem("sl_ready"), 1)

            def glu_step(e, p):
                wkv_exp(3 * NBLK + e, p)
                for j in range(8):
                    silu_gate(8 * e + j, j % 2)

            glu_step(0, 0)
            glu_step(1, 1)
            with act.Fori(1, E2 // 2) as i:
                glu_step(2 * i, 0)
                glu_step(2 * i + 1, 1)

            sigmoid_x(3)
            for t in range(NT):
                act.wait_ge(sem("cond_ready"), 12 + t // 2 + 1)
                ins = act.activation(xp[:, t // TH, C * (t % TH):C * (t % TH) + C], cond[:, t, :], ACT.Square, scale=C ** -0.5, accum_out=st[:, 4, t:t + 1])
            ins.then_inc(sem("c3_sq"), 1)

            def l3_first(t):
                p = t % 2
                act.wait_ge(sem("q1t3_ready"), t + 1)
                wait(act, sem("m13_ready"), 2 * t - 2)
                act.activation(qT[:, p, :, :], bank[4][:, 0:C], ACT.Copy, bias=-ROUND).then_inc(sem("q1T3_ready"), 1)

            def l3_silu(t):
                p = t % 2
                for h in range(2):
                    act.wait_ge(sem("m13_ready"), 2 * t + h + 1)
                    wait(act, sem("h3_ready"), 2 * t + h - 3)
                    act.activation(xp[:, p, 512 * h:512 * h + 512], bank[h][:], ACT.Silu, scale=st[:, 9, t:t + 1]
                                   ).then_inc(sem("silu3_ready"), 1)

            def l3_square(t):
                p = t % 2
                act.wait_ge(sem("h3_ready"), 2 * t + 2)
                wait(act, sem("h3_sq"), t)
                wait(act, sem("q23_ready"), t - 1)
                act.activation(junk[:], gl[:, p, :], ACT.Square, scale=HID ** -0.5, accum_out=pt[:, 4, p:p + 1]
                               ).then_inc(sem("h3_sq"), 1)

            for t in range(-2, NT):
                if 0 <= t + 1 < NT:
                    l3_silu(t + 1)
                if t + 2 < NT:
                    l3_first(t + 2)
                if 0 <= t + 1 < NT:
                    l3_square(t + 1)
                if t >= 0:
                    l1_second(t, "3")

        @block.vector
        def _(dve):
            count = [0]

            def chain(ins):
                count[0] += 1
                ins.then_inc(sem("dve_step"), 1)
                dve.wait_ge(sem("dve_step"), count[0])

            dve.wait_ge(sem("small_in"), 48)
            dve.tensor_reduce(tfb[:, 0, :], te[:], AX.X, ALU.add).then_inc(sem("te_sum"), 1)

            def side_exp(b):
                dve.wait_ge(sem(f"kT_in{b}"), 16)
                dve.tensor_scalar(ekk[:, 2 * b:2 * b + 2, 1, :], kT[:, 2 * b:2 * b + 2, :], 30.0, None, ALU.min
                                  ).then_inc(sem("kmin_ready"), 1)

            side_exp(0)
            dve.wait_ge(sem("te_exp"), 1)
            chain(dve.tensor_scalar(tfb[:, 1, :], tfb[:, 1, :], 1.0, None, ALU.add))
            chain(dve.reciprocal(tfb[:, 0, :], tfb[:, 1, :]))
            dve.tensor_scalar(tfb[:, 2, :], tfb[:, 0, :], 0.5, 0.5, ALU.mult, ALU.add)
            chain(dve.tensor_scalar(tfb[:, 3, :], tfb[:, 0, :], 0.2, 0.8, ALU.mult, ALU.add))
            dve.wait_ge(sem("wl_ready"), 1)
            for b in range(B):
                dve.tensor_scalar(dec[:, :, b, :], wl[:], tfb[:, 2, b:b + 1], None, ALU.mult)
                dve.tensor_copy(ubk[:, :, b, :], ul[:])
                ins = dve.tensor_scalar(gain[:, b, :], wl[:, 0, :], 0.0, tfb[:, 3, b:b + 1], ALU.mult, ALU.add)
            chain(ins)
            decf = dec[:].rearrange("p l b k -> p (l b k)")
            ubf = ubk[:].rearrange("p l b k -> p (l b k)")
            gf = gain[:].rearrange("p b k -> p (b k)")

            def col(ap, i):
                return ap[:, i:i + 1] if isinstance(i, int) else ap[:, bass.ds(i, 1)]

            def wkv_kup(n, l, blk, p):
                wait(dve, sem("sums_ready"), n - 1)
                dve.tensor_scalar(eu[:, p, 1, :], kT[:, blk, :], col(ubf, NBLK * l + blk), 30.0, ALU.add, ALU.min
                                  ).then_inc(sem("kup_ready"), 1)
                dve.tensor_copy(ekb[:, p, :, :], ekk[:, blk, :, :]).then_inc(sem("ekb_ready"), 1)

            def wkv_scan(n, l, blk, p, part):
                d = part % 2
                if part == 0:
                    wait(dve, sem("G_ready"), n - 1)
                if part < 2:
                    dve.tensor_tensor_scan(fw[:, p, d, :], col(decf, NBLK * l + blk).to_broadcast([P, S]),
                                           ekk[:, blk, d, :], 0.0, ALU.mult, ALU.add)
                else:
                    wait(dve, sem("ekb_ready"), n + 1)
                    ins = dve.tensor_tensor_scan(bw[:, p, d, S - 2::-1], ekb[:, p, d, S - 1:0:-1],
                                                 col(decf, NBLK * l + blk).to_broadcast([P, S - 1]), 0.0, ALU.add, ALU.mult)
                    if part == 3:
                        ins.then_inc(sem("scan_ready"), 1)

            def wkv_gain(n, l, blk, p):
                wait(dve, sem("sums_ready"), n + 1)
                dve.tensor_scalar(fw[:, p, 1, :], fw[:, p, 1, :], 1e-8, None, ALU.max).then_inc(sem("den_ready"), 1)
                wait(dve, sem("den_ready"), n + 1)
                dve.reciprocal(fw[:, p, 1, :], fw[:, p, 1, :]).then_inc(sem("rden_ready"), 1)
                wait(dve, sem("rden_ready"), n + 1)
                dve.scalar_tensor_tensor(out=GT[:, l % 2, blk, :], in0=fw[:, p, 0, :], scalar=col(gf, blk),
                                         in1=fw[:, p, 1, :], op0=ALU.mult, op1=ALU.mult).then_inc(sem("G_ready"), 1)

            dve.wait_ge(sem("bw_zero"), 1)
            for b in range(B):
                dve.wait_ge(sem("ek_ready"), b + 1)
                chain(dve.tensor_tensor(ekk[:, 2 * b:2 * b + 2, 0, :], ekk[:, 2 * b:2 * b + 2, 1, :],
                                        kT[:, 2 * b:2 * b + 2, :], ALU.mult))
                if b + 1 < B:
                    side_exp(b + 1)
                for n in (2 * b, 2 * b + 1):
                    wkv_kup(n, 0, n, n % 2)
                    for part in range(4):
                        wkv_scan(n, 0, n, n % 2, part)
                    if n:
                        wkv_gain(n - 1, 0, n - 1, (n - 1) % 2)
            wkv_gain(NBLK - 1, 0, NBLK - 1, 1)

            def make_cond(l):
                for b in range(B):
                    m = 4 * l + b
                    dve.wait_ge(sem("G_turned"), m + 1)
                    dve.wait_ge(sem("sig_ready"), 2 * l + b // 2 + 1)
                    dve.tensor_tensor(cond[:, 2 * b:2 * b + 2, :], bank[b % 2][:].rearrange("p (t c) -> p t c", t=2),
                                      cond[:, 2 * b:2 * b + 2, :], ALU.mult).then_inc(sem("cond_ready"), 1)

            def cond_low(n0):
                for s in range(2):
                    for k in range(KC):
                        n = n0 + 2 * s + k
                        dve.wait_ge(sem("cT_high"), n + 1)
                        dve.tensor_tensor(cTlo[:, k, HALF * s:HALF * s + HALF], bank[2 + n % 2][:],
                                          cThi[:, k, HALF * s:HALF * s + HALF].bitcast(F32), ALU.subtract
                                          ).then_inc(sem("cT_low"), 1)

            def ranks(score, low, n, a, b, rank):
                four = dict(o=1)
                other = score.rearrange("p t (o g) -> p t o g", **four).to_broadcast([P, NT, n, n])
                own = score.rearrange("p t (g o) -> p t g o", **four).to_broadcast([P, NT, n, n])
                lowb = low[:].rearrange("p (o g) h -> p o g h", **four).to_broadcast([P, NT, n, n])
                dve.tensor_tensor(a, other, own, ALU.is_gt)
                chain(dve.tensor_tensor(b, other, own, ALU.is_equal))
                chain(dve.tensor_tensor(b, b, lowb, ALU.mult))
                chain(dve.tensor_tensor(a, a, b, ALU.add))
                chain(dve.tensor_reduce(rank, a, AX.X, ALU.add))

            make_cond(0)
            dve.wait_ge(sem("sm_high"), 1)
            dve.tensor_tensor(sm_lo[:], sm_raw[:], sm_hi[:].bitcast(F32), ALU.subtract).then_inc(sem("sm_low"), 1)
            cond_low(0)
            for s in range(2):
                dve.wait_ge(sem("xl_high"), s + 1)
                dve.tensor_tensor(xllo[:, HALF * s:HALF * s + HALF], bank[5 + s][:],
                                  xlhi[:, HALF * s:HALF * s + HALF].bitcast(F32), ALU.subtract).then_inc(sem("xl_low"), 1)

            def shared_h(u):
                dve.wait_ge(sem("sr_ready"), u + 1)
                dve.scalar_tensor_tensor(out=hx[:, u // 4, u % 4, :], in0=bank[u % 4][:], scalar=0.0, in1=rl[:, u % 2, :],
                                         op0=ALU.max, op1=ALU.mult).then_inc(sem("sh_ready"), 1)

            for u in range(4):
                shared_h(u)

            def r(i, n=NT * E0):
                return rt[:, i, 0:n]

            def g8(i, w=8):
                return rt[:, i, 0:NT * G0 * w].rearrange("p (t w) -> p t w", w=w)

            dve.wait_ge(sem("score_ready"), 1)
            dve.wait_ge(sem("gbias_in"), 16)
            dve.wait_ge(sem("low_ready"), 2)
            chain(dve.tensor_tensor(r(1).rearrange("p (t e) -> p t e", e=E0), r(0).rearrange("p (t e) -> p t e", e=E0),
                                    gbias[:].rearrange("p (o e) -> p o e", o=1).to_broadcast([P, NT, E0]), ALU.add))
            sc = g8(1)
            hi4, lo4 = g8(2, 4), g8(3, 4)
            dve.tensor_tensor(hi4, sc[:, :, 0:4], sc[:, :, 4:8], ALU.max)
            chain(dve.tensor_tensor(lo4, sc[:, :, 0:4], sc[:, :, 4:8], ALU.min))
            hi, lo = hi4, lo4
            for lev, w in ((0, 2), (1, 1)):
                nh, nl, ml, ll = (g8(4 + 4 * lev + i, w) for i in range(4))
                dve.tensor_tensor(nh, hi[:, :, 0:w], hi[:, :, w:2 * w], ALU.max)
                dve.tensor_tensor(ml, hi[:, :, 0:w], hi[:, :, w:2 * w], ALU.min)
                chain(dve.tensor_tensor(ll, lo[:, :, 0:w], lo[:, :, w:2 * w], ALU.max))
                chain(dve.tensor_tensor(nl, ml, ll, ALU.max))
                hi, lo = nh, nl
            gs = rt[:, 2, 0:NT * G0].rearrange("p (t g) -> p t g", g=G0)
            chain(dve.tensor_tensor(rt[:, 2, 0:NT * G0], rt[:, 8, 0:NT * G0], rt[:, 9, 0:NT * G0], ALU.add))
            sq = [rt[:, i, 0:NT * G0 * G0].rearrange("p (t g h) -> p t g h", g=G0, h=G0) for i in (3, 4)]
            ranks(gs, low4, G0, sq[0], sq[1], rt[:, 5, 0:NT * G0].rearrange("p (t g) -> p t g", g=G0))
            chain(dve.tensor_scalar(rt[:, 6, 0:NT * G0], rt[:, 5, 0:NT * G0], 2.0, None, ALU.is_lt))
            dve.tensor_scalar(rt[:, 7, 0:NT * G0], rt[:, 6, 0:NT * G0], -1.0, 3.0e38, ALU.add, ALU.mult)

            def over8(i):
                return rt[:, i, 0:NT * G0].rearrange("p (t o) -> p t o", o=1).to_broadcast([P, NT * G0, 8])

            chain(dve.tensor_tensor(g8(8), sc, over8(6), ALU.mult))
            chain(dve.tensor_tensor(g8(8), g8(8), over8(7), ALU.add))
            for t in range(NT):
                ins = dve.max(top8[:, t, :], rt[:, 8, t * E0:t * E0 + E0])
            chain(ins)
            for t in range(NT):
                ins = dve.match_replace(rt[:, 9, t * E0:t * E0 + E0], top8[:, t, :], rt[:, 8, t * E0:t * E0 + E0], -3.3e38)
            chain(ins)
            chain(dve.tensor_tensor(r(10), r(9), r(8), ALU.not_equal))
            chain(dve.tensor_tensor(r(10), r(10), r(0), ALU.mult))
            chain(dve.tensor_reduce(rt[:, 11, 0:NT], r(10).rearrange("p (t e) -> p t e", e=E0), AX.X, ALU.add))
            chain(dve.reciprocal(rt[:, 11, NT:2 * NT], rt[:, 11, 0:NT]))
            chain(dve.tensor_scalar(rt[:, 11, 2 * NT:3 * NT], rt[:, 11, NT:2 * NT], ROUTED_SCALE, None, ALU.mult))
            dve.tensor_tensor(cw0[:], r(10).rearrange("p (t e) -> p t e", e=E0),
                              rt[:, 11, 2 * NT:3 * NT].rearrange("p (t o) -> p t o", o=1).to_broadcast([P, NT, E0]),
                              ALU.mult).then_inc(sem("cw0_ready"), 1)

            for u in range(4, 8):
                shared_h(u)
            for v in range(4):
                dve.wait_ge(sem("sd_ready"), v + 1)
                dve.tensor_tensor(x[:, 2 * v:2 * v + 2, :], bank[4 + v][:].rearrange("p (t c) -> p t c", t=2),
                                  x[:, 2 * v:2 * v + 2, :], ALU.add).then_inc(sem("sx_done"), 1)

            dve.wait_ge(sem("q_in"), 32)
            dve.tensor_reduce(ws[:, 0:1], q1raw[:].rearrange("p k n -> p (k n)"), AX.X, ALU.max,
                              apply_absolute_value=True).then_inc(sem("wmax_part"), 1)
            dve.tensor_reduce(ws[:, 1:2], q2raw[:].rearrange("p k n -> p (k n)"), AX.X, ALU.max,
                              apply_absolute_value=True).then_inc(sem("wmax_part"), 1)

            def expert_h(q, o, j):
                wait(dve, sem("r_ready"), 4 * q + j + 1)
                dve.scalar_tensor_tensor(out=hx[:, o % 2, j, :], in0=bank[j][:], scalar=0.0, in1=rl[:, j % 2, :],
                                         op0=ALU.max, op1=ALU.mult).then_inc(sem("h0_ready"), 1)

            for j in range(4):
                expert_h(0, 0, j)
            dve.wait_ge(sem("G_turned"), 4)

            def expert_steps(i, last):
                for o in range(4):
                    q = 4 * i + o
                    n, l, blk, p = NBLK + q, 1 + o % 2, 2 * i + o // 2, o % 2
                    wkv_kup(n, l, blk, p)
                    for j in range(4):
                        if not (last and o == 3):
                            expert_h(q + 1, o + 1, j)
                        wkv_scan(n, l, blk, p, j)
                        if j == 2 and o:
                            wkv_gain(n - 1, 1 + (o - 1) % 2, 2 * i + (o - 1) // 2, 1 - p)
                wkv_gain(n, l, blk, p)

            expert_steps(0, False)
            with dve.Fori(1, EG // 2 - 1) as i:
                expert_steps(i, False)
            expert_steps(EG // 2 - 1, True)

            dve.wait_ge(sem("wmax_ready"), 1)
            chain(dve.reciprocal(ws[:, 4:6], ws[:, 2:4]))
            dve.tensor_scalar(ws[:, 6:8], ws[:, 4:6], Q, None, ALU.mult).then_inc(sem("wscale_ready"), 1)
            dve.wait_ge(sem("wscale_ready"), 1)
            chain(dve.tensor_scalar(ws[:, 4:6], ws[:, 2:4], 1.0 / (Q * Q), None, ALU.mult))
            for v in range(4):
                dve.wait_ge(sem("fo_ready"), v + 1)
                dve.tensor_tensor(x[:, 2 * v:2 * v + 2, :], bank[v][:].rearrange("p (t c) -> p t c", t=2),
                                  x[:, 2 * v:2 * v + 2, :], ALU.add).then_inc(sem("x1_ready"), 1)

            make_cond(1)
            dve.wait_ge(sem("cond_ready"), 8)
            chain(dve.tensor_reduce(st[:, 0, :], cond[:], AX.X, ALU.max, apply_absolute_value=True))
            chain(dve.reciprocal(st[:, 1, :], st[:, 0, :]))
            dve.tensor_scalar(st[:, 2, :], st[:, 1, :], Q, None, ALU.mult)
            chain(dve.tensor_scalar(st[:, 3, :], st[:, 0, :], ws[:, 4:5], None, ALU.mult))

            def quant_rows(t, scale, ready, free):
                p = t % 2
                wait(dve, sem(free), t - 1)
                dve.tensor_scalar(qf[:, p, :], cond[:, t, :], scale[:, t:t + 1], ROUND, ALU.mult, ALU.add
                                  ).then_inc(sem(ready), 1)

            def l1_pre(t):
                p = t % 2
                dve.wait_ge(sem("m1_ready"), t + 1)
                wait(dve, sem("gelu_ready"), t - 1)
                for h in range(2):
                    ins = dve.scalar_tensor_tensor(out=xp[:, p, 512 * h:512 * h + 512], in0=bank[2 * p + h][:],
                                                   scalar=st[:, 3, t:t + 1], in1=b1bc[:, 512 * h:512 * h + 512],
                                                   op0=ALU.mult, op1=ALU.add)
                ins.then_inc(sem("pre_ready"), 1)

            def l1_quant(t):
                p = t % 2
                dve.wait_ge(sem("gelu_ready"), t + 1)
                chain(dve.tensor_reduce(pt[:, 0, p:p + 1], gl[:, p, :], AX.X, ALU.max, apply_absolute_value=True))
                chain(dve.reciprocal(pt[:, 1, p:p + 1], pt[:, 0, p:p + 1]))
                dve.tensor_scalar(pt[:, 3, p:p + 1], pt[:, 0, p:p + 1], ws[:, 5:6], None, ALU.mult)
                chain(dve.tensor_scalar(pt[:, 2, p:p + 1], pt[:, 1, p:p + 1], Q, None, ALU.mult))
                dve.tensor_scalar(gl[:, p, :], gl[:, p, :], pt[:, 2, p:p + 1], ROUND, ALU.mult, ALU.add
                                  ).then_inc(sem("q2_ready"), 1)

            def l1_out(t):
                dve.wait_ge(sem("m2_ready"), t + 1)
                dve.wait_ge(sem("xb_ready"), t + 1)
                dve.scalar_tensor_tensor(out=x[:, t, :], in0=bank[7][:, 0:C], scalar=pt[:, 3, t % 2:t % 2 + 1],
                                         in1=x[:, t, :], op0=ALU.mult, op1=ALU.add).then_inc(sem("x2_ready"), 1)

            dve.wait_ge(sem("qb_in"), 32)
            for t in range(-3, NT + 1):
                if t + 3 < NT:
                    quant_rows(t + 3, st[:, 2, :], "q1_ready", "q1t_ready")
                if 0 <= t + 1 < NT:
                    l1_pre(t + 1)
                if 0 <= t < NT:
                    l1_quant(t)
                if t >= 1:
                    l1_out(t - 1)

            make_cond(2)
            dve.wait_ge(sem("rt_in"), 16)
            chain(dve.tensor_copy(rthi[:], rtraw[:]))
            dve.tensor_tensor(rtlo[:], rtraw[:], rthi[:].bitcast(F32), ALU.subtract).then_inc(sem("rt_split"), 1)
            cond_low(4)
            lg = bank[4][:, 0:NT * E2].rearrange("p (t e) -> p t e", e=E2)

            def per_token(i):
                return r2[:, i, :, 0:1].to_broadcast([P, NT, E2])

            dve.wait_ge(sem("logit_ready"), 1)
            chain(dve.tensor_reduce(r2[:, 0, :, 0:1], lg, AX.X, ALU.max))
            dve.tensor_tensor(r2[:, 1, :, :], lg, per_token(0), ALU.subtract).then_inc(sem("lsub_ready"), 1)
            dve.wait_ge(sem("lexp_ready"), 1)
            chain(dve.tensor_reduce(r2[:, 2, :, 0:1], r2[:, 1, :, :], AX.X, ALU.add))
            chain(dve.reciprocal(r2[:, 3, :, 0:1], r2[:, 2, :, 0:1]))
            chain(dve.tensor_tensor(r2[:, 4, :, :], r2[:, 1, :, :], per_token(3), ALU.mult))
            sq = [r2c[:, i, :, :].rearrange("p t (g h) -> p t g h", g=E2) for i in range(2)]
            ranks(r2[:, 4, :, :], low8, E2, sq[0], sq[1], r2[:, 5, :, :])
            chain(dve.tensor_scalar(r2[:, 5, :, :], r2[:, 5, :, :], 2.0, None, ALU.is_lt))
            chain(dve.tensor_tensor(r2[:, 6, :, :], r2[:, 5, :, :], r2[:, 4, :, :], ALU.mult))
            chain(dve.tensor_reduce(r2[:, 7, :, 0:1], r2[:, 6, :, :], AX.X, ALU.add))
            chain(dve.reciprocal(r2[:, 8, :, 0:1], r2[:, 7, :, 0:1]))
            chain(dve.tensor_tensor(cw2[:], r2[:, 6, :, :], per_token(8), ALU.mult))
            def ternary_scale(m):
                dve.wait_ge(sem("t_in"), 16 * m + 16)
                dve.tensor_reduce(ws[:, 9 + m:10 + m], traw[:], AX.X, ALU.add, apply_absolute_value=True).then_inc(sem("tsum_part"), 1)
                dve.wait_ge(sem("tsum_ready"), m + 1)
                chain(dve.tensor_scalar(ws[:, 15 + m:16 + m], ws[:, 12 + m:13 + m], 1.0 / (C * HID), 1e-5, ALU.mult, ALU.max))
                dve.reciprocal(ws[:, 18 + m:19 + m], ws[:, 15 + m:16 + m]).then_inc(sem("tscale_ready"), 1)

            def glu_h(e, s, j):
                u, p = 8 * e + 4 * s + j, j % 2
                wait(dve, sem("sl_ready"), u + 1)
                dve.tensor_tensor(hh[:, p, :], bank[2 * p + 1][:], sl[:, p, :], ALU.mult).then_inc(sem("hh_ready"), 1)
                wait(dve, sem("d_done"), 8 * e - 4 + 4 * s)
                wait(dve, sem("hh_ready"), u + 1)
                dve.tensor_copy(hhi[:, s, j, :], hh[:, p, :]).then_inc(sem("hhi_ready"), 1)
                wait(dve, sem("hhi_ready"), u + 1)
                dve.tensor_tensor(hlo[:, s, j, :], hh[:, p, :], hhi[:, s, j, :].bitcast(F32), ALU.subtract
                                  ).then_inc(sem("hlo_ready"), 1)

            cw2f = cw2[:].rearrange("p t e -> p (t e)")

            def glu_step(e, p):
                n = 3 * NBLK + e
                wkv_kup(n, 3, e, p)
                for s in range(2):
                    for j in range(4):
                        glu_h(e, s, j)
                        if j % 2:
                            wkv_scan(n, 3, e, p, 2 * s + j // 2)
                wkv_gain(n, 3, e, p)
                for t in range(NT):
                    v = 8 * e + t
                    wait(dve, sem("d_done"), v + 1)
                    dve.scalar_tensor_tensor(out=x[:, t, :], in0=bank[4 + t % 4][:, 0:C], scalar=col(cw2f, E2 * t + e),
                                             in1=x[:, t, :], op0=ALU.mult, op1=ALU.add).then_inc(sem("acc_ready"), 1)

            for e in range(4):
                glu_step(e, e % 2)
                if e < 3:
                    ternary_scale(e)
            with dve.Fori(2, E2 // 2) as i:
                glu_step(2 * i, 0)
                glu_step(2 * i + 1, 1)

            make_cond(3)
            dve.wait_ge(sem("cond_ready"), 16)
            dve.tensor_reduce(st[:, 6, :], cond[:], AX.X, ALU.max, apply_absolute_value=True).then_inc(sem("c3_max"), 1)
            dve.tensor_scalar(ws[:, 21:24], ws[:, 15:18], 1.0 / Q, None, ALU.mult)
            dve.wait_ge(sem("c3_stat"), 1)
            chain(dve.tensor_scalar(st[:, 7, :], st[:, 7, :], 1e-5, None, ALU.max))
            chain(dve.reciprocal(st[:, 8, :], st[:, 7, :]))
            chain(dve.tensor_tensor(st[:, 8, :], st[:, 8, :], st[:, 5, :], ALU.mult))
            dve.tensor_scalar(st[:, 8, :], st[:, 8, :], Q, None, ALU.mult)
            dve.tensor_scalar(st[:, 9, :], st[:, 7, :], ws[:, 21:22], None, ALU.mult)
            chain(dve.tensor_scalar(st[:, 10, :], st[:, 7, :], ws[:, 22:23], None, ALU.mult))

            def l3_h(t):
                p = t % 2
                wait(dve, sem("q2t_ready3"), 2 * t - 2)
                for h in range(2):
                    dve.wait_ge(sem("silu3_ready"), 2 * t + h + 1)
                    dve.scalar_tensor_tensor(out=gl[:, p, 512 * h:512 * h + 512], in0=bank[2 + h][:],
                                                   scalar=st[:, 10, t:t + 1], in1=xp[:, p, 512 * h:512 * h + 512],
                                                   op0=ALU.mult, op1=ALU.mult).then_inc(sem("h3_ready"), 1)

            def l3_max(t):
                p = t % 2
                dve.wait_ge(sem("h3_ready"), 2 * t + 2)
                dve.tensor_reduce(pt[:, 6, p:p + 1], gl[:, p, :], AX.X, ALU.max, apply_absolute_value=True
                                  ).then_inc(sem("h3_max"), 1)

            def l3_quant(t):
                p = t % 2
                dve.wait_ge(sem("h3_stat"), t + 1)
                chain(dve.tensor_scalar(pt[:, 0, p:p + 1], pt[:, 7, p:p + 1], 1e-5, None, ALU.max))
                chain(dve.reciprocal(pt[:, 1, p:p + 1], pt[:, 0, p:p + 1]))
                dve.tensor_scalar(pt[:, 3, p:p + 1], pt[:, 0, p:p + 1], ws[:, 23:24], None, ALU.mult)
                chain(dve.tensor_scalar(pt[:, 2, p:p + 1], pt[:, 1, p:p + 1], pt[:, 5, p:p + 1], Q, ALU.mult, ALU.mult))
                dve.tensor_scalar(gl[:, p, :], gl[:, p, :], pt[:, 2, p:p + 1], ROUND, ALU.mult, ALU.add
                                  ).then_inc(sem("q23_ready"), 1)

            def l3_out(t):
                dve.wait_ge(sem("m2_ready3"), t + 1)
                dve.scalar_tensor_tensor(out=x[:, t, :], in0=bank[7][:, 0:C], scalar=pt[:, 3, t % 2:t % 2 + 1],
                                         in1=x[:, t, :], op0=ALU.mult, op1=ALU.add).then_inc(sem("x4_ready"), 1)

            for t in range(-3, NT + 1):
                if t + 3 < NT:
                    quant_rows(t + 3, st[:, 8, :], "q13_ready", "q1t3_ready")
                if 0 <= t + 1 < NT:
                    l3_h(t + 1)
                    l3_max(t + 1)
                if 0 <= t < NT:
                    l3_quant(t)
                if t >= 1:
                    l3_out(t - 1)

        @block.tensor
        def _(pe):
            def mm3(out, lhs, rhs, start, stop):
                pe.matmul(out, lhs[0], rhs[0], start=start, stop=False)
                pe.matmul(out, lhs[0], rhs[1], start=False, stop=False)
                return pe.matmul(out, lhs[1], rhs[0], start=False, stop=stop)

            def turn_gain(l):
                for b in range(B):
                    m = 4 * l + b
                    pe.wait_ge(sem("G_ready"), 2 * b + 2 if l == 0 else DONE[l])
                    wait(pe, sem("cond_ready"), m - 1)
                    for u in range(2):
                        for k in range(KC):
                            ins = pe.transpose(bank[b % 2][:, u * C + k * P:u * C + k * P + P],
                                               GT[:, l % 2, 2 * b + k, u * P:u * P + P], ident[:])
                    ins.then_inc(sem("G_turned"), 1)

            def turn_cond(l, n0):
                for s in range(2):
                    pe.wait_ge(sem("cond_ready"), 4 * l + 2 * s + 2)
                    for k in range(KC):
                        n = n0 + 2 * s + k
                        wait(pe, sem("cT_low"), n - 1)
                        for j in range(TH):
                            ins = pe.transpose(bank[2 + n % 2][:, j * P:j * P + P], cond[:, TH * s + j, k * P:k * P + P], ident[:])
                        ins.then_inc(sem("cT_ready"), 1)

            def cT(k, a, b):
                return cThi[:, k, a:b], cTlo[:, k, a:b]

            pe.wait_ge(sem("ident_ready"), 1)
            turn_gain(0)
            turn_cond(0, 0)
            pe.wait_ge(sem("sm_low"), 1)
            pe.wait_ge(sem("cT_low"), 4)
            for t in range(NT):
                for k in range(KC):
                    ins = mm3(bank[4][:, t * E0:t * E0 + E0], cT(k, t * P, t * P + P),
                              (sm_hi[:, k, 0:E0], sm_lo[:, k, 0:E0]), k == 0, k == KC - 1)
            ins.then_inc(sem("gate_ready"), 1)
            for s in range(2):
                for k in range(KC):
                    w = slice(E0, E0 + LAT)
                    ins = mm3(bank[5 + s][:], (sm_hi[:, k, w], sm_lo[:, k, w]), cT(k, HALF * s, HALF * s + HALF),
                              k == 0, k == KC - 1)
                ins.then_inc(sem("xl_ready"), 1)

            def shared_up(u):
                s, j = u // 4, u % 4
                wait(pe, sem("sh_ready"), u - 3)
                for k in range(KC):
                    w = slice(E0 + LAT + j * P, E0 + LAT + j * P + P)
                    ins = mm3(bank[u % 4][:], (sm_hi[:, k, w], sm_lo[:, k, w]), cT(k, HALF * s, HALF * s + HALF),
                              k == 0, k == KC - 1)
                ins.then_inc(sem("sz_ready"), 1)

            def shared_down(s):
                pe.wait_ge(sem("sh_ready"), 4 * s + 4)
                for v in range(2 * s, 2 * s + 2):
                    if v == 0:
                        pe.wait_ge(sem("score_ready"), 1)
                    if v == 1 or v == 2:
                        pe.wait_ge(sem("xl_low"), v)
                    for half in range(2):
                        t = 2 * (v % 2) + half
                        for j in range(4):
                            ins = pe.matmul(bank[4 + v][:, half * C:half * C + C], hx[:, s, j, t * P:t * P + P],
                                            downw[:, j, :], start=(j == 0), stop=(j == 3))
                    ins.then_inc(sem("sd_ready"), 1)

            for u in range(8):
                shared_up(u)
            pe.wait_ge(sem("down_in"), 16)
            shared_down(0)
            shared_down(1)

            def expert_z(q, i, o, j):
                slot, t = (o // 2) % 2, TH * (o % 2) + j
                wait(pe, sem("h0_ready"), 4 * q - 3 + j)
                if j == 0 and o % 2 == 0:
                    wait(pe, sem("w1_split"), 2 * i + o // 2 + 1)
                w = (w1hi[:, slot, :], w1lo[:, slot, :])
                mm3(bank[j][:], (xlhi[:, t * P:t * P + P], xllo[:, t * P:t * P + P]), w, True, True).then_inc(sem("z_ready"), 1)

            def expert_turn(q, o, e):
                if e == 0:
                    wait(pe, sem("h0_ready"), 4 * q + 4)
                wait(pe, sem("hT_ready"), 4 * q + e - 1)
                for j in range(4):
                    ins = pe.transpose(bank[6 + e % 2][:, j * P:j * P + P], hx[:, o % 2, j, e * P:e * P + P], ident[:])
                ins.then_inc(sem("t_ready"), 1)

            def expert_y(q, i, o, e):
                slot = o // 2
                if o % 2 == 0 and e == 0:
                    pe.wait_ge(sem(f"w2_in{slot}"), 16 * (i + 1))
                wait(pe, sem("hT_ready"), 4 * q + e + 1)
                pe.matmul(bank[4 + o % 2][:], w2raw[:, slot, e, :], hT[:, e % 2, :], start=False, stop=False,
                          skip_group_check=True).then_inc(sem("y_done"), 1)

            pe.wait_ge(sem("sx_done"), 4)
            for s in range(2):
                pe.matmul(bank[4 + s][:], zeros[:], hx[:, 1, 0, :], start=True, stop=False, skip_group_check=True)
            pe.wait_ge(sem("sh_ready"), 8)
            for j in range(4):
                expert_z(0, 0, 0, j)

            def expert_steps(i, last):
                for o in range(4):
                    q = 4 * i + o
                    z = (lambda j: None) if last and o == 3 else (lambda j: expert_z(q + 1, i, o + 1, j))
                    z(0)
                    z(1)
                    expert_turn(q, o, 0)
                    z(2)
                    expert_turn(q, o, 1)
                    expert_y(q, i, o, 0)
                    z(3)
                    expert_turn(q, o, 2)
                    expert_y(q, i, o, 1)
                    expert_turn(q, o, 3)
                    expert_y(q, i, o, 2)
                    expert_y(q, i, o, 3)

            expert_steps(0, False)
            with pe.Fori(1, EG // 2 - 1) as i:
                expert_steps(i, False)
            expert_steps(EG // 2 - 1, True)
            for s in range(2):
                ins = pe.matmul(bank[4 + s][:], zeros[:], hx[:, 1, 0, :], start=False, stop=True, skip_group_check=True)
            ins.then_inc(sem("y_closed"), 1)
            pe.wait_ge(sem("fc2_in"), 16)
            for s in range(2):
                pe.wait_ge(sem("ylat_ready"), s + 1)
                for v in range(2 * s, 2 * s + 2):
                    for half in range(2):
                        t = 2 * (v % 2) + half
                        ins = pe.matmul(bank[v][:, half * C:half * C + C], ylat[:, s, t * P:t * P + P], fc2w[:],
                                        start=True, stop=True)
                    ins.then_inc(sem("fo_ready"), 1)

            turn_gain_1 = turn_gain
            pe.wait_ge(sem("x1_ready"), 2)
            turn_gain_1(1)
            pe.wait_ge(sem("q_quant"), 2)

            def first(t, tag, quant, weights, banks):
                p = t % 2
                pe.wait_ge(sem(quant), t + 1)
                wait(pe, sem("q1T" + tag + "_ready"), t)
                for k in range(KC):
                    ins = pe.transpose(bank[4][:, k * P:k * P + P], qf[:, p, k * P:k * P + P], ident[:])
                ins.then_inc(sem("q1t" + tag + "_ready"), 1)
                pe.wait_ge(sem("q1T" + tag + "_ready"), t + 1)
                if not tag:
                    wait(pe, sem("pre_ready"), t - 1)
                for n, (b, w) in enumerate(zip(banks(p), weights)):
                    if tag and n % 2 == 0:
                        wait(pe, sem("h3_ready"), 2 * t + n // 2 - 1)
                    for k in range(KC):
                        ins = pe.matmul(bank[b][:], qT[:, p, k, :], w(k), start=(k == 0), stop=(k == KC - 1))
                    if n % 2:
                        ins.then_inc(sem("m1" + tag + "_ready"), 1)

            def second(t, tag, quant, out_ready, weight):
                p = t % 2
                pe.wait_ge(sem(quant), t + 1)
                for h in range(2):
                    wait(pe, sem("q2T_ready" + tag), 2 * t - 1 + h)
                    for j in range(4):
                        c = 4 * h + j
                        ins = pe.transpose(bank[5 + h][:, j * P:j * P + P], gl[:, p, c * P:c * P + P], ident[:])
                    ins.then_inc(sem("q2t_ready" + tag), 1)
                wait(pe, sem(out_ready), t)
                for c in range(8):
                    if c % 4 == 0:
                        pe.wait_ge(sem("q2T_ready" + tag), 2 * t + c // 4 + 1)
                    ins = pe.matmul(bank[7][:, 0:C], q2T[:, p, c, :], weight(c), start=(c == 0), stop=(c == 7))
                ins.then_inc(sem("m2_ready" + tag), 1)

            w_first = [lambda k, h=h: q1w[:, k, 512 * h:512 * h + 512] for h in range(2)]
            pe.wait_ge(sem("cond_ready"), 8)
            for t in range(-2, NT):
                if t + 2 < NT:
                    first(t + 2, "", "q1_ready", w_first, lambda p: (2 * p, 2 * p + 1))
                if t >= 0:
                    second(t, "", "q2_ready", "x2_ready", lambda c: q2w[:, c, :])

            turn_gain(2)
            turn_cond(2, 4)
            pe.wait_ge(sem("rt_split"), 1)
            pe.wait_ge(sem("cT_low"), 8)
            for t in range(NT):
                for k in range(KC):
                    ins = mm3(bank[4][:, t * E2:t * E2 + E2], cT(k, t * P, t * P + P), (rthi[:, k, :], rtlo[:, k, :]),
                              k == 0, k == KC - 1)
            ins.then_inc(sem("logit_ready"), 1)

            def glu_step(e):
                pe.wait_ge(sem("gu_split"), e + 1)
                for s in range(2):
                    for j in range(4):
                        u, p = 8 * e + 4 * s + j, j % 2
                        wait(pe, sem("hh_ready"), u - 1)
                        for up in range(2):
                            for k in range(KC):
                                w = slice(up * I2 + j * P, up * I2 + j * P + P)
                                ins = mm3(bank[2 * p + up][:], (guhi[:, k, w], gulo[:, k, w]),
                                          cT(k, HALF * s, HALF * s + HALF), k == 0, k == KC - 1)
                        ins.then_inc(sem("gu_done"), 1)
                pe.wait_ge(sem("dn_split"), e + 1)
                for s in range(2):
                    wait(pe, sem("hlo_ready"), 8 * e + 4 * s + 4)
                    for t in range(TH):
                        v = 8 * e + 4 * s + t
                        wait(pe, sem("acc_ready"), v - 3)
                        for j in range(4):
                            ins = mm3(bank[4 + t][:, 0:C], (hhi[:, s, j, t * P:t * P + P], hlo[:, s, j, t * P:t * P + P]),
                                      (dnhi[:, j, :], dnlo[:, j, :]), j == 0, j == 3)
                        ins.then_inc(sem("d_done"), 1)

            pe.wait_ge(sem("lexp_ready"), 1)
            glu_step(0)
            with pe.Fori(1, E2) as e:
                glu_step(e)

            turn_gain(3)
            pe.wait_ge(sem("t_quant"), 3)
            pe.wait_ge(sem("cond_ready"), 16)
            w_first = [lambda k, m=m, h=h: tw[:, m, HID * k + 512 * h:HID * k + 512 * h + 512]
                       for h in range(2) for m in range(2)]
            for t in range(-2, NT):
                if t + 2 < NT:
                    first(t + 2, "3", "q13_ready", w_first, lambda p: (0, 2, 1, 3))
                if t >= 0:
                    second(t, "3", "q23_ready", "x4_ready", lambda c: tw[:, 2, C * c:C * c + C])


def kernel(x, fside_BxSxS_0, cond_512, L0_cond_w, L0_cond_u, L0_ffn_gate_w, L0_ffn_gate_bias, L0_ffn_fc1_w,
           L0_ffn_fc2_w, L0_ffn_w1, L0_ffn_w2, L0_ffn_shared_up_w, L0_ffn_shared_down_w, L1_cond_w, L1_cond_u,
           L1_ffn_W1, L1_ffn_B1, L1_ffn_W2, L1_ffn_B2, L2_cond_w, L2_cond_u, L2_ffn_gate_weight,
           L2_ffn_gate_up_proj, L2_ffn_down_proj, L3_cond_w, L3_cond_u, L3_ffn_w1, L3_ffn_w2, L3_ffn_w3):
    import numpy as np
    import concourse.bacc as bacc
    from concourse.bass_utils import run_bass_kernel_spmd

    def rows(w, inner):
        w = np.asarray(w).T
        return w.reshape(inner // P, P, w.shape[1]).transpose(1, 0, 2)

    def spread(v):
        v = np.asarray(v).reshape(1, -1)
        return np.broadcast_to(v, (P, v.shape[1]))

    def channels(*vs):
        return np.stack([np.asarray(v).reshape(KC, P).T for v in vs], axis=1)

    xs = np.asarray(x)
    small = np.concatenate([rows(L0_ffn_gate_w, C), rows(L0_ffn_fc1_w, C), rows(L0_ffn_shared_up_w, C)], axis=2)
    gu = np.asarray(L2_ffn_gate_up_proj).transpose(0, 2, 1).reshape(E2, KC, P, 2 * I2).transpose(0, 2, 1, 3)
    dn = np.asarray(L2_ffn_down_proj).transpose(0, 2, 1).reshape(E2, I2 // P, P, C).transpose(0, 2, 1, 3)
    ins = {
        "x": xs.reshape(NT, P, C).transpose(1, 0, 2),
        "kt": np.asarray(fside_BxSxS_0).reshape(B, S, KC, P).transpose(3, 0, 2, 1).reshape(P, NBLK, S),
        "te": spread(cond_512).reshape(P, B, 64),
        "w": channels(L0_cond_w, L1_cond_w, L2_cond_w, L3_cond_w),
        "u": channels(L0_cond_u, L1_cond_u, L2_cond_u, L3_cond_u),
        "sm": small,
        "gbias": spread(L0_ffn_gate_bias),
        "down": rows(L0_ffn_shared_down_w, SH),
        "fc2": np.asarray(L0_ffn_fc2_w).T,
        "w1": np.asarray(L0_ffn_w1).transpose(2, 0, 1).reshape(P, EG, 4 * INTER),
        "w2": np.asarray(L0_ffn_w2).transpose(2, 0, 1).reshape(P, EG, 4, LAT),
        "q1": rows(L1_ffn_W1, C), "q1b": spread(L1_ffn_B1),
        "q2": rows(L1_ffn_W2, HID), "q2b": spread(L1_ffn_B2),
        "rt": rows(L2_ffn_gate_weight, C),
        "gu": gu, "dn": dn,
        "t1": rows(L3_ffn_w1, C).reshape(P, -1), "t2": rows(L3_ffn_w2, C).reshape(P, -1),
        "t3": rows(L3_ffn_w3, HID).reshape(P, -1),
    }
    nc = bacc.Bacc("TRN2", target_bir_lowering=False, num_devices=1)
    arrays, args = {}, []
    for name, a in ins.items():
        a = np.ascontiguousarray(a)
        arrays["in_" + name] = a
        args.append(nc.dram_tensor("in_" + name, a.shape, mybir.dt.from_np(a.dtype), kind="ExternalInput").ap())
    out = nc.dram_tensor("out_x", (P, NT, C), F32, kind="ExternalOutput").ap()
    build(nc, *args, out)
    got = run_bass_kernel_spmd(nc, [arrays], core_ids=[0]).results[0]["out_x"]
    return np.ascontiguousarray(got.transpose(1, 0, 2)).reshape(xs.shape)
```

```python
from contextlib import ExitStack

import concourse.bass as bass
from concourse import mybir

F32 = mybir.dt.float32
F32R = mybir.dt.float32r
BF16 = mybir.dt.bfloat16
ALU = mybir.AluOpType
ACT = mybir.ActivationFunctionType
AX = mybir.AxisListType

P = 128
B, S, C = 4, 256, 256
TOK = B * S
NT = TOK // P
KC = C // P
NBLK = B * KC
HALF = TOK // 2
TH = NT // 2
LAT = INTER = 128
E0, G0 = 32, 4
EG = E0 // G0
SH = 512
HID = 1024
E2, I2 = 8, 512
ROUND = 12582912.0
Q = 127.0
ROUTED_SCALE = 2.5


def wait(eng, sem, value):
    if not isinstance(value, int) or value > 0:
        eng.wait_ge(sem, value)


def build(nc, x_d, kt_d, te_d, w_d, u_d, sm_d, gbias_d, down_d, fc2_d, w1_d, w2_d,
          q1_d, q1b_d, q2_d, q2b_d, rt_d, gu_d, dn_d, t1_d, t2_d, t3_d, out_d):
    with ExitStack() as ctx:
        sems = {}

        def sem(name):
            if name not in sems:
                sems[name] = ctx.enter_context(nc.semaphore(name))
            return sems[name]

        cursor = [-(-nc.sbuf_base // 32) * 32]

        def sb(name, shape, dt=F32):
            size = 2 if dt == BF16 else 4
            for n in shape[1:]:
                size *= n
            t = nc.alloc_sbuf_tensor_at(name, shape, dt, offset=cursor[0])
            cursor[0] += -(-size // 32) * 32
            return t

        ident = sb("ident", [P, P])
        x = sb("x", [P, NT, C])
        kT = sb("kT", [P, NBLK, S])
        ekk = sb("ekk", [P, NBLK, 2, S])
        GT = sb("GT", [P, 2, NBLK, S])
        eu = sb("eu", [P, 2, 2, S])
        fw = sb("fw", [P, 2, 2, S])
        ekb = sb("ekb", [P, 2, 2, S])
        bw = sb("bw", [P, 2, 2, S])
        cond = sb("cond", [P, NT, C])
        cThi = sb("cThi", [P, KC, TOK], F32R)
        cTlo = sb("cTlo", [P, KC, TOK], F32R)
        b1bc = sb("b1bc", [P, HID])
        b2bc = sb("b2bc", [P, C])
        te = sb("te", [P, B, 64])
        wl = sb("wl", [P, 4, KC])
        ul = sb("ul", [P, 4, KC])
        dec = sb("dec", [P, 4, B, KC])
        ubk = sb("ubk", [P, 4, B, KC])
        gain = sb("gain", [P, B, KC])
        tfb = sb("tfb", [P, 4, B])
        low4 = sb("low4", [P, G0, G0])
        low8 = sb("low8", [P, E2, E2])
        cw0 = sb("cw0", [P, NT, E0])
        cw2 = sb("cw2", [P, NT, E2])
        st = sb("st", [P, 12, NT])
        pt = sb("pt", [P, 8, 2])
        ws = sb("ws", [P, 24])
        region = cursor[0]

        sm_raw = sb("sm_raw", [P, KC, E0 + LAT + SH])
        sm_hi = sb("sm_hi", [P, KC, E0 + LAT + SH], F32R)
        sm_lo = sb("sm_lo", [P, KC, E0 + LAT + SH], F32R)
        downw = sb("downw", [P, SH // P, C])
        fc2w = sb("fc2w", [P, C])
        xlhi = sb("xlhi", [P, TOK], F32R)
        xllo = sb("xllo", [P, TOK], F32R)
        hx = sb("hx", [P, 2, TH, 512])
        hT = sb("hT", [P, 2, 512])
        rl = sb("rl", [P, 2, 512])
        w1raw = sb("w1raw", [P, 2, 512])
        w1hi = sb("w1hi", [P, 2, 512], F32R)
        w1lo = sb("w1lo", [P, 2, 512], F32R)
        w2raw = sb("w2raw", [P, 2, 4, LAT])
        gbias = sb("gbias", [P, E0])
        rt = sb("rt", [P, 12, NT * E0])
        ylat = sb("ylat", [P, 2, HALF])
        top8 = sb("top8", [P, NT, 8])
        ends = [cursor[0]]

        cursor[0] = region
        guraw = sb("guraw", [P, KC, 2 * I2])
        dnraw = sb("dnraw", [P, I2 // P, C])
        guhi = sb("guhi", [P, KC, 2 * I2], F32R)
        gulo = sb("gulo", [P, KC, 2 * I2], F32R)
        dnhi = sb("dnhi", [P, I2 // P, C], F32R)
        dnlo = sb("dnlo", [P, I2 // P, C], F32R)
        rtraw = sb("rtraw", [P, KC, E2])
        rthi = sb("rthi", [P, KC, E2], F32R)
        rtlo = sb("rtlo", [P, KC, E2], F32R)
        region2 = cursor[0]
        hhi = sb("hhi", [P, 2, I2 // P, HALF], F32R)
        hlo = sb("hlo", [P, 2, I2 // P, HALF], F32R)
        sl = sb("sl", [P, 2, HALF])
        hh = sb("hh", [P, 2, HALF])
        r2 = sb("r2", [P, 10, NT, E2])
        r2c = sb("r2c", [P, 2, NT, E2 * E2])
        ends.append(cursor[0])

        cursor[0] = region2
        qf = sb("qf", [P, 2, C])
        qT = sb("qT", [P, 2, KC, P], BF16)
        xp = sb("xp", [P, 2, HID])
        gl = sb("gl", [P, 2, HID])
        q2T = sb("q2T", [P, 2, HID // P, P], BF16)
        junk = sb("junk", [P, HID])
        ends.append(cursor[0])

        cursor[0] = max(ends)
        region3 = cursor[0]
        q1raw = sb("q1raw", [P, KC, HID])
        q2raw = sb("q2raw", [P, HID // P, C])
        q1w = sb("q1w", [P, KC, HID], BF16)
        q2w = sb("q2w", [P, HID // P, C], BF16)
        cursor[0] = region3
        traw = sb("traw", [P, KC * HID])
        tw = sb("tw", [P, 3, KC * HID], BF16)
        assert max(cursor[0], region3 + 24 * 1024) <= nc.sbuf_usable_end

        bank = [ctx.enter_context(nc.psum_tensor(f"bank{i}", [P, 512], F32)) for i in range(8)]

        def one(ap, spec, **kw):
            return ap.rearrange(spec, **kw)

        DONE = [NBLK, 3 * NBLK, 3 * NBLK, 4 * NBLK]

        def sT(n):
            return (hT if n == E0 else hh)[0:n, :, :].rearrange("p a n -> p (a n)")

        def gain_bank(l, b):
            return bank[(0, 1, 4, 7)[b] if l == 0 else b % 2 + (2 if l == 1 else 0)]

        def cond_bank(n):
            return bank[(2, 3, 5, 6)[n] if n < 4 else 2 + n % 2]

        def down_bank(v):
            return bank[(5, 6, 4, 7)[v]]

        block = ctx.enter_context(nc.Block())

        @block.sync
        def _(sp):
            for b in range(B):
                sp.dma_start(kT[:, 2 * b:2 * b + 2, :], kt_d[:, 2 * b:2 * b + 2, :]).then_inc(sem(f"kT_in{b}"), 16)
                if b == 0:
                    for dst, src in ((te, te_d), (wl, w_d), (ul, u_d)):
                        sp.dma_start(dst[:], src).then_inc(sem("small_in"), 16)
                if b < 2:
                    sp.dma_start(x[:, TH * b:TH * b + TH, :], x_d[:, TH * b:TH * b + TH, :]).then_inc(sem(f"x_in{b}"), 16)
            sp.dma_start(sm_raw[:], sm_d).then_inc(sem("sm_in"), 16)
            sp.dma_start(gbias[:], gbias_d).then_inc(sem("gbias_in"), 16)
            sp.dma_start(downw[:], down_d).then_inc(sem("down_in"), 16)
            sp.dma_start(fc2w[:], fc2_d).then_inc(sem("fc2_in"), 16)
            for dst, src in ((q1raw, q1_d), (q2raw, q2_d)):
                sp.dma_start(dst[:], src).then_inc(sem("q_in"), 16)
            for dst, src in ((b1bc, q1b_d), (b2bc, q2b_d)):
                sp.dma_start(dst[:], src).then_inc(sem("qb_in"), 16)

            def expert_weights(i, o):
                eg = 2 * i + o
                wait(sp, sem("w1_split"), eg - 1)
                sp.dma_start(w1raw[:, o, :], w1_d[:, eg, :]).then_inc(sem(f"w1_in{o}"), 16)
                wait(sp, sem("y_done"), 8 * eg - 8)
                sp.dma_start(w2raw[:, o, :, :], w2_d[:, eg, :, :]).then_inc(sem(f"w2_in{o}"), 16)

            expert_weights(0, 0)
            expert_weights(0, 1)
            with sp.Fori(1, EG // 2) as i:
                expert_weights(i, 0)
                expert_weights(i, 1)

            sp.wait_ge(sem("x1_ready"), 4)
            sp.dma_start(rtraw[:], rt_d).then_inc(sem("rt_in"), 16)

            def glu_weights(e):
                wait(sp, sem("gu_split"), e)
                sp.dma_start(guraw[:], gu_d[bass.ds(e, 1), :, :, :].rearrange("o p k n -> p (o k) n")
                             ).then_inc(sem("gu_in"), 16)
                wait(sp, sem("dn_split"), e)
                sp.dma_start(dnraw[:], dn_d[bass.ds(e, 1), :, :, :].rearrange("o p k n -> p (o k) n")
                             ).then_inc(sem("dn_in"), 16)

            glu_weights(0)
            sp.wait_ge(sem("x2_ready"), NT)
            for m, src in enumerate((t1_d, t2_d, t3_d)):
                wait(sp, sem("t_quant"), m)
                sp.dma_start(traw[:], src).then_inc(sem("t_in"), 16)
                if m < 2:
                    glu_weights(m + 1)
            with sp.Fori(3, E2) as e:
                glu_weights(e)
            for t in range(NT):
                sp.wait_ge(sem("x4_ready"), t + 1)
                sp.dma_start(out_d[:, t, :], x[:, t, :]).then_inc(sem("out_done"), 16)
            sp.wait_ge(sem("out_done"), 16 * NT)

        @block.gpsimd
        def _(pool):
            def wait_alone(name, value):
                wait(pool, sem(name), value)
                if not isinstance(value, int):
                    pool.sem_inc(sem("pool_waited"), 1)

            pool.memset(ident[:], 0.0).then_inc(sem("consts"), 1)
            pool.memset(low4[:], 1.0).then_inc(sem("consts"), 1)
            pool.memset(low8[:], 1.0).then_inc(sem("consts"), 1)
            pool.memset(bw[:], 0.0).then_inc(sem("bw_zero"), 1)
            pool.wait_ge(sem("consts"), 3)
            pool.affine_select(out=ident[:], in_=ident[:], compare_op=ALU.not_equal, fill=1.0, base=0,
                               pattern=[[-1, P]], channel_multiplier=1).then_inc(sem("ident_ready"), 1)
            for low, n in ((low4, G0), (low8, E2)):
                pool.affine_select(out=low[:], in_=low[:], compare_op=ALU.is_gt, fill=0.0, base=0,
                                   pattern=[[1, n], [-1, n]], channel_multiplier=0).then_inc(sem("low_ready"), 1)

            def wkv_sums(n, blk, p):
                wait_alone("eu_ready", n + 1)
                pool.tensor_tensor(eu[:, p, 0, :], eu[:, p, 1, :], kT[:, blk, :], ALU.mult).then_inc(sem("euv_ready"), 1)
                wait_alone("scan_ready", n + 1)
                pool.tensor_tensor(fw[:, p, :, :], fw[:, p, :, :], bw[:, p, :, :], ALU.add).then_inc(sem("both_ready"), 1)
                wait_alone("euv_ready", n + 1)
                wait_alone("both_ready", n + 1)
                pool.tensor_tensor(fw[:, p, :, :], fw[:, p, :, :], eu[:, p, :, :], ALU.add).then_inc(sem("sums_ready"), 1)

            for n in range(NBLK):
                wkv_sums(n, n, n % 2)

            def split_w1(i, o):
                eg = 2 * i + o
                wait_alone(f"w1_in{o}", 16 * (i + 1))
                wait_alone("z_ready", 8 * eg - 8)
                pool.tensor_scalar(w1hi[:, o, :], w1raw[:, o, :], 1.0, 0.0, ALU.mult, ALU.add).then_inc(sem("w1_high"), 1)
                wait_alone("w1_high", eg + 1)
                pool.tensor_tensor(w1lo[:, o, :], w1raw[:, o, :], w1hi[:, o, :].bitcast(F32), ALU.subtract
                                   ).then_inc(sem("w1_split"), 1)

            split_w1(0, 0)
            split_w1(0, 1)

            def expert_steps(i, last):
                for o in range(4):
                    q = 4 * i + o
                    if o % 2 and not last:
                        split_w1(i + 1, o // 2)
                    wkv_sums(NBLK + q, 2 * i + o // 2, o % 2)
                    if isinstance(i, int) and i == 0 and o == 1:
                        pool.wait_ge(sem("wmax_part"), 2)
                        pool.partition_all_reduce(ws[:, 2:4], ws[:, 0:2], P, bass.bass_isa.ReduceOp.max
                                                  ).then_inc(sem("wmax_ready"), 1)
                    if isinstance(i, int) and i == 0 and o >= 2:
                        raw = (q1raw, q2raw)[o - 2]
                        pool.wait_ge(sem("wscale_ready"), 1)
                        pool.tensor_scalar(raw[:], raw[:], ws[:, 4 + o:5 + o], ROUND, ALU.mult, ALU.add
                                           ).then_inc(sem("q_round"), 1)
                    if last and o < 2:
                        pool.wait_ge(sem("q_round"), o + 1)
                        pool.tensor_scalar((q1w, q2w)[o][:], (q1raw, q2raw)[o][:], -ROUND, 1.0, ALU.add, ALU.mult
                                           ).then_inc(sem("q_quant"), 1)

            expert_steps(0, False)
            with pool.Fori(1, EG // 2 - 1) as i:
                expert_steps(i, False)
            expert_steps(EG // 2 - 1, True)

            def quant_rows(t, scale, known, ready, free):
                p = t % 2
                pool.wait_ge(sem(known), t // TH + 1)
                wait(pool, sem(free), t - 1)
                pool.tensor_scalar(qf[:, p, :], cond[:, t, :], scale[:, t:t + 1], ROUND, ALU.mult, ALU.add
                                   ).then_inc(sem(ready), 1)

            for t in range(3):
                quant_rows(t, st[:, 2, :], "row_scale", "q1_ready", "q1t_ready")
            pool.wait_ge(sem("qb_in"), 32)
            for t in range(NT):
                if t + 3 < NT:
                    quant_rows(t + 3, st[:, 2, :], "row_scale", "q1_ready", "q1t_ready")
                pool.wait_ge(sem("sig_ready"), 2 + t // TH + 1)
                pool.tensor_tensor(x[:, t, :], x[:, t, :], b2bc[:], ALU.add).then_inc(sem("xb_ready"), 1)

            def split_glu(e):
                wait_alone("gu_in", 16 * (e + 1))
                wait_alone("gu_done", 8 * e)
                for k in range(KC):
                    pool.tensor_scalar(guhi[:, k, :], guraw[:, k, :], 1.0, 0.0, ALU.mult, ALU.add).then_inc(sem("gu_high"), 1)
                for k in range(KC):
                    wait_alone("gu_high", 2 * e + k + 1)
                    ins = pool.tensor_tensor(gulo[:, k, :], guraw[:, k, :], guhi[:, k, :].bitcast(F32), ALU.subtract)
                ins.then_inc(sem("gu_split"), 1)
                wait_alone("dn_in", 16 * (e + 1))
                wait_alone("d_done", 8 * e)
                pool.tensor_scalar(dnhi[:], dnraw[:], 1.0, 0.0, ALU.mult, ALU.add).then_inc(sem("dn_high"), 1)
                wait_alone("dn_high", e + 1)
                pool.tensor_tensor(dnlo[:], dnraw[:], dnhi[:].bitcast(F32), ALU.subtract).then_inc(sem("dn_split"), 1)

            def ternary(m):
                pool.wait_ge(sem("tsum_part"), m + 1)
                pool.partition_all_reduce(ws[:, 12 + m:13 + m], ws[:, 9 + m:10 + m], P,
                                          bass.bass_isa.ReduceOp.add).then_inc(sem("tsum_ready"), 1)
                pool.wait_ge(sem("tscale_ready"), m + 1)
                pool.tensor_scalar(traw[:], traw[:], ws[:, 18 + m:19 + m], ROUND, ALU.mult, ALU.add).then_inc(sem("t_step"), 1)
                pool.wait_ge(sem("t_step"), 2 * m + 1)
                pool.tensor_scalar(traw[:], traw[:], ROUND + 1.0, ROUND - 1.0, ALU.min, ALU.max).then_inc(sem("t_step"), 1)
                pool.wait_ge(sem("t_step"), 2 * m + 2)
                pool.tensor_scalar(tw[:, m, :], traw[:], -ROUND, 1.0, ALU.add, ALU.mult).then_inc(sem("t_quant"), 1)

            def glu_step(e, p):
                split_glu(e)
                wkv_sums(3 * NBLK + e - 1, e - 1, 1 - p)

            split_glu(0)
            for e in range(1, 4):
                glu_step(e, e % 2)
                ternary(e - 1)
            with pool.Fori(2, E2 // 2) as i:
                glu_step(2 * i, 0)
                glu_step(2 * i + 1, 1)
            wkv_sums(4 * NBLK - 1, NBLK - 1, 1)

            def rms_stats(mean_sq, root, absmax, out, sum_name, max_name, n, out_name):
                pool.wait_ge(sem(sum_name), n)
                pool.tensor_scalar(mean_sq, mean_sq, 1.0, 1e-6, ALU.mult, ALU.add).then_inc(sem("p3"), 1)
                p3[0] += 1
                pool.wait_ge(sem("p3"), p3[0])
                pool.tensor_tensor(root, mean_sq, half, ALU.pow).then_inc(sem("p3"), 1)
                p3[0] += 1
                pool.wait_ge(sem("p3"), p3[0])
                pool.wait_ge(sem(max_name), n)
                pool.tensor_tensor(out, absmax, root, ALU.mult).then_inc(sem(out_name), 1)

            p3 = [0]
            pool.memset(st[:, 11, :], -0.5).then_inc(sem("p3"), 1)
            p3[0] += 1
            pool.wait_ge(sem("p3"), p3[0])
            for s in range(2):
                half = st[:, 11, TH * s:TH * s + TH]
                rms_stats(*(st[:, i, TH * s:TH * s + TH] for i in range(4, 8)), "c3_sq", "c3_max", s + 1, "c3_stat")
            half = st[:, 11, 0:1]
            for t in range(3):
                quant_rows(t, st[:, 8, :], "c3_scale", "q13_ready", "q1t3_ready")
            for t in range(NT):
                p = t % 2
                if t + 3 < NT:
                    quant_rows(t + 3, st[:, 8, :], "c3_scale", "q13_ready", "q1t3_ready")
                rms_stats(pt[:, 4, p:p + 1], pt[:, 5, p:p + 1], pt[:, 6, p:p + 1], pt[:, 7, p:p + 1],
                          "h3_sq", "h3_max", t + 1, "h3_stat")

        @block.scalar
        def _(act):
            act.wait_ge(sem("small_in"), 48)
            act.activation(wl[:], wl[:], ACT.Exp).then_inc(sem("a0"), 1)
            act.wait_ge(sem("a0"), 1)
            act.activation(wl[:], wl[:], ACT.Exp, scale=-1.0).then_inc(sem("wl_ready"), 1)
            act.wait_ge(sem("te_sum"), 1)
            act.activation(tfb[:, 1, :], tfb[:, 0, :], ACT.Exp, scale=-1.0).then_inc(sem("te_exp"), 1)

            def wkv_exp(n, p):
                wait(act, sem("kup_ready"), n + 1)
                act.activation(eu[:, p, 1, :], eu[:, p, 1, :], ACT.Exp).then_inc(sem("eu_ready"), 1)

            def side_exp(b):
                act.wait_ge(sem("kmin_ready"), b + 1)
                act.activation(ekk[:, 2 * b:2 * b + 2, 1, :], ekk[:, 2 * b:2 * b + 2, 1, :], ACT.Exp).then_inc(sem("ek_ready"), 1)

            def sigmoid_x(l, halves=(0, 1)):
                for s in halves:
                    if l == 0:
                        act.wait_ge(sem(f"x_in{s}"), 16)
                    elif l == 1:
                        act.wait_ge(sem("x1_ready"), 2 * s + 2)
                    elif l == 2:
                        act.wait_ge(sem("x2_ready"), TH * s + TH)
                    else:
                        act.wait_ge(sem("acc_ready"), 8 * (E2 - 1) + TH * s + TH)
                    act.activation(cond[:, TH * s:TH * s + TH, :], x[:, TH * s:TH * s + TH, :],
                                   ACT.Sigmoid).then_inc(sem("sig_ready"), 1)

            def cond_high(n0, halves=(0, 1)):
                for s in halves:
                    for k in range(KC):
                        n = n0 + 2 * s + k
                        act.wait_ge(sem("cT_ready"), n + 1)
                        act.activation(cThi[:, k, HALF * s:HALF * s + HALF], cond_bank(n)[:], ACT.Copy
                                       ).then_inc(sem("cT_high"), 1)

            def scores_copy(n, src, s, done):
                act.wait_ge(sem("sT_ready"), done + s)
                act.activation(sT(n)[:, HALF * s:HALF * s + HALF], src[0:n, :], ACT.Copy).then_inc(sem("sT_copied"), 1)

            def xl_high(s):
                act.wait_ge(sem("xl_ready"), s + 1)
                act.activation(xlhi[:, HALF * s:HALF * s + HALF], bank[5 + 2 * s][:], ACT.Copy).then_inc(sem("xl_high"), 1)

            def shared_relu(u):
                act.wait_ge(sem("sz_ready"), u + 1)
                wait(act, sem("sh_ready"), u - 1)
                act.activation(rl[:, u % 2, :], bank[u % 4][:], ACT.Relu).then_inc(sem("sr_ready"), 1)

            side_exp(0)
            side_exp(1)
            wkv_exp(0, 0)
            wkv_exp(1, 1)
            sigmoid_x(0)
            side_exp(2)
            wkv_exp(2, 0)
            wkv_exp(3, 1)
            side_exp(3)
            wkv_exp(4, 0)
            act.wait_ge(sem("sm_in"), 16)
            act.activation(sm_hi[:], sm_raw[:], ACT.Copy).then_inc(sem("sm_high"), 1)
            wkv_exp(5, 1)
            cond_high(0, (0,))
            wkv_exp(6, 0)
            scores_copy(E0, bank[6], 0, 1)
            xl_high(0)
            wkv_exp(7, 1)
            for u in range(4):
                shared_relu(u)
            cond_high(0, (1,))
            scores_copy(E0, bank[4], 1, 1)
            xl_high(1)
            act.wait_ge(sem("gate_ready"), 1)
            act.activation(rt[:, 0, :], bank[4][:, 0:NT * E0], ACT.Sigmoid).then_inc(sem("score_ready"), 1)
            for u in range(4, 8):
                shared_relu(u)

            def relu_scaled(q, i, o, j):
                eg = 2 * i + o // 2
                t = TH * (o % 2) + j
                wait(act, sem("h0_ready"), 4 * q + j - 1)
                wait(act, sem("z_ready"), 4 * q + j + 1)
                act.wait_ge(sem("cw0_ready"), 1)
                for e in range(4):
                    ins = act.activation(rl[:, j % 2, e * P:e * P + P], bank[j][:, e * P:e * P + P], ACT.Relu,
                                         scale=cw0[:, t, bass.ds(4 * eg + e, 1)])
                ins.then_inc(sem("r_ready"), 1)

            def hT_copy(q, e):
                wait(act, sem("y_done"), 4 * q + e - 1)
                wait(act, sem("t_ready"), 4 * q + e + 1)
                act.activation(hT[:, e % 2, :], bank[6 + e % 2][:], ACT.Copy).then_inc(sem("hT_ready"), 1)

            def latent_copy(s):
                act.wait_ge(sem("y_done"), 8 * EG - 4 + 4 * s)
                act.activation(ylat[:, s, :], bank[4 + s][:], ACT.Copy).then_inc(sem("ylat_ready"), 1)

            for j in range(4):
                relu_scaled(0, 0, 0, j)
            relu_scaled(1, 0, 1, 0)
            relu_scaled(1, 0, 1, 1)

            def expert_steps(i, last):
                for o in range(4):
                    q = 4 * i + o
                    more, more2 = not (last and o == 3), not (last and o >= 2)
                    hT_copy(q, 0)
                    if more:
                        relu_scaled(q + 1, i, o + 1, 2)
                    hT_copy(q, 1)
                    if more:
                        relu_scaled(q + 1, i, o + 1, 3)
                    else:
                        latent_copy(0)
                    wkv_exp(NBLK + q, o % 2)
                    hT_copy(q, 2)
                    if more2:
                        relu_scaled(q + 2, i, o + 2, 0)
                    hT_copy(q, 3)
                    if more2:
                        relu_scaled(q + 2, i, o + 2, 1)

            expert_steps(0, False)
            with act.Fori(1, EG // 2 - 1) as i:
                expert_steps(i, False)
            expert_steps(EG // 2 - 1, True)
            latent_copy(1)

            sigmoid_x(1)

            def l1_first(t):
                p = t % 2
                act.wait_ge(sem("q1t_ready"), t + 1)
                wait(act, sem("m1_ready"), t - 1)
                act.activation(qT[:, p, :, :], bank[4][:, 0:C], ACT.Copy, bias=-ROUND).then_inc(sem("q1T_ready"), 1)

            def l1_gelu(t):
                p = t % 2
                wait(act, sem("q2t_ready"), 2 * t - 2)
                act.wait_ge(sem("pre_ready"), t + 1)
                act.activation(gl[:, p, :], xp[:, p, :], ACT.Gelu_apprx_tanh).then_inc(sem("gelu_ready"), 1)

            def l1_second(t, tag=""):
                p = t % 2
                wait(act, sem("m2_ready" + tag), t - 1)
                for h in range(2):
                    act.wait_ge(sem("q2t_ready" + tag), 2 * t + h + 1)
                    act.activation(q2T[:, p, 4 * h:4 * h + 4, :], bank[5 + h][:], ACT.Copy, bias=-ROUND
                                   ).then_inc(sem("q2T_ready" + tag), 1)

            for t in range(-2, NT):
                if t + 2 < NT:
                    l1_first(t + 2)
                if 0 <= t + 1 < NT:
                    l1_gelu(t + 1)
                if t == NT - 2:
                    sigmoid_x(2, (0,))
                if t >= 0:
                    l1_second(t)

            cond_high(4, (0,))
            sigmoid_x(2, (1,))
            scores_copy(E2, bank[5], 0, 3)
            cond_high(4, (1,))
            scores_copy(E2, bank[6], 1, 3)
            act.wait_ge(sem("lsub_ready"), 1)
            act.activation(r2[:, 1, :, :], r2[:, 1, :, :], ACT.Exp).then_inc(sem("lexp_ready"), 1)

            def silu_gate(u, p):
                wait(act, sem("hh_ready"), u - 1)
                wait(act, sem("gu_done"), u + 1)
                act.activation(sl[:, p, :], bank[2 * p][:], ACT.Silu).then_inc(sem("sl_ready"), 1)

            def glu_step(e, p):
                for j in range(8):
                    silu_gate(8 * e + j, j % 2)
                wkv_exp(3 * NBLK + e, p)

            glu_step(0, 0)
            glu_step(1, 1)
            with act.Fori(1, E2 // 2) as i:
                glu_step(2 * i, 0)
                glu_step(2 * i + 1, 1)

            sigmoid_x(3)
            for t in range(NT):
                act.wait_ge(sem("cond_ready"), 12 + t // 2 + 1)
                if t == TH:
                    ins.then_inc(sem("c3_sq"), 1)
                ins = act.activation(xp[:, t // TH, C * (t % TH):C * (t % TH) + C], cond[:, t, :], ACT.Square, scale=C ** -0.5, accum_out=st[:, 4, t:t + 1])
            ins.then_inc(sem("c3_sq"), 1)

            def l3_first(t):
                p = t % 2
                act.wait_ge(sem("q1t3_ready"), t + 1)
                wait(act, sem("m13_ready"), 2 * t - 2)
                act.activation(qT[:, p, :, :], bank[4][:, 0:C], ACT.Copy, bias=-ROUND).then_inc(sem("q1T3_ready"), 1)

            def l3_silu(t):
                p = t % 2
                act.wait_ge(sem("c3_scale"), t // TH + 1)
                for h in range(2):
                    act.wait_ge(sem("m13_ready"), 2 * t + h + 1)
                    wait(act, sem("h3_ready"), 2 * t + h - 3)
                    act.activation(xp[:, p, 512 * h:512 * h + 512], bank[h][:], ACT.Silu, scale=st[:, 9, t:t + 1]
                                   ).then_inc(sem("silu3_ready"), 1)

            def l3_square(t):
                p = t % 2
                act.wait_ge(sem("h3_ready"), 2 * t + 2)
                wait(act, sem("h3_sq"), t)
                wait(act, sem("q23_ready"), t - 1)
                act.activation(junk[:], gl[:, p, :], ACT.Square, scale=HID ** -0.5, accum_out=pt[:, 4, p:p + 1]
                               ).then_inc(sem("h3_sq"), 1)

            for t in range(-2, NT):
                if 0 <= t + 1 < NT:
                    l3_square(t + 1)
                if t + 2 < NT:
                    l3_first(t + 2)
                    l3_silu(t + 2)
                if t >= 0:
                    l1_second(t, "3")

        @block.vector
        def _(dve):
            count = [0]

            def chain(ins):
                count[0] += 1
                ins.then_inc(sem("dve_step"), 1)
                dve.wait_ge(sem("dve_step"), count[0])

            dve.wait_ge(sem("small_in"), 48)
            dve.tensor_reduce(tfb[:, 0, :], te[:], AX.X, ALU.add).then_inc(sem("te_sum"), 1)

            def side_exp(b):
                dve.wait_ge(sem(f"kT_in{b}"), 16)
                dve.tensor_scalar(ekk[:, 2 * b:2 * b + 2, 1, :], kT[:, 2 * b:2 * b + 2, :], 30.0, None, ALU.min
                                  ).then_inc(sem("kmin_ready"), 1)

            side_exp(0)
            side_exp(1)
            dve.wait_ge(sem("te_exp"), 1)
            chain(dve.tensor_scalar(tfb[:, 1, :], tfb[:, 1, :], 1.0, None, ALU.add))
            chain(dve.reciprocal(tfb[:, 0, :], tfb[:, 1, :]))
            dve.tensor_scalar(tfb[:, 2, :], tfb[:, 0, :], 0.5, 0.5, ALU.mult, ALU.add)
            chain(dve.tensor_scalar(tfb[:, 3, :], tfb[:, 0, :], 0.2, 0.8, ALU.mult, ALU.add))
            dve.wait_ge(sem("wl_ready"), 1)
            for b in range(B):
                dve.tensor_scalar(dec[:, :, b, :], wl[:], tfb[:, 2, b:b + 1], None, ALU.mult)
                dve.tensor_copy(ubk[:, :, b, :], ul[:])
                ins = dve.tensor_scalar(gain[:, b, :], wl[:, 0, :], 0.0, tfb[:, 3, b:b + 1], ALU.mult, ALU.add)
            chain(ins)
            decf = dec[:].rearrange("p l b k -> p (l b k)")
            ubf = ubk[:].rearrange("p l b k -> p (l b k)")
            gf = gain[:].rearrange("p b k -> p (b k)")

            def col(ap, i):
                return ap[:, i:i + 1] if isinstance(i, int) else ap[:, bass.ds(i, 1)]

            def early(n):
                return isinstance(n, int) and n < NBLK

            def wkv_kup(n, l, blk, p):
                wait(dve, sem("sums_ready"), n - 1)
                dve.tensor_scalar(eu[:, p, 1, :], kT[:, blk, :], col(ubf, NBLK * l + blk), 30.0, ALU.add, ALU.min
                                  ).then_inc(sem("kup_ready"), 1)
                if not early(n):
                    dve.tensor_copy(ekb[:, p, :, :], ekk[:, blk, :, :]).then_inc(sem("ekb_ready"), 1)

            def wkv_scan(n, l, blk, p, part):
                d = part % 2
                if part == 0:
                    wait(dve, sem("G_ready"), n - 1)
                if part < 2:
                    dve.tensor_tensor_scan(fw[:, p, d, :], col(decf, NBLK * l + blk).to_broadcast([P, S]),
                                           ekk[:, blk, d, :], 0.0, ALU.mult, ALU.add)
                else:
                    if not early(n):
                        wait(dve, sem("ekb_ready"), n - NBLK + 1)
                    back = ekk[:, blk, d, S - 1:0:-1] if early(n) else ekb[:, p, d, S - 1:0:-1]
                    ins = dve.tensor_tensor_scan(bw[:, p, d, S - 2::-1], back,
                                                 col(decf, NBLK * l + blk).to_broadcast([P, S - 1]), 0.0, ALU.add, ALU.mult)
                    if part == 3:
                        ins.then_inc(sem("scan_ready"), 1)

            def wkv_gain(n, l, blk, p):
                wait(dve, sem("sums_ready"), n + 1)
                dve.tensor_scalar(fw[:, p, 1, :], fw[:, p, 1, :], 1e-8, None, ALU.max).then_inc(sem("den_ready"), 1)
                wait(dve, sem("den_ready"), n + 1)
                dve.reciprocal(fw[:, p, 1, :], fw[:, p, 1, :]).then_inc(sem("rden_ready"), 1)
                wait(dve, sem("rden_ready"), n + 1)
                dve.scalar_tensor_tensor(out=GT[:, l % 2, blk, :], in0=fw[:, p, 0, :], scalar=col(gf, blk),
                                         in1=fw[:, p, 1, :], op0=ALU.mult, op1=ALU.mult).then_inc(sem("G_ready"), 1)

            def make_cond(l, b):
                m = 4 * l + b
                dve.wait_ge(sem("G_turned"), m + 1)
                dve.wait_ge(sem("sig_ready"), 2 * l + b // 2 + 1)
                dve.tensor_tensor(cond[:, 2 * b:2 * b + 2, :], gain_bank(l, b)[:].rearrange("p (t c) -> p t c", t=2),
                                  cond[:, 2 * b:2 * b + 2, :], ALU.mult).then_inc(sem("cond_ready"), 1)

            def cond_low(n0, s, k):
                n = n0 + 2 * s + k
                dve.wait_ge(sem("cT_high"), n + 1)
                dve.tensor_tensor(cTlo[:, k, HALF * s:HALF * s + HALF], cond_bank(n)[:],
                                  cThi[:, k, HALF * s:HALF * s + HALF].bitcast(F32), ALU.subtract
                                  ).then_inc(sem("cT_low"), 1)

            def xl_low(s):
                dve.wait_ge(sem("xl_high"), s + 1)
                dve.tensor_tensor(xllo[:, HALF * s:HALF * s + HALF], bank[5 + 2 * s][:],
                                  xlhi[:, HALF * s:HALF * s + HALF].bitcast(F32), ALU.subtract).then_inc(sem("xl_low"), 1)

            def shared_h(u):
                dve.wait_ge(sem("sr_ready"), u + 1)
                dve.scalar_tensor_tensor(out=hx[:, u // 4, u % 4, :], in0=bank[u % 4][:], scalar=0.0, in1=rl[:, u % 2, :],
                                         op0=ALU.max, op1=ALU.mult).then_inc(sem("sh_ready"), 1)

            def add_shared(v):
                dve.wait_ge(sem("sd_ready"), v + 1)
                dve.tensor_tensor(x[:, 2 * v:2 * v + 2, :], down_bank(v)[:].rearrange("p (t c) -> p t c", t=2),
                                  x[:, 2 * v:2 * v + 2, :], ALU.add).then_inc(sem("sx_done"), 1)

            def small_low():
                dve.wait_ge(sem("sm_high"), 1)
                dve.tensor_tensor(sm_lo[:], sm_raw[:], sm_hi[:].bitcast(F32), ALU.subtract).then_inc(sem("sm_low"), 1)

            between = {(5, 2): [small_low], (5, 3): [lambda: make_cond(0, 0), lambda: make_cond(0, 1)],
                       (6, 1): [lambda: cond_low(0, 0, 0)], (6, 2): [lambda: cond_low(0, 0, 1)],
                       (7, 0): [lambda: xl_low(0)]}
            dve.wait_ge(sem("bw_zero"), 1)
            for b in range(B):
                dve.wait_ge(sem("ek_ready"), b + 1)
                chain(dve.tensor_tensor(ekk[:, 2 * b:2 * b + 2, 0, :], ekk[:, 2 * b:2 * b + 2, 1, :],
                                        kT[:, 2 * b:2 * b + 2, :], ALU.mult))
                if 0 < b < B - 1:
                    side_exp(b + 1)
                for n in (2 * b, 2 * b + 1):
                    wkv_kup(n, 0, n, n % 2)
                    for part in range(4):
                        wkv_scan(n, 0, n, n % 2, part)
                        for step in between.get((n, part), ()):
                            step()
                    if n:
                        wkv_gain(n - 1, 0, n - 1, (n - 1) % 2)
            make_cond(0, 2)
            shared_h(0)
            wkv_gain(NBLK - 1, 0, NBLK - 1, 1)
            shared_h(1)
            shared_h(2)
            make_cond(0, 3)
            shared_h(3)
            cond_low(0, 1, 0)
            cond_low(0, 1, 1)
            xl_low(1)

            def ranks(score, low, n, a, b, rank):
                four = dict(o=1)
                other = score.rearrange("p t (o g) -> p t o g", **four).to_broadcast([P, NT, n, n])
                own = score.rearrange("p t (g o) -> p t g o", **four).to_broadcast([P, NT, n, n])
                lowb = low[:].rearrange("p (o g) h -> p o g h", **four).to_broadcast([P, NT, n, n])
                dve.tensor_tensor(a, other, own, ALU.is_gt)
                chain(dve.tensor_tensor(b, other, own, ALU.is_equal))
                chain(dve.tensor_tensor(b, b, lowb, ALU.mult))
                chain(dve.tensor_tensor(a, a, b, ALU.add))
                chain(dve.tensor_reduce(rank, a, AX.X, ALU.add))

            def r(i, n=NT * E0):
                return rt[:, i, 0:n]

            def g8(i, w=8):
                return rt[:, i, 0:NT * G0 * w].rearrange("p (t w) -> p t w", w=w)

            dve.wait_ge(sem("score_ready"), 1)
            dve.wait_ge(sem("gbias_in"), 16)
            dve.wait_ge(sem("low_ready"), 2)
            chain(dve.tensor_tensor(r(1).rearrange("p (t e) -> p t e", e=E0), r(0).rearrange("p (t e) -> p t e", e=E0),
                                    gbias[:].rearrange("p (o e) -> p o e", o=1).to_broadcast([P, NT, E0]), ALU.add))
            sc = g8(1)
            hi4, lo4 = g8(2, 4), g8(3, 4)
            dve.tensor_tensor(hi4, sc[:, :, 0:4], sc[:, :, 4:8], ALU.max)
            chain(dve.tensor_tensor(lo4, sc[:, :, 0:4], sc[:, :, 4:8], ALU.min))
            hi, lo = hi4, lo4
            for lev, w in ((0, 2), (1, 1)):
                nh, nl, ml, ll = (g8(4 + 4 * lev + i, w) for i in range(4))
                dve.tensor_tensor(nh, hi[:, :, 0:w], hi[:, :, w:2 * w], ALU.max)
                dve.tensor_tensor(ml, hi[:, :, 0:w], hi[:, :, w:2 * w], ALU.min)
                chain(dve.tensor_tensor(ll, lo[:, :, 0:w], lo[:, :, w:2 * w], ALU.max))
                chain(dve.tensor_tensor(nl, ml, ll, ALU.max))
                hi, lo = nh, nl
            gs = rt[:, 2, 0:NT * G0].rearrange("p (t g) -> p t g", g=G0)
            chain(dve.tensor_tensor(rt[:, 2, 0:NT * G0], rt[:, 8, 0:NT * G0], rt[:, 9, 0:NT * G0], ALU.add))
            sq = [rt[:, i, 0:NT * G0 * G0].rearrange("p (t g h) -> p t g h", g=G0, h=G0) for i in (3, 4)]
            ranks(gs, low4, G0, sq[0], sq[1], rt[:, 5, 0:NT * G0].rearrange("p (t g) -> p t g", g=G0))
            shared_h(4)
            shared_h(5)
            chain(dve.tensor_scalar(rt[:, 6, 0:NT * G0], rt[:, 5, 0:NT * G0], 2.0, None, ALU.is_lt))
            dve.tensor_scalar(rt[:, 7, 0:NT * G0], rt[:, 6, 0:NT * G0], -1.0, 3.0e38, ALU.add, ALU.mult)

            def over8(i):
                return rt[:, i, 0:NT * G0].rearrange("p (t o) -> p t o", o=1).to_broadcast([P, NT * G0, 8])

            chain(dve.tensor_tensor(g8(8), sc, over8(6), ALU.mult))
            chain(dve.tensor_tensor(g8(8), g8(8), over8(7), ALU.add))
            for t in range(NT):
                ins = dve.max(top8[:, t, :], rt[:, 8, t * E0:t * E0 + E0])
            chain(ins)
            for t in range(NT):
                ins = dve.match_replace(rt[:, 9, t * E0:t * E0 + E0], top8[:, t, :], rt[:, 8, t * E0:t * E0 + E0], -3.3e38)
            chain(ins)
            shared_h(6)
            shared_h(7)
            chain(dve.tensor_tensor(r(10), r(9), r(8), ALU.not_equal))
            chain(dve.tensor_tensor(r(10), r(10), r(0), ALU.mult))
            chain(dve.tensor_reduce(rt[:, 11, 0:NT], r(10).rearrange("p (t e) -> p t e", e=E0), AX.X, ALU.add))
            chain(dve.reciprocal(rt[:, 11, NT:2 * NT], rt[:, 11, 0:NT]))
            chain(dve.tensor_scalar(rt[:, 11, 2 * NT:3 * NT], rt[:, 11, NT:2 * NT], ROUTED_SCALE, None, ALU.mult))
            dve.tensor_tensor(cw0[:], r(10).rearrange("p (t e) -> p t e", e=E0),
                              rt[:, 11, 2 * NT:3 * NT].rearrange("p (t o) -> p t o", o=1).to_broadcast([P, NT, E0]),
                              ALU.mult).then_inc(sem("cw0_ready"), 1)

            for v in range(4):
                add_shared(v)

            def weight_max(m):
                if m == 0:
                    dve.wait_ge(sem("q_in"), 32)
                dve.tensor_reduce(ws[:, m:m + 1], (q1raw, q2raw)[m][:].rearrange("p k n -> p (k n)"), AX.X, ALU.max,
                                  apply_absolute_value=True).then_inc(sem("wmax_part"), 1)

            def weight_scale():
                dve.wait_ge(sem("wmax_ready"), 1)
                chain(dve.reciprocal(ws[:, 4:6], ws[:, 2:4]))
                dve.tensor_scalar(ws[:, 6:8], ws[:, 4:6], Q, None, ALU.mult).then_inc(sem("wscale_ready"), 1)
                dve.wait_ge(sem("wscale_ready"), 1)
                chain(dve.tensor_scalar(ws[:, 4:6], ws[:, 2:4], 1.0 / (Q * Q), None, ALU.mult))

            def add_routed(v):
                dve.wait_ge(sem("fo_ready"), v + 1)
                dve.tensor_tensor(x[:, 2 * v:2 * v + 2, :], bank[v if v < 2 else 4 + v][:].rearrange("p (t c) -> p t c", t=2),
                                  x[:, 2 * v:2 * v + 2, :], ALU.add).then_inc(sem("x1_ready"), 1)

            def expert_h(q, o, j):
                wait(dve, sem("r_ready"), 4 * q + j + 1)
                dve.scalar_tensor_tensor(out=hx[:, o % 2, j, :], in0=bank[j][:], scalar=0.0, in1=rl[:, j % 2, :],
                                         op0=ALU.max, op1=ALU.mult).then_inc(sem("h0_ready"), 1)

            for j in range(4):
                expert_h(0, 0, j)
            expert_h(1, 1, 0)
            expert_h(1, 1, 1)
            dve.wait_ge(sem("G_turned"), 4)

            def expert_steps(i, last):
                for o in range(4):
                    q = 4 * i + o
                    n, l, blk, p = NBLK + q, 1 + o % 2, 2 * i + o // 2, o % 2
                    wkv_kup(n, l, blk, p)
                    for j in range(4):
                        if j < 2 and not (last and o == 3):
                            expert_h(q + 1, o + 1, j + 2)
                        if j >= 2 and not (last and o >= 2):
                            expert_h(q + 2, o + 2, j - 2)
                        wkv_scan(n, l, blk, p, j)
                        if last and o == 3 and j == 2:
                            add_routed(0)
                            add_routed(1)
                        if j == 2 and not (o == 0 and isinstance(i, int) and i == 0):
                            wkv_gain(n - 1, 1 + (o - 1) % 2, 2 * i + (o - 1) // 2, 1 - p)
                    if isinstance(i, int) and i == 0:
                        (lambda: weight_max(0), lambda: weight_max(1), weight_scale, lambda: None)[o]()

            expert_steps(0, False)
            with dve.Fori(1, EG // 2 - 1) as i:
                expert_steps(i, False)
            expert_steps(EG // 2 - 1, True)

            wkv_gain(3 * NBLK - 1, 2, NBLK - 1, 1)

            def row_scales(s):
                t = slice(TH * s, TH * s + TH)
                dve.wait_ge(sem("cond_ready"), 6 + 2 * s)
                chain(dve.tensor_reduce(st[:, 0, t], cond[:, t, :], AX.X, ALU.max, apply_absolute_value=True))
                chain(dve.reciprocal(st[:, 1, t], st[:, 0, t]))
                dve.tensor_scalar(st[:, 2, t], st[:, 1, t], Q, None, ALU.mult).then_inc(sem("row_scale"), 1)
                chain(dve.tensor_scalar(st[:, 3, t], st[:, 0, t], ws[:, 4:5], None, ALU.mult))

            def l1_pre(t):
                p = t % 2
                dve.wait_ge(sem("m1_ready"), t + 1)
                wait(dve, sem("gelu_ready"), t - 1)
                for h in range(2):
                    ins = dve.scalar_tensor_tensor(out=xp[:, p, 512 * h:512 * h + 512], in0=bank[2 * p + h][:],
                                                   scalar=st[:, 3, t:t + 1], in1=b1bc[:, 512 * h:512 * h + 512],
                                                   op0=ALU.mult, op1=ALU.add)
                ins.then_inc(sem("pre_ready"), 1)

            def l1_quant(t):
                p = t % 2
                dve.wait_ge(sem("gelu_ready"), t + 1)
                chain(dve.tensor_reduce(pt[:, 0, p:p + 1], gl[:, p, :], AX.X, ALU.max, apply_absolute_value=True))
                chain(dve.reciprocal(pt[:, 1, p:p + 1], pt[:, 0, p:p + 1]))
                dve.tensor_scalar(pt[:, 3, p:p + 1], pt[:, 0, p:p + 1], ws[:, 5:6], None, ALU.mult)
                chain(dve.tensor_scalar(pt[:, 2, p:p + 1], pt[:, 1, p:p + 1], Q, None, ALU.mult))
                dve.tensor_scalar(gl[:, p, :], gl[:, p, :], pt[:, 2, p:p + 1], ROUND, ALU.mult, ALU.add
                                  ).then_inc(sem("q2_ready"), 1)

            def l1_out(t):
                dve.wait_ge(sem("m2_ready"), t + 1)
                dve.wait_ge(sem("xb_ready"), t + 1)
                dve.scalar_tensor_tensor(out=x[:, t, :], in0=bank[7][:, 0:C], scalar=pt[:, 3, t % 2:t % 2 + 1],
                                         in1=x[:, t, :], op0=ALU.mult, op1=ALU.add).then_inc(sem("x2_ready"), 1)

            dve.wait_ge(sem("qb_in"), 32)
            make_cond(1, 0)
            make_cond(1, 1)
            row_scales(0)
            for t in range(-3, NT + 1):
                if t == -2:
                    add_routed(2)
                    add_routed(3)
                    make_cond(1, 2)
                    make_cond(1, 3)
                    row_scales(1)
                if 0 <= t + 1 < NT:
                    l1_pre(t + 1)
                if 0 <= t < NT:
                    l1_quant(t)
                if t == NT - 1:
                    make_cond(2, 0)
                    make_cond(2, 1)
                if t >= 1:
                    l1_out(t - 1)

            dve.wait_ge(sem("rt_in"), 16)
            chain(dve.tensor_copy(rthi[:], rtraw[:]))
            dve.tensor_tensor(rtlo[:], rtraw[:], rthi[:].bitcast(F32), ALU.subtract).then_inc(sem("rt_split"), 1)
            cond_low(4, 0, 0)
            cond_low(4, 0, 1)
            make_cond(2, 2)
            make_cond(2, 3)
            cond_low(4, 1, 0)
            cond_low(4, 1, 1)
            lg = bank[4][:, 0:NT * E2].rearrange("p (t e) -> p t e", e=E2)

            def per_token(i):
                return r2[:, i, :, 0:1].to_broadcast([P, NT, E2])

            dve.wait_ge(sem("logit_ready"), 1)
            chain(dve.tensor_reduce(r2[:, 0, :, 0:1], lg, AX.X, ALU.max))
            dve.tensor_tensor(r2[:, 1, :, :], lg, per_token(0), ALU.subtract).then_inc(sem("lsub_ready"), 1)
            def route2():
                dve.wait_ge(sem("lexp_ready"), 1)
                chain(dve.tensor_reduce(r2[:, 2, :, 0:1], r2[:, 1, :, :], AX.X, ALU.add))
                chain(dve.reciprocal(r2[:, 3, :, 0:1], r2[:, 2, :, 0:1]))
                chain(dve.tensor_tensor(r2[:, 4, :, :], r2[:, 1, :, :], per_token(3), ALU.mult))
                sq = [r2c[:, i, :, :].rearrange("p t (g h) -> p t g h", g=E2) for i in range(2)]
                ranks(r2[:, 4, :, :], low8, E2, sq[0], sq[1], r2[:, 5, :, :])
                chain(dve.tensor_scalar(r2[:, 5, :, :], r2[:, 5, :, :], 2.0, None, ALU.is_lt))
                chain(dve.tensor_tensor(r2[:, 6, :, :], r2[:, 5, :, :], r2[:, 4, :, :], ALU.mult))
                chain(dve.tensor_reduce(r2[:, 7, :, 0:1], r2[:, 6, :, :], AX.X, ALU.add))
                chain(dve.reciprocal(r2[:, 8, :, 0:1], r2[:, 7, :, 0:1]))
                chain(dve.tensor_tensor(cw2[:], r2[:, 6, :, :], per_token(8), ALU.mult))

            def ternary_scale(m):
                dve.wait_ge(sem("t_in"), 16 * m + 16)
                dve.tensor_reduce(ws[:, 9 + m:10 + m], traw[:], AX.X, ALU.add, apply_absolute_value=True).then_inc(sem("tsum_part"), 1)
                dve.wait_ge(sem("tsum_ready"), m + 1)
                chain(dve.tensor_scalar(ws[:, 15 + m:16 + m], ws[:, 12 + m:13 + m], 1.0 / (C * HID), 1e-5, ALU.mult, ALU.max))
                dve.reciprocal(ws[:, 18 + m:19 + m], ws[:, 15 + m:16 + m]).then_inc(sem("tscale_ready"), 1)

            def glu_h(e, s, j):
                u, p = 8 * e + 4 * s + j, j % 2
                wait(dve, sem("sl_ready"), u + 1)
                dve.tensor_tensor(hh[:, p, :], bank[2 * p + 1][:], sl[:, p, :], ALU.mult).then_inc(sem("hh_ready"), 1)
                wait(dve, sem("d_done"), 8 * e - 4 + 4 * s)
                wait(dve, sem("hh_ready"), u + 1)
                dve.tensor_copy(hhi[:, s, j, :], hh[:, p, :]).then_inc(sem("hhi_ready"), 1)
                wait(dve, sem("hhi_ready"), u + 1)
                dve.tensor_tensor(hlo[:, s, j, :], hh[:, p, :], hhi[:, s, j, :].bitcast(F32), ALU.subtract
                                  ).then_inc(sem("hlo_ready"), 1)

            cw2f = cw2[:].rearrange("p t e -> p (t e)")

            def glu_step(e, p, first=False):
                n = 3 * NBLK + e
                for s in range(2):
                    for j in range(4):
                        glu_h(e, s, j)
                        if s == 0 and j == 0:
                            wkv_kup(n, 3, e, p)
                        if j % 2:
                            wkv_scan(n, 3, e, p, 2 * s + j // 2)
                if first:
                    route2()
                for t in range(NT):
                    if t == TH and not first:
                        wkv_gain(n - 1, 3, e - 1, 1 - p)
                    v = 8 * e + t
                    wait(dve, sem("d_done"), v + 1)
                    dve.scalar_tensor_tensor(out=x[:, t, :], in0=bank[4 + t % 4][:, 0:C], scalar=col(cw2f, E2 * t + e),
                                             in1=x[:, t, :], op0=ALU.mult, op1=ALU.add).then_inc(sem("acc_ready"), 1)

            for e in range(4):
                glu_step(e, e % 2, e == 0)
                if e < 3:
                    ternary_scale(e)
            with dve.Fori(2, E2 // 2) as i:
                glu_step(2 * i, 0)
                glu_step(2 * i + 1, 1)

            wkv_gain(4 * NBLK - 1, 3, NBLK - 1, 1)

            for b in range(B):
                make_cond(3, b)
                if b % 2:
                    t = slice(TH * (b // 2), TH * (b // 2) + TH)
                    dve.wait_ge(sem("cond_ready"), 12 + b + 1)
                    dve.tensor_reduce(st[:, 6, t], cond[:, t, :], AX.X, ALU.max, apply_absolute_value=True
                                      ).then_inc(sem("c3_max"), 1)
            dve.tensor_scalar(ws[:, 21:24], ws[:, 15:18], 1.0 / Q, None, ALU.mult)
            for s in range(2):
                t = slice(TH * s, TH * s + TH)
                dve.wait_ge(sem("c3_stat"), s + 1)
                chain(dve.tensor_scalar(st[:, 7, t], st[:, 7, t], 1e-5, None, ALU.max))
                dve.tensor_scalar(st[:, 9, t], st[:, 7, t], ws[:, 21:22], None, ALU.mult)
                dve.tensor_scalar(st[:, 10, t], st[:, 7, t], ws[:, 22:23], None, ALU.mult)
                chain(dve.reciprocal(st[:, 8, t], st[:, 7, t]))
                dve.scalar_tensor_tensor(out=st[:, 8, t], in0=st[:, 8, t], scalar=Q, in1=st[:, 5, t],
                                         op0=ALU.mult, op1=ALU.mult).then_inc(sem("c3_scale"), 1)
            dve.wait_ge(sem("c3_scale"), 2)

            def l3_h(t):
                p = t % 2
                wait(dve, sem("q2t_ready3"), 2 * t - 2)
                for h in range(2):
                    dve.wait_ge(sem("silu3_ready"), 2 * t + h + 1)
                    dve.scalar_tensor_tensor(out=gl[:, p, 512 * h:512 * h + 512], in0=bank[2 + h][:],
                                                   scalar=st[:, 10, t:t + 1], in1=xp[:, p, 512 * h:512 * h + 512],
                                                   op0=ALU.mult, op1=ALU.mult).then_inc(sem("h3_ready"), 1)

            def l3_max(t):
                p = t % 2
                dve.wait_ge(sem("h3_ready"), 2 * t + 2)
                dve.tensor_reduce(pt[:, 6, p:p + 1], gl[:, p, :], AX.X, ALU.max, apply_absolute_value=True
                                  ).then_inc(sem("h3_max"), 1)

            def l3_quant(t):
                p = t % 2
                dve.wait_ge(sem("h3_stat"), t + 1)
                chain(dve.tensor_scalar(pt[:, 0, p:p + 1], pt[:, 7, p:p + 1], 1e-5, None, ALU.max))
                chain(dve.reciprocal(pt[:, 1, p:p + 1], pt[:, 0, p:p + 1]))
                dve.tensor_scalar(pt[:, 3, p:p + 1], pt[:, 0, p:p + 1], ws[:, 23:24], None, ALU.mult)
                chain(dve.tensor_scalar(pt[:, 2, p:p + 1], pt[:, 1, p:p + 1], pt[:, 5, p:p + 1], Q, ALU.mult, ALU.mult))
                dve.tensor_scalar(gl[:, p, :], gl[:, p, :], pt[:, 2, p:p + 1], ROUND, ALU.mult, ALU.add
                                  ).then_inc(sem("q23_ready"), 1)

            def l3_out(t):
                dve.wait_ge(sem("m2_ready3"), t + 1)
                dve.scalar_tensor_tensor(out=x[:, t, :], in0=bank[7][:, 0:C], scalar=pt[:, 3, t % 2:t % 2 + 1],
                                         in1=x[:, t, :], op0=ALU.mult, op1=ALU.add).then_inc(sem("x4_ready"), 1)

            for t in range(-3, NT + 1):
                if 0 <= t + 1 < NT:
                    l3_h(t + 1)
                    l3_max(t + 1)
                if 0 <= t < NT:
                    l3_quant(t)
                if t >= 1:
                    l3_out(t - 1)

        @block.tensor
        def _(pe):
            def mm3(out, lhs, rhs, start, stop):
                pe.matmul(out, lhs[0], rhs[0], start=start, stop=False)
                pe.matmul(out, lhs[0], rhs[1], start=False, stop=False)
                return pe.matmul(out, lhs[1], rhs[0], start=False, stop=stop)

            def turn_gain(l, b):
                units = {0: 2 * b + 2, 1: (2 if b < 2 else 3) * NBLK}
                pe.wait_ge(sem("G_ready"), units.get(l, DONE[l]))
                if b >= 2:
                    pe.wait_ge(sem("cond_ready"), 4 * l + b - 1)
                for u in range(2):
                    for k in range(KC):
                        ins = pe.transpose(gain_bank(l, b)[:, u * C + k * P:u * C + k * P + P],
                                           GT[:, l % 2, 2 * b + k, u * P:u * P + P], ident[:])
                ins.then_inc(sem("G_turned"), 1)

            def turn_cond(l, n0, s):
                pe.wait_ge(sem("cond_ready"), 4 * l + 2 * s + 2)
                for k in range(KC):
                    n = n0 + 2 * s + k
                    wait(pe, sem("cT_low"), n - 1)
                    for j in range(TH):
                        ins = pe.transpose(cond_bank(n)[:, j * P:j * P + P], cond[:, TH * s + j, k * P:k * P + P], ident[:])
                    ins.then_inc(sem("cT_ready"), 1)

            def cT(k, a, b):
                return cThi[:, k, a:b], cTlo[:, k, a:b]

            pe.wait_ge(sem("ident_ready"), 1)
            ins_back = [None]

            def scores_up(out, n, high, low, s):
                for k in range(KC):
                    ins = mm3(out[0:n, :], (high[:, k, 0:n], low[:, k, 0:n]), cT(k, HALF * s, HALF * s + HALF),
                              k == 0, k == KC - 1)
                ins.then_inc(sem("sT_ready"), 1)

            def scores_back(out, n, done):
                pe.wait_ge(sem("sT_copied"), done)
                for t in range(NT):
                    ins_back[0] = pe.transpose(out[:, t * n:t * n + n], sT(n)[:, t * P:t * P + P], ident[0:n, 0:n])

            def shared_up(u):
                s, j = u // 4, u % 4
                wait(pe, sem("sh_ready"), u - 3)
                for k in range(KC):
                    w = slice(E0 + LAT + j * P, E0 + LAT + j * P + P)
                    ins = mm3(bank[u % 4][:], (sm_hi[:, k, w], sm_lo[:, k, w]), cT(k, HALF * s, HALF * s + HALF),
                              k == 0, k == KC - 1)
                ins.then_inc(sem("sz_ready"), 1)

            def latent(s):
                for k in range(KC):
                    w = slice(E0, E0 + LAT)
                    ins = mm3(bank[5 + 2 * s][:], (sm_hi[:, k, w], sm_lo[:, k, w]), cT(k, HALF * s, HALF * s + HALF),
                              k == 0, k == KC - 1)
                ins.then_inc(sem("xl_ready"), 1)

            def shared_down(v):
                if v == 0:
                    pe.wait_ge(sem("down_in"), 16)
                for half in range(2):
                    t = 2 * (v % 2) + half
                    for j in range(4):
                        ins = pe.matmul(down_bank(v)[:, half * C:half * C + C], hx[:, v // 2, j, t * P:t * P + P],
                                        downw[:, j, :], start=(j == 0), stop=(j == 3))
                ins.then_inc(sem("sd_ready"), 1)

            turn_gain(0, 0)
            turn_gain(0, 1)
            turn_cond(0, 0, 0)
            pe.wait_ge(sem("sm_low"), 1)
            pe.wait_ge(sem("cT_low"), 2)
            scores_up(bank[6], E0, sm_hi, sm_lo, 0)
            latent(0)
            for u in range(4):
                shared_up(u)
            turn_gain(0, 2)
            turn_gain(0, 3)
            pe.wait_ge(sem("sT_copied"), 1)
            pe.wait_ge(sem("xl_low"), 1)
            turn_cond(0, 0, 1)
            pe.wait_ge(sem("cT_low"), 4)
            scores_up(bank[4], E0, sm_hi, sm_lo, 1)
            latent(1)
            shared_up(4)
            scores_back(bank[4], E0, 2)
            ins_back[0].then_inc(sem("gate_ready"), 1)
            for u in range(5, 8):
                shared_up(u)
            shared_down(0)
            shared_down(1)
            pe.wait_ge(sem("sh_ready"), 8)
            pe.wait_ge(sem("score_ready"), 1)
            shared_down(2)
            pe.wait_ge(sem("xl_low"), 2)
            shared_down(3)

            def expert_z(q, i, o, j):
                slot, t = (o // 2) % 2, TH * (o % 2) + j
                wait(pe, sem("h0_ready"), 4 * q - 3 + j)
                if j == 0 and o % 2 == 0:
                    wait(pe, sem("w1_split"), 2 * i + o // 2 + 1)
                w = (w1hi[:, slot, :], w1lo[:, slot, :])
                mm3(bank[j][:], (xlhi[:, t * P:t * P + P], xllo[:, t * P:t * P + P]), w, True, True).then_inc(sem("z_ready"), 1)

            def expert_turn(q, o, e):
                if e == 0:
                    wait(pe, sem("h0_ready"), 4 * q + 4)
                wait(pe, sem("hT_ready"), 4 * q + e - 1)
                for j in range(4):
                    ins = pe.transpose(bank[6 + e % 2][:, j * P:j * P + P], hx[:, o % 2, j, e * P:e * P + P], ident[:])
                ins.then_inc(sem("t_ready"), 1)

            def expert_y(q, i, o, e):
                slot = o // 2
                if o % 2 == 0 and e == 0:
                    pe.wait_ge(sem(f"w2_in{slot}"), 16 * (i + 1))
                wait(pe, sem("hT_ready"), 4 * q + e + 1)
                start = isinstance(i, int) and i == 0 and o < 2 and e == 0
                stop = isinstance(i, int) and i == EG // 2 - 1 and o >= 2 and e == 3
                pe.matmul(bank[4 + o % 2][:], w2raw[:, slot, e, :], hT[:, e % 2, :], start=start, stop=stop,
                          skip_group_check=True).then_inc(sem("y_done"), 1)

            for j in range(4):
                expert_z(0, 0, 0, j)
            expert_z(1, 0, 1, 0)
            expert_z(1, 0, 1, 1)
            pe.wait_ge(sem("sx_done"), 4)

            def expert_steps(i, last):
                for o in range(4):
                    q = 4 * i + o
                    z = (lambda j: None) if last and o == 3 else (lambda j: expert_z(q + 1, i, o + 1, j))
                    zz = (lambda j: None) if last and o >= 2 else (lambda j: expert_z(q + 2, i, o + 2, j))
                    expert_turn(q, o, 0)
                    z(2)
                    expert_turn(q, o, 1)
                    expert_y(q, i, o, 0)
                    z(3)
                    expert_turn(q, o, 2)
                    expert_y(q, i, o, 1)
                    if last and o == 3:
                        latent_out(0)
                        turn_gain(1, 0)
                        turn_gain(1, 1)
                    expert_turn(q, o, 3)
                    zz(0)
                    expert_y(q, i, o, 2)
                    zz(1)
                    expert_y(q, i, o, 3)

            def latent_out(s):
                if s == 0:
                    pe.wait_ge(sem("fc2_in"), 16)
                    pe.wait_ge(sem("h0_ready"), 4 * 2 * EG)
                pe.wait_ge(sem("ylat_ready"), s + 1)
                for v in range(2 * s, 2 * s + 2):
                    for half in range(2):
                        t = 2 * (v % 2) + half
                        ins = pe.matmul(bank[v if v < 2 else 4 + v][:, half * C:half * C + C],
                                        ylat[:, s, t * P:t * P + P], fc2w[:], start=True, stop=True)
                    ins.then_inc(sem("fo_ready"), 1)

            expert_steps(0, False)
            with pe.Fori(1, EG // 2 - 1) as i:
                expert_steps(i, False)
            expert_steps(EG // 2 - 1, True)
            latent_out(1)

            turn_gain(1, 2)
            turn_gain(1, 3)
            pe.wait_ge(sem("q_quant"), 2)

            def first(t, tag, quant, weights, banks):
                p = t % 2
                pe.wait_ge(sem(quant), t + 1)
                wait(pe, sem("q1T" + tag + "_ready"), t)
                for k in range(KC):
                    ins = pe.transpose(bank[4][:, k * P:k * P + P], qf[:, p, k * P:k * P + P], ident[:])
                ins.then_inc(sem("q1t" + tag + "_ready"), 1)
                pe.wait_ge(sem("q1T" + tag + "_ready"), t + 1)
                if not tag:
                    wait(pe, sem("pre_ready"), t - 1)
                for n, (b, w) in enumerate(zip(banks(p), weights)):
                    if tag and n % 2 == 0:
                        wait(pe, sem("h3_ready"), 2 * t + n // 2 - 1)
                    for k in range(KC):
                        ins = pe.matmul(bank[b][:], qT[:, p, k, :], w(k), start=(k == 0), stop=(k == KC - 1))
                    if n % 2:
                        ins.then_inc(sem("m1" + tag + "_ready"), 1)

            def second(t, tag, quant, out_ready, weight):
                p = t % 2
                pe.wait_ge(sem(quant), t + 1)
                for h in range(2):
                    wait(pe, sem("q2T_ready" + tag), 2 * t - 1 + h)
                    for j in range(4):
                        c = 4 * h + j
                        ins = pe.transpose(bank[5 + h][:, j * P:j * P + P], gl[:, p, c * P:c * P + P], ident[:])
                    ins.then_inc(sem("q2t_ready" + tag), 1)
                wait(pe, sem(out_ready), t)
                for c in range(8):
                    if c % 4 == 0:
                        pe.wait_ge(sem("q2T_ready" + tag), 2 * t + c // 4 + 1)
                    ins = pe.matmul(bank[7][:, 0:C], q2T[:, p, c, :], weight(c), start=(c == 0), stop=(c == 7))
                ins.then_inc(sem("m2_ready" + tag), 1)

            w_first = [lambda k, h=h: q1w[:, k, 512 * h:512 * h + 512] for h in range(2)]
            for t in range(-2, NT):
                if t == -1:
                    pe.wait_ge(sem("cond_ready"), 8)
                if t == 0:
                    pe.wait_ge(sem("x1_ready"), 4)
                if t + 2 < NT:
                    first(t + 2, "", "q1_ready", w_first, lambda p: (2 * p, 2 * p + 1))
                if t == NT - 2:
                    pe.wait_ge(sem("pre_ready"), NT)
                    turn_gain(2, 0)
                    turn_gain(2, 1)
                if t >= 0:
                    second(t, "", "q2_ready", "x2_ready", lambda c: q2w[:, c, :])

            turn_cond(2, 4, 0)
            turn_gain(2, 2)
            turn_gain(2, 3)
            pe.wait_ge(sem("rt_split"), 1)
            pe.wait_ge(sem("cT_low"), 6)
            scores_up(bank[5], E2, rthi, rtlo, 0)
            turn_cond(2, 4, 1)
            pe.wait_ge(sem("cT_low"), 8)
            scores_up(bank[6], E2, rthi, rtlo, 1)
            scores_back(bank[4], E2, 4)
            ins_back[0].then_inc(sem("logit_ready"), 1)

            def glu_step(e):
                pe.wait_ge(sem("gu_split"), e + 1)
                for s in range(2):
                    for j in range(4):
                        u, p = 8 * e + 4 * s + j, j % 2
                        wait(pe, sem("hh_ready"), u - 1)
                        for up in range(2):
                            for k in range(KC):
                                w = slice(up * I2 + j * P, up * I2 + j * P + P)
                                ins = mm3(bank[2 * p + up][:], (guhi[:, k, w], gulo[:, k, w]),
                                          cT(k, HALF * s, HALF * s + HALF), k == 0, k == KC - 1)
                        ins.then_inc(sem("gu_done"), 1)
                pe.wait_ge(sem("dn_split"), e + 1)
                for s in range(2):
                    wait(pe, sem("hlo_ready"), 8 * e + 4 * s + 4)
                    for t in range(TH):
                        v = 8 * e + 4 * s + t
                        wait(pe, sem("acc_ready"), v - 3)
                        for j in range(4):
                            ins = mm3(bank[4 + t][:, 0:C], (hhi[:, s, j, t * P:t * P + P], hlo[:, s, j, t * P:t * P + P]),
                                      (dnhi[:, j, :], dnlo[:, j, :]), j == 0, j == 3)
                        ins.then_inc(sem("d_done"), 1)

            pe.wait_ge(sem("lexp_ready"), 1)
            glu_step(0)
            with pe.Fori(1, E2) as e:
                glu_step(e)

            for b in range(B):
                turn_gain(3, b)
            pe.wait_ge(sem("t_quant"), 3)
            pe.wait_ge(sem("cond_ready"), 16)
            w_first = [lambda k, m=m, h=h: tw[:, m, HID * k + 512 * h:HID * k + 512 * h + 512]
                       for h in range(2) for m in range(2)]
            for t in range(-2, NT):
                if t + 2 < NT:
                    first(t + 2, "3", "q13_ready", w_first, lambda p: (0, 2, 1, 3))
                if t >= 0:
                    second(t, "3", "q23_ready", "x4_ready", lambda c: tw[:, 2, C * c:C * c + C])


def kernel(x, fside_BxSxS_0, cond_512, L0_cond_w, L0_cond_u, L0_ffn_gate_w, L0_ffn_gate_bias, L0_ffn_fc1_w,
           L0_ffn_fc2_w, L0_ffn_w1, L0_ffn_w2, L0_ffn_shared_up_w, L0_ffn_shared_down_w, L1_cond_w, L1_cond_u,
           L1_ffn_W1, L1_ffn_B1, L1_ffn_W2, L1_ffn_B2, L2_cond_w, L2_cond_u, L2_ffn_gate_weight,
           L2_ffn_gate_up_proj, L2_ffn_down_proj, L3_cond_w, L3_cond_u, L3_ffn_w1, L3_ffn_w2, L3_ffn_w3):
    import numpy as np
    import concourse.bacc as bacc
    from concourse.bass_utils import run_bass_kernel_spmd

    def rows(w, inner):
        w = np.asarray(w).T
        return w.reshape(inner // P, P, w.shape[1]).transpose(1, 0, 2)

    def spread(v):
        v = np.asarray(v).reshape(1, -1)
        return np.broadcast_to(v, (P, v.shape[1]))

    def channels(*vs):
        return np.stack([np.asarray(v).reshape(KC, P).T for v in vs], axis=1)

    xs = np.asarray(x)
    small = np.concatenate([rows(L0_ffn_gate_w, C), rows(L0_ffn_fc1_w, C), rows(L0_ffn_shared_up_w, C)], axis=2)
    gu = np.asarray(L2_ffn_gate_up_proj).transpose(0, 2, 1).reshape(E2, KC, P, 2 * I2).transpose(0, 2, 1, 3)
    dn = np.asarray(L2_ffn_down_proj).transpose(0, 2, 1).reshape(E2, I2 // P, P, C).transpose(0, 2, 1, 3)
    ins = {
        "x": xs.reshape(NT, P, C).transpose(1, 0, 2),
        "kt": np.asarray(fside_BxSxS_0).reshape(B, S, KC, P).transpose(3, 0, 2, 1).reshape(P, NBLK, S),
        "te": spread(cond_512).reshape(P, B, 64),
        "w": channels(L0_cond_w, L1_cond_w, L2_cond_w, L3_cond_w),
        "u": channels(L0_cond_u, L1_cond_u, L2_cond_u, L3_cond_u),
        "sm": small,
        "gbias": spread(L0_ffn_gate_bias),
        "down": rows(L0_ffn_shared_down_w, SH),
        "fc2": np.asarray(L0_ffn_fc2_w).T,
        "w1": np.asarray(L0_ffn_w1).transpose(2, 0, 1).reshape(P, EG, 4 * INTER),
        "w2": np.asarray(L0_ffn_w2).transpose(2, 0, 1).reshape(P, EG, 4, LAT),
        "q1": rows(L1_ffn_W1, C), "q1b": spread(L1_ffn_B1),
        "q2": rows(L1_ffn_W2, HID), "q2b": spread(L1_ffn_B2),
        "rt": rows(L2_ffn_gate_weight, C),
        "gu": gu, "dn": dn,
        "t1": rows(L3_ffn_w1, C).reshape(P, -1), "t2": rows(L3_ffn_w2, C).reshape(P, -1),
        "t3": rows(L3_ffn_w3, HID).reshape(P, -1),
    }
    nc = bacc.Bacc("TRN2", target_bir_lowering=False, num_devices=1)
    arrays, args = {}, []
    for name, a in ins.items():
        a = np.ascontiguousarray(a)
        arrays["in_" + name] = a
        args.append(nc.dram_tensor("in_" + name, a.shape, mybir.dt.from_np(a.dtype), kind="ExternalInput").ap())
    out = nc.dram_tensor("out_x", (P, NT, C), F32, kind="ExternalOutput").ap()
    build(nc, *args, out)
    got = run_bass_kernel_spmd(nc, [arrays], core_ids=[0]).results[0]["out_x"]
    return np.ascontiguousarray(got.transpose(1, 0, 2)).reshape(xs.shape)
```

```python
from contextlib import ExitStack

import concourse.bass as bass
from concourse import mybir

F32 = mybir.dt.float32
F32R = mybir.dt.float32r
BF16 = mybir.dt.bfloat16
ALU = mybir.AluOpType
ACT = mybir.ActivationFunctionType
AX = mybir.AxisListType

P = 128
B, S, C = 4, 256, 256
TOK = B * S
NT = TOK // P
KC = C // P
NBLK = B * KC
HALF = TOK // 2
TH = NT // 2
LAT = INTER = 128
E0, G0 = 32, 4
EG = E0 // G0
SH = 512
HID = 1024
E2, I2 = 8, 512
ROUND = 12582912.0
Q = 127.0
ROUTED_SCALE = 2.5


def wait(eng, sem, value):
    if not isinstance(value, int) or value > 0:
        eng.wait_ge(sem, value)


def build(nc, x_d, kt_d, te_d, w_d, u_d, sm_d, gbias_d, down_d, fc2_d, w1_d, w2_d,
          q1_d, q1b_d, q2_d, q2b_d, rt_d, gu_d, dn_d, t1_d, t2_d, t3_d, out_d):
    with ExitStack() as ctx:
        sems = {}

        def sem(name):
            if name not in sems:
                sems[name] = ctx.enter_context(nc.semaphore(name))
            return sems[name]

        cursor = [-(-nc.sbuf_base // 32) * 32]

        def sb(name, shape, dt=F32):
            size = 2 if dt == BF16 else 4
            for n in shape[1:]:
                size *= n
            t = nc.alloc_sbuf_tensor_at(name, shape, dt, offset=cursor[0])
            cursor[0] += -(-size // 32) * 32
            return t

        ident = sb("ident", [P, P])
        x = sb("x", [P, NT, C])
        kT = sb("kT", [P, NBLK, S])
        ekk = sb("ekk", [P, NBLK, 2, S])
        GT = sb("GT", [P, 2, NBLK, S])
        eu = sb("eu", [P, 2, 2, S])
        fw = sb("fw", [P, 2, 2, S])
        ekb = sb("ekb", [P, 2, 2, S])
        bw = sb("bw", [P, 2, 2, S])
        cond = sb("cond", [P, NT, C])
        cThi = sb("cThi", [P, KC, TOK], F32R)
        cTlo = sb("cTlo", [P, KC, TOK], F32R)
        b1bc = sb("b1bc", [P, HID])
        b2bc = sb("b2bc", [P, C])
        table = sb("table", [P, 5])
        te = sb("te", [P, B, 64])
        wl = sb("wl", [P, 4, KC])
        ul = sb("ul", [P, 4, KC])
        dec = sb("dec", [P, 4, B, KC])
        ubk = sb("ubk", [P, 4, B, KC])
        gain = sb("gain", [P, B, KC])
        tfb = sb("tfb", [P, 4, B])
        low4 = sb("low4", [P, G0, G0])
        low8 = sb("low8", [P, E2, E2])
        cw0 = sb("cw0", [P, NT, E0])
        cw2 = sb("cw2", [P, NT, E2])
        st = sb("st", [P, 12, NT])
        pt = sb("pt", [P, 8, 2])
        ws = sb("ws", [P, 24])
        region = cursor[0]

        sm_raw = sb("sm_raw", [P, KC, E0 + LAT + SH])
        sm_hi = sb("sm_hi", [P, KC, E0 + LAT + SH], F32R)
        sm_lo = sb("sm_lo", [P, KC, E0 + LAT + SH], F32R)
        downw = sb("downw", [P, SH // P, C])
        fc2w = sb("fc2w", [P, C])
        xlhi = sb("xlhi", [P, TOK], F32R)
        xllo = sb("xllo", [P, TOK], F32R)
        hx = sb("hx", [P, 2, TH, 512])
        hT = sb("hT", [P, 2, 512])
        rl = sb("rl", [P, 2, 512])
        w1raw = sb("w1raw", [P, 2, 512])
        w1hi = sb("w1hi", [P, 2, 512], F32R)
        w1lo = sb("w1lo", [P, 2, 512], F32R)
        w2raw = sb("w2raw", [P, 2, 4, LAT])
        gbias = sb("gbias", [P, E0])
        rt = sb("rt", [P, 12, NT * E0])
        ylat = sb("ylat", [P, 2, HALF])
        top8 = sb("top8", [P, NT, 8])
        ends = [cursor[0]]

        cursor[0] = region
        guraw = sb("guraw", [P, KC, 2 * I2])
        dnraw = sb("dnraw", [P, I2 // P, C])
        guhi = sb("guhi", [P, KC, 2 * I2], F32R)
        gulo = sb("gulo", [P, KC, 2 * I2], F32R)
        dnhi = sb("dnhi", [P, I2 // P, C], F32R)
        dnlo = sb("dnlo", [P, I2 // P, C], F32R)
        rtraw = sb("rtraw", [P, KC, E2])
        rthi = sb("rthi", [P, KC, E2], F32R)
        rtlo = sb("rtlo", [P, KC, E2], F32R)
        region2 = cursor[0]
        hhi = sb("hhi", [P, 2, I2 // P, HALF], F32R)
        hlo = sb("hlo", [P, 2, I2 // P, HALF], F32R)
        sl = sb("sl", [P, 2, HALF])
        hh = sb("hh", [P, 2, HALF])
        r2 = sb("r2", [P, 10, NT, E2])
        r2c = sb("r2c", [P, 2, NT, E2 * E2])
        ends.append(cursor[0])

        cursor[0] = region2
        qf = sb("qf", [P, 2, C])
        qT = sb("qT", [P, 2, KC, P], BF16)
        xp = sb("xp", [P, 2, HID])
        gl = sb("gl", [P, 3, HID])
        q2T = sb("q2T", [P, 2, HID // P, P], BF16)
        junk = sb("junk", [P, HID])
        ends.append(cursor[0])

        cursor[0] = max(ends)
        region3 = cursor[0]
        q1raw = sb("q1raw", [P, KC, HID])
        q2raw = sb("q2raw", [P, HID // P, C])
        q1w = sb("q1w", [P, KC, HID], BF16)
        q2w = sb("q2w", [P, HID // P, C], BF16)
        cursor[0] = region3
        traw = sb("traw", [P, KC * HID])
        tw = sb("tw", [P, 3, KC * HID], BF16)
        assert max(cursor[0], region3 + 24 * 1024) <= nc.sbuf_usable_end

        bank = [ctx.enter_context(nc.psum_tensor(f"bank{i}", [P, 512], F32)) for i in range(8)]

        def one(ap, spec, **kw):
            return ap.rearrange(spec, **kw)

        DONE = [NBLK, 3 * NBLK, 3 * NBLK, 4 * NBLK]

        def sT(n):
            if n == E0:
                return hT[0:n, :, :].rearrange("p a n -> p (a n)")
            return r2c[0:n, :, :, :].rearrange("p a t n -> p (a t n)")

        def gain_bank(l, b):
            return bank[((0, 1, 4, 7), (2, 3, 5, 6), (0, 1, 4, 7), (0, 1, 5, 6))[l][b]]

        def cond_bank(n):
            return bank[(2, 3, 5, 6)[n % 4]]

        def down_bank(v):
            return bank[(5, 6, 4, 7)[v]]

        block = ctx.enter_context(nc.Block())

        @block.sync
        def _(sp):
            for b in range(B):
                sp.dma_start(kT[:, 2 * b:2 * b + 2, :], kt_d[:, 2 * b:2 * b + 2, :]).then_inc(sem(f"kT_in{b}"), 16)
                if b == 0:
                    for dst, src in ((te, te_d), (wl, w_d), (ul, u_d)):
                        sp.dma_start(dst[:], src).then_inc(sem("small_in"), 16)
                if b < 2:
                    sp.dma_start(x[:, TH * b:TH * b + TH, :], x_d[:, TH * b:TH * b + TH, :]).then_inc(sem(f"x_in{b}"), 16)
            sp.dma_start(sm_raw[:], sm_d).then_inc(sem("sm_in"), 16)
            sp.dma_start(gbias[:], gbias_d).then_inc(sem("gbias_in"), 16)
            sp.dma_start(downw[:], down_d).then_inc(sem("down_in"), 16)
            sp.dma_start(fc2w[:], fc2_d).then_inc(sem("fc2_in"), 16)
            for dst, src in ((q1raw, q1_d), (q2raw, q2_d)):
                sp.dma_start(dst[:], src).then_inc(sem("q_in"), 16)
            for dst, src in ((b1bc, q1b_d), (b2bc, q2b_d)):
                sp.dma_start(dst[:], src).then_inc(sem("qb_in"), 16)

            def expert_weights(i, o):
                eg = 2 * i + o
                wait(sp, sem("w1_split"), eg - 1)
                sp.dma_start(w1raw[:, o, :], w1_d[:, eg, :]).then_inc(sem(f"w1_in{o}"), 16)
                wait(sp, sem("y_done"), 8 * eg - 8)
                sp.dma_start(w2raw[:, o, :, :], w2_d[:, eg, :, :]).then_inc(sem(f"w2_in{o}"), 16)

            expert_weights(0, 0)
            expert_weights(0, 1)
            with sp.Fori(1, EG // 2) as i:
                expert_weights(i, 0)
                expert_weights(i, 1)

            sp.wait_ge(sem("x1_ready"), 4)
            sp.dma_start(rtraw[:], rt_d).then_inc(sem("rt_in"), 16)

            def glu_weights(e):
                wait(sp, sem("gu_split"), e)
                sp.dma_start(guraw[:], gu_d[bass.ds(e, 1), :, :, :].rearrange("o p k n -> p (o k) n")
                             ).then_inc(sem("gu_in"), 16)
                wait(sp, sem("dn_split"), e)
                sp.dma_start(dnraw[:], dn_d[bass.ds(e, 1), :, :, :].rearrange("o p k n -> p (o k) n")
                             ).then_inc(sem("dn_in"), 16)

            glu_weights(0)
            glu_weights(1)
            sp.wait_ge(sem("x2_ready"), NT)
            for m, src in enumerate((t1_d, t2_d, t3_d)):
                wait(sp, sem("t_quant"), m)
                sp.dma_start(traw[:], src).then_inc(sem("t_in"), 16)
                glu_weights(m + 2)
            with sp.Fori(5, E2) as e:
                glu_weights(e)
            for t in range(NT):
                sp.wait_ge(sem("x4_ready"), t + 1)
                sp.dma_start(out_d[:, t, :], x[:, t, :]).then_inc(sem("out_done"), 16)
            sp.wait_ge(sem("out_done"), 16 * NT)

        @block.gpsimd
        def _(pool):
            def wait_alone(name, value):
                wait(pool, sem(name), value)
                if not isinstance(value, int):
                    pool.sem_inc(sem("pool_waited"), 1)

            pool.memset(ident[:], 0.0).then_inc(sem("consts"), 1)
            pool.memset(low4[:], 1.0).then_inc(sem("consts"), 1)
            pool.memset(low8[:], 1.0).then_inc(sem("consts"), 1)
            pool.memset(bw[:], 0.0).then_inc(sem("bw_zero"), 1)
            pool.wait_ge(sem("consts"), 3)
            pool.affine_select(out=ident[:], in_=ident[:], compare_op=ALU.not_equal, fill=1.0, base=0,
                               pattern=[[-1, P]], channel_multiplier=1).then_inc(sem("ident_ready"), 1)
            for low, n in ((low4, G0), (low8, E2)):
                pool.affine_select(out=low[:], in_=low[:], compare_op=ALU.is_gt, fill=0.0, base=0,
                                   pattern=[[1, n], [-1, n]], channel_multiplier=0).then_inc(sem("low_ready"), 1)

            def wkv_sums(n, blk, p):
                wait_alone("eu_ready", n + 1)
                pool.tensor_tensor(eu[:, p, 0, :], eu[:, p, 1, :], kT[:, blk, :], ALU.mult).then_inc(sem("euv_ready"), 1)
                for d, part in ((1, "den"), (0, "num")):
                    wait_alone("scan_" + part, n + 1)
                    pool.tensor_tensor(fw[:, p, d, :], fw[:, p, d, :], bw[:, p, d, :], ALU.add).then_inc(sem("both_" + part), 1)
                    if part == "num":
                        wait_alone("euv_ready", n + 1)
                    wait_alone("both_" + part, n + 1)
                    pool.tensor_tensor(fw[:, p, d, :], fw[:, p, d, :], eu[:, p, d, :], ALU.add).then_inc(sem("sum_" + part), 1)

            for n in range(NBLK):
                wkv_sums(n, n, n % 2)

            def split_w1(i, o):
                eg = 2 * i + o
                wait_alone(f"w1_in{o}", 16 * (i + 1))
                wait_alone("z_ready", 8 * eg - 8)
                pool.tensor_scalar(w1hi[:, o, :], w1raw[:, o, :], 1.0, 0.0, ALU.mult, ALU.add).then_inc(sem("w1_high"), 1)
                wait_alone("w1_high", eg + 1)
                pool.tensor_tensor(w1lo[:, o, :], w1raw[:, o, :], w1hi[:, o, :].bitcast(F32), ALU.subtract
                                   ).then_inc(sem("w1_split"), 1)

            split_w1(0, 0)
            split_w1(0, 1)

            def expert_steps(i, last):
                for o in range(4):
                    q = 4 * i + o
                    if o % 2 and not last:
                        split_w1(i + 1, o // 2)
                    wkv_sums(NBLK + q, 2 * i + o // 2, o % 2)
                    if isinstance(i, int) and i == 0 and o == 1:
                        pool.wait_ge(sem("wmax_part"), 2)
                        pool.partition_all_reduce(ws[:, 2:4], ws[:, 0:2], P, bass.bass_isa.ReduceOp.max
                                                  ).then_inc(sem("wmax_ready"), 1)
                    if isinstance(i, int) and i == 0 and o >= 2:
                        raw = (q1raw, q2raw)[o - 2]
                        pool.wait_ge(sem("wscale_ready"), 1)
                        pool.tensor_scalar(raw[:], raw[:], ws[:, 4 + o:5 + o], ROUND, ALU.mult, ALU.add
                                           ).then_inc(sem("q_round"), 1)
                    if last and o < 2:
                        pool.wait_ge(sem("q_round"), o + 1)
                        pool.tensor_scalar((q1w, q2w)[o][:], (q1raw, q2raw)[o][:], -ROUND, 1.0, ALU.add, ALU.mult
                                           ).then_inc(sem("q_quant"), 1)

            expert_steps(0, False)
            with pool.Fori(1, EG // 2 - 1) as i:
                expert_steps(i, False)
            expert_steps(EG // 2 - 1, True)

            def quant_rows(t, scale, known, ready, free):
                p = t % 2
                pool.wait_ge(sem(known), t // TH + 1)
                wait(pool, sem(free), t - 1)
                pool.tensor_scalar(qf[:, p, :], cond[:, t, :], scale[:, t:t + 1], ROUND, ALU.mult, ALU.add
                                   ).then_inc(sem(ready), 1)

            for t in range(3):
                quant_rows(t, st[:, 2, :], "row_scale", "q1_ready", "q1t_ready")
            pool.wait_ge(sem("qb_in"), 32)
            for t in range(NT):
                if t + 3 < NT:
                    quant_rows(t + 3, st[:, 2, :], "row_scale", "q1_ready", "q1t_ready")
                pool.wait_ge(sem("sig_ready"), 2 + t // TH + 1)
                pool.tensor_tensor(x[:, t, :], x[:, t, :], b2bc[:], ALU.add).then_inc(sem("xb_ready"), 1)

            def split_glu(e):
                wait_alone("gu_in", 16 * (e + 1))
                wait_alone("gu_done", 8 * e)
                for k in range(KC):
                    pool.tensor_scalar(guhi[:, k, :], guraw[:, k, :], 1.0, 0.0, ALU.mult, ALU.add).then_inc(sem("gu_high"), 1)
                for k in range(KC):
                    wait_alone("gu_high", 2 * e + k + 1)
                    ins = pool.tensor_tensor(gulo[:, k, :], guraw[:, k, :], guhi[:, k, :].bitcast(F32), ALU.subtract)
                ins.then_inc(sem("gu_split"), 1)
                wait_alone("dn_in", 16 * (e + 1))
                wait_alone("d_done", 8 * e)
                pool.tensor_scalar(dnhi[:], dnraw[:], 1.0, 0.0, ALU.mult, ALU.add).then_inc(sem("dn_high"), 1)
                wait_alone("dn_high", e + 1)
                pool.tensor_tensor(dnlo[:], dnraw[:], dnhi[:].bitcast(F32), ALU.subtract).then_inc(sem("dn_split"), 1)

            def ternary_total(m):
                pool.wait_ge(sem("tsum_part"), m + 1)
                pool.partition_all_reduce(ws[:, 12 + m:13 + m], ws[:, 9 + m:10 + m], P,
                                          bass.bass_isa.ReduceOp.add).then_inc(sem("tsum_ready"), 1)

            def ternary_write(m):
                pool.wait_ge(sem("t_clipped"), m + 1)
                pool.tensor_scalar(tw[:, m, :], traw[:], -ROUND, 1.0, ALU.add, ALU.mult).then_inc(sem("t_quant"), 1)

            def glu_step(e, p):
                split_glu(e)
                ternary = isinstance(e, int) and e <= 3
                if ternary:
                    ternary_total(e - 1)
                wkv_sums(3 * NBLK + e - 1, e - 1, 1 - p)
                if ternary:
                    ternary_write(e - 1)

            split_glu(0)
            for e in range(1, 4):
                glu_step(e, e % 2)
            with pool.Fori(2, E2 // 2) as i:
                glu_step(2 * i, 0)
                glu_step(2 * i + 1, 1)
            wkv_sums(4 * NBLK - 1, NBLK - 1, 1)

            def rms_stats(mean_sq, root, absmax, out, sum_name, max_name, n, out_name):
                pool.wait_ge(sem(sum_name), n)
                pool.tensor_scalar(mean_sq, mean_sq, 1.0, 1e-6, ALU.mult, ALU.add).then_inc(sem("p3"), 1)
                p3[0] += 1
                pool.wait_ge(sem("p3"), p3[0])
                pool.tensor_tensor(root, mean_sq, half, ALU.pow).then_inc(sem("p3"), 1)
                p3[0] += 1
                pool.wait_ge(sem("p3"), p3[0])
                pool.wait_ge(sem(max_name), n)
                pool.tensor_tensor(out, absmax, root, ALU.mult).then_inc(sem(out_name), 1)

            p3 = [0]
            pool.memset(st[:, 11, :], -0.5).then_inc(sem("p3"), 1)
            p3[0] += 1
            pool.wait_ge(sem("p3"), p3[0])
            for s in range(2):
                half = st[:, 11, TH * s:TH * s + TH]
                rms_stats(*(st[:, i, TH * s:TH * s + TH] for i in range(4, 8)), "c3_sq", "c3_max", s + 1, "c3_stat")
                if s == 0:
                    quant_rows(0, st[:, 8, :], "c3_scale", "q13_ready", "q1t3_ready")
                    quant_rows(1, st[:, 8, :], "c3_scale", "q13_ready", "q1t3_ready")
            half = st[:, 11, 0:1]
            quant_rows(2, st[:, 8, :], "c3_scale", "q13_ready", "q1t3_ready")
            for t in range(NT):
                p = t % 2
                if t + 3 < NT:
                    quant_rows(t + 3, st[:, 8, :], "c3_scale", "q13_ready", "q1t3_ready")
                rms_stats(pt[:, 4, p:p + 1], pt[:, 5, p:p + 1], pt[:, 6, p:p + 1], pt[:, 7, p:p + 1],
                          "h3_sq", "h3_max", t + 1, "h3_norm")
                pool.wait_ge(sem("h3_norm"), t + 1)
                pool.tensor_scalar(st[:, 0, t:t + 1], pt[:, 7, p:p + 1], 1e-5, 1.0, ALU.max, ALU.mult).then_inc(sem("h3_stat"), 1)
                pool.wait_ge(sem("h3_stat"), t + 1)
                pool.tensor_tensor(st[:, 1, t:t + 1], st[:, 0, t:t + 1], ws[:, 23:24], ALU.mult).then_inc(sem("h3_scale"), 1)

        @block.scalar
        def _(act):
            act.wait_ge(sem("small_in"), 48)
            act.activation(wl[:], wl[:], ACT.Exp).then_inc(sem("a0"), 1)
            act.wait_ge(sem("a0"), 1)
            act.activation(wl[:], wl[:], ACT.Exp, scale=-1.0).then_inc(sem("wl_ready"), 1)
            act.wait_ge(sem("wl_ready"), 1)
            act.wait_ge(sem("te_sum"), 1)
            act.activation(tfb[:, 1, :], tfb[:, 0, :], ACT.Exp, scale=-1.0).then_inc(sem("te_exp"), 1)

            def load_table(i, func):
                act.activation(table[:, i:i + 1], wl[:, 0, 0:1], func)

            def wkv_exp(n, p):
                wait(act, sem("kup_ready"), n + 1)
                act.activation(eu[:, p, 1, :], eu[:, p, 1, :], ACT.Exp).then_inc(sem("eu_ready"), 1)

            def side_exp(b):
                act.wait_ge(sem("kmin_ready"), b + 1)
                act.activation(ekk[:, 2 * b:2 * b + 2, 1, :], ekk[:, 2 * b:2 * b + 2, 1, :], ACT.Exp).then_inc(sem("ek_ready"), 1)

            def sigmoid_x(l, halves=(0, 1)):
                for s in halves:
                    if l == 0:
                        act.wait_ge(sem(f"x_in{s}"), 16)
                    elif l == 1:
                        act.wait_ge(sem("x1_ready"), 2 * s + 2)
                    elif l == 2:
                        act.wait_ge(sem("x2_ready"), TH * s + TH)
                    else:
                        act.wait_ge(sem("acc_ready"), 8 * (E2 - 1) + TH * s + TH)
                    act.activation(cond[:, TH * s:TH * s + TH, :], x[:, TH * s:TH * s + TH, :],
                                   ACT.Sigmoid).then_inc(sem("sig_ready"), 1)

            def cond_high(n0, halves=(0, 1)):
                for s in halves:
                    for k in range(KC):
                        n = n0 + 2 * s + k
                        act.wait_ge(sem("cT_ready"), n + 1)
                        act.activation(cThi[:, k, HALF * s:HALF * s + HALF], cond_bank(n)[:], ACT.Copy
                                       ).then_inc(sem("cT_high"), 1)

            def scores_copy(n, src, s, done):
                act.wait_ge(sem("sT_ready"), done + s)
                act.activation(sT(n)[:, HALF * s:HALF * s + HALF], src[0:n, :], ACT.Copy).then_inc(sem("sT_copied"), 1)

            def xl_high(s):
                act.wait_ge(sem("xl_ready"), s + 1)
                act.activation(xlhi[:, HALF * s:HALF * s + HALF], bank[5 + 2 * s][:], ACT.Copy).then_inc(sem("xl_high"), 1)

            def shared_relu(u):
                act.wait_ge(sem("sz_ready"), u + 1)
                wait(act, sem("sh_ready"), u - 1)
                act.activation(rl[:, u % 2, :], bank[u % 4][:], ACT.Relu).then_inc(sem("sr_ready"), 1)

            side_exp(0)
            side_exp(1)
            wkv_exp(0, 0)
            wkv_exp(1, 1)
            sigmoid_x(0)
            side_exp(2)
            wkv_exp(2, 0)
            wkv_exp(3, 1)
            side_exp(3)
            wkv_exp(4, 0)
            act.wait_ge(sem("sm_in"), 16)
            act.activation(sm_hi[:], sm_raw[:], ACT.Copy).then_inc(sem("sm_high"), 1)
            wkv_exp(5, 1)
            def shared_first(u):
                shared_relu(u)
                act.wait_ge(sem("sr_ready"), u + 1)
                act.activation(hx[:, 0, u, :], rl[:, u % 2, :], ACT.Square).then_inc(sem("sh_ready"), 1)

            wkv_exp(6, 0)
            cond_high(0, (0,))
            wkv_exp(7, 1)
            scores_copy(E0, bank[6], 0, 1)
            xl_high(0)
            shared_first(0)
            shared_first(1)
            cond_high(0, (1,))
            shared_first(2)
            scores_copy(E0, bank[4], 1, 1)
            load_table(0, ACT.Sigmoid)
            xl_high(1)
            shared_first(3)
            act.wait_ge(sem("gate_ready"), 1)
            act.activation(rt[:, 0, :], bank[4][:, 0:NT * E0], ACT.Sigmoid).then_inc(sem("score_ready"), 1)
            for u in range(4, 8):
                shared_relu(u)

            def relu_scaled(q, i, o, j):
                eg = 2 * i + o // 2
                t = TH * (o % 2) + j
                wait(act, sem("h0_ready"), 4 * q + j - 1)
                wait(act, sem("z_ready"), 4 * q + j + 1)
                act.wait_ge(sem("cw0_ready"), 1)
                for e in range(4):
                    ins = act.activation(rl[:, j % 2, e * P:e * P + P], bank[j][:, e * P:e * P + P], ACT.Relu,
                                         scale=cw0[:, t, bass.ds(4 * eg + e, 1)])
                ins.then_inc(sem("r_ready"), 1)

            def hT_copy(q, e):
                wait(act, sem("y_done"), 4 * q + e - 1)
                wait(act, sem("t_ready"), 4 * q + e + 1)
                act.activation(hT[:, e % 2, :], bank[6 + e % 2][:], ACT.Copy).then_inc(sem("hT_ready"), 1)

            def latent_copy(s):
                act.wait_ge(sem("y_done"), 8 * EG - 4 + 4 * s)
                act.activation(ylat[:, s, :], bank[4 + s][:], ACT.Copy).then_inc(sem("ylat_ready"), 1)

            for j in range(4):
                relu_scaled(0, 0, 0, j)
            load_table(4, ACT.Exp)
            relu_scaled(1, 0, 1, 0)
            relu_scaled(1, 0, 1, 1)

            def expert_steps(i, last):
                for o in range(4):
                    q = 4 * i + o
                    more, more2 = not (last and o == 3), not (last and o >= 2)
                    hT_copy(q, 0)
                    if more:
                        relu_scaled(q + 1, i, o + 1, 2)
                    hT_copy(q, 1)
                    if more:
                        relu_scaled(q + 1, i, o + 1, 3)
                    else:
                        latent_copy(0)
                    wkv_exp(NBLK + q, o % 2)
                    hT_copy(q, 2)
                    if not more:
                        sigmoid_x(1, (0,))
                    hT_copy(q, 3)
                    if more2:
                        relu_scaled(q + 2, i, o + 2, 0)
                        relu_scaled(q + 2, i, o + 2, 1)

            expert_steps(0, False)
            with act.Fori(1, EG // 2 - 1) as i:
                expert_steps(i, False)
            expert_steps(EG // 2 - 1, True)
            latent_copy(1)


            def l1_first(t):
                p = t % 2
                act.wait_ge(sem("q1t_ready"), t + 1)
                wait(act, sem("m1_ready"), t - 1)
                act.activation(qT[:, p, :, :], bank[4][:, 0:C], ACT.Copy, bias=-ROUND).then_inc(sem("q1T_ready"), 1)

            def l1_gelu(t):
                p = t % 2
                wait(act, sem("q2t_ready"), 2 * t - 2)
                act.wait_ge(sem("pre_ready"), t + 1)
                act.activation(gl[:, p, :], xp[:, p, :], ACT.Gelu_apprx_tanh).then_inc(sem("gelu_ready"), 1)

            def l1_quant(t):
                p = t % 2
                act.wait_ge(sem("q2_scale"), t + 1)
                act.activation(gl[:, p, :], gl[:, p, :], ACT.Copy, bias=ROUND, scale=pt[:, 2, p:p + 1]
                               ).then_inc(sem("q2_ready"), 1)

            def l1_second(t, tag=""):
                p = t % 2
                wait(act, sem("m2_ready" + tag), t - 1)
                for h in range(2):
                    act.wait_ge(sem("q2t_ready" + tag), 2 * t + h + 1)
                    act.activation(q2T[:, p, 4 * h:4 * h + 4, :], bank[5 + h][:], ACT.Copy, bias=-ROUND
                                   ).then_inc(sem("q2T_ready" + tag), 1)

            for t in range(-2, NT):
                if t + 2 < NT:
                    l1_first(t + 2)
                if t == -2:
                    sigmoid_x(1, (1,))
                    load_table(1, ACT.Gelu_apprx_tanh)
                if t == 0:
                    l1_quant(t)
                if 0 <= t + 1 < NT:
                    l1_gelu(t + 1)
                if t > 0:
                    l1_quant(t)
                if t == NT - 1:
                    sigmoid_x(2, (0,))
                if t >= 0:
                    l1_second(t)

            cond_high(4, (0,))
            sigmoid_x(2, (1,))
            scores_copy(E2, bank[0], 0, 3)
            cond_high(4, (1,))

            def silu_gate(u, p):
                wait(act, sem("hh_ready"), u - 1)
                wait(act, sem("gu_done"), u + 1)
                act.activation(sl[:, p, :], bank[2 * p][:], ACT.Silu).then_inc(sem("sl_ready"), 1)

            def glu_step(e, p, first=False):
                for j in range(8):
                    if first and j == 1:
                        scores_copy(E2, bank[5], 1, 3)
                    silu_gate(8 * e + j, j % 2)
                    if first and j == 3:
                        act.wait_ge(sem("lsub_ready"), 1)
                        act.activation(r2[:, 1, :, :], r2[:, 1, :, :], ACT.Exp).then_inc(sem("lexp_ready"), 1)
                        load_table(2, ACT.Silu)
                wkv_exp(3 * NBLK + e, p)

            glu_step(0, 0, True)
            glu_step(1, 1)
            with act.Fori(1, E2 // 2) as i:
                glu_step(2 * i, 0)
                glu_step(2 * i + 1, 1)

            sigmoid_x(3)
            for t in range(NT):
                act.wait_ge(sem("cond_ready"), 12 + t // 2 + 1)
                if t == TH:
                    ins.then_inc(sem("c3_sq"), 1)
                ins = act.activation(xp[:, t // TH, C * (t % TH):C * (t % TH) + C], cond[:, t, :], ACT.Square, scale=C ** -0.5, accum_out=st[:, 4, t:t + 1])
            ins.then_inc(sem("c3_sq"), 1)
            load_table(3, ACT.Silu)

            def l3_first(t):
                p = t % 2
                act.wait_ge(sem("q1t3_ready"), t + 1)
                wait(act, sem("m13_ready"), 2 * t - 2)
                act.activation(qT[:, p, :, :], bank[4][:, 0:C], ACT.Copy, bias=-ROUND).then_inc(sem("q1T3_ready"), 1)

            def l3_silu(t):
                p = t % 2
                act.wait_ge(sem("c3_scale"), t // TH + 1)
                for h in range(2):
                    act.wait_ge(sem("m13_ready"), 2 * t + h + 1)
                    wait(act, sem("h3_ready"), 2 * t + h - 3)
                    act.activation(xp[:, p, 512 * h:512 * h + 512], bank[h][:], ACT.Silu, scale=st[:, 9, t:t + 1]
                                   ).then_inc(sem("silu3_ready"), 1)

            def l3_square(t):
                p = t % 2
                act.wait_ge(sem("h3_ready"), 2 * t + 2)
                wait(act, sem("h3_sq"), t)
                wait(act, sem("q23_ready"), t - 1)
                act.activation(junk[:], gl[:, t % 3, :], ACT.Square, scale=HID ** -0.5, accum_out=pt[:, 4, p:p + 1]
                               ).then_inc(sem("h3_sq"), 1)

            for t in range(-2, NT):
                if t + 2 < NT:
                    l3_first(t + 2)
                if 0 <= t + 1 < NT:
                    l3_square(t + 1)
                if t + 2 < NT:
                    l3_silu(t + 2)
                if t >= 0:
                    l1_second(t, "3")

        @block.vector
        def _(dve):
            count = [0]

            def chain(ins):
                count[0] += 1
                ins.then_inc(sem("dve_step"), 1)
                dve.wait_ge(sem("dve_step"), count[0])

            dve.wait_ge(sem("small_in"), 48)
            dve.tensor_reduce(tfb[:, 0, :], te[:], AX.X, ALU.add).then_inc(sem("te_sum"), 1)

            def side_exp(b):
                dve.wait_ge(sem(f"kT_in{b}"), 16)
                dve.tensor_scalar(ekk[:, 2 * b:2 * b + 2, 1, :], kT[:, 2 * b:2 * b + 2, :], 30.0, None, ALU.min
                                  ).then_inc(sem("kmin_ready"), 1)

            side_exp(0)
            dve.wait_ge(sem("te_exp"), 1)
            chain(dve.tensor_scalar(tfb[:, 1, :], tfb[:, 1, :], 1.0, None, ALU.add))
            chain(dve.reciprocal(tfb[:, 0, :], tfb[:, 1, :]))
            dve.tensor_scalar(tfb[:, 2, :], tfb[:, 0, :], 0.5, 0.5, ALU.mult, ALU.add)
            chain(dve.tensor_scalar(tfb[:, 3, :], tfb[:, 0, :], 0.2, 0.8, ALU.mult, ALU.add))
            dve.wait_ge(sem("wl_ready"), 1)
            lbk, per_b = [P, 4, B, KC], tfb[:].rearrange("p i (o b q) -> p i o b q", o=1, q=1)
            dve.tensor_tensor(dec[:], wl[:].rearrange("p l (o k) -> p l o k", o=1).to_broadcast(lbk),
                              per_b[:, 2, :, :, :].to_broadcast(lbk), ALU.mult)
            dve.tensor_copy(ubk[:], ul[:].rearrange("p l (o k) -> p l o k", o=1).to_broadcast(lbk))
            chain(dve.tensor_copy(gain[:], per_b[:, 3, 0, :, :].to_broadcast([P, B, KC])))
            side_exp(1)
            decf = dec[:].rearrange("p l b k -> p (l b k)")
            ubf = ubk[:].rearrange("p l b k -> p (l b k)")
            gf = gain[:].rearrange("p b k -> p (b k)")

            def col(ap, i):
                return ap[:, i:i + 1] if isinstance(i, int) else ap[:, bass.ds(i, 1)]

            def early(n):
                return isinstance(n, int) and n < NBLK

            def wkv_kup(n, l, blk, p):
                wait(dve, sem("sum_num"), n - 1)
                dve.tensor_scalar(eu[:, p, 1, :], kT[:, blk, :], col(ubf, NBLK * l + blk), 30.0, ALU.add, ALU.min
                                  ).then_inc(sem("kup_ready"), 1)
                if not early(n):
                    dve.tensor_copy(ekb[:, p, :, :], ekk[:, blk, :, :]).then_inc(sem("ekb_ready"), 1)

            def wkv_scan(n, l, blk, p, part):
                d = 1 - part // 2
                if part == 0:
                    wait(dve, sem("G_ready"), n - 1)
                if part % 2 == 0:
                    dve.tensor_tensor_scan(fw[:, p, d, :], col(decf, NBLK * l + blk).to_broadcast([P, S]),
                                           ekk[:, blk, d, :], 0.0, ALU.mult, ALU.add)
                else:
                    if not early(n):
                        wait(dve, sem("ekb_ready"), n - NBLK + 1)
                    back = ekk[:, blk, d, S - 1:0:-1] if early(n) else ekb[:, p, d, S - 1:0:-1]
                    dve.tensor_tensor_scan(bw[:, p, d, S - 2::-1], back, col(decf, NBLK * l + blk).to_broadcast([P, S - 1]),
                                           0.0, ALU.add, ALU.mult).then_inc(sem("scan_num" if part == 3 else "scan_den"), 1)

            def gain_max(n, p):
                wait(dve, sem("sum_den"), n + 1)
                dve.tensor_scalar(fw[:, p, 1, :], fw[:, p, 1, :], 1e-8, None, ALU.max).then_inc(sem("den_ready"), 1)

            def gain_reciprocal(n, p):
                wait(dve, sem("den_ready"), n + 1)
                dve.reciprocal(fw[:, p, 1, :], fw[:, p, 1, :]).then_inc(sem("rden_ready"), 1)

            def gain_out(n, l, blk, p):
                wait(dve, sem("sum_num"), n + 1)
                wait(dve, sem("rden_ready"), n + 1)
                dve.scalar_tensor_tensor(out=GT[:, l % 2, blk, :], in0=fw[:, p, 0, :], scalar=col(gf, blk),
                                         in1=fw[:, p, 1, :], op0=ALU.mult, op1=ALU.mult).then_inc(sem("G_ready"), 1)

            def wkv_gain(n, l, blk, p):
                gain_max(n, p)
                gain_reciprocal(n, p)
                gain_out(n, l, blk, p)

            def make_cond(l, b):
                m = 4 * l + b
                dve.wait_ge(sem("G_turned"), m + 1)
                dve.wait_ge(sem("sig_ready"), 2 * l + b // 2 + 1)
                dve.tensor_tensor(cond[:, 2 * b:2 * b + 2, :], gain_bank(l, b)[:].rearrange("p (t c) -> p t c", t=2),
                                  cond[:, 2 * b:2 * b + 2, :], ALU.mult).then_inc(sem("cond_ready"), 1)

            def cond_low(n0, s, k):
                n = n0 + 2 * s + k
                dve.wait_ge(sem("cT_high"), n + 1)
                dve.tensor_tensor(cTlo[:, k, HALF * s:HALF * s + HALF], cond_bank(n)[:],
                                  cThi[:, k, HALF * s:HALF * s + HALF].bitcast(F32), ALU.subtract
                                  ).then_inc(sem("cT_low"), 1)

            def xl_low(s):
                dve.wait_ge(sem("xl_high"), s + 1)
                dve.tensor_tensor(xllo[:, HALF * s:HALF * s + HALF], bank[5 + 2 * s][:],
                                  xlhi[:, HALF * s:HALF * s + HALF].bitcast(F32), ALU.subtract).then_inc(sem("xl_low"), 1)

            def shared_h(u):
                dve.wait_ge(sem("sr_ready"), u + 1)
                dve.scalar_tensor_tensor(out=hx[:, u // 4, u % 4, :], in0=bank[u % 4][:], scalar=0.0, in1=rl[:, u % 2, :],
                                         op0=ALU.max, op1=ALU.mult).then_inc(sem("sh_ready"), 1)

            def add_shared(v):
                dve.wait_ge(sem("sd_ready"), v + 1)
                dve.tensor_tensor(x[:, 2 * v:2 * v + 2, :], down_bank(v)[:].rearrange("p (t c) -> p t c", t=2),
                                  x[:, 2 * v:2 * v + 2, :], ALU.add).then_inc(sem("sx_done"), 1)

            def small_low():
                dve.wait_ge(sem("sm_high"), 1)
                dve.tensor_tensor(sm_lo[:], sm_raw[:], sm_hi[:].bitcast(F32), ALU.subtract).then_inc(sem("sm_low"), 1)

            between = {(5, 2): [small_low], (5, 3): [lambda: make_cond(0, 0), lambda: make_cond(0, 1)],
                       (6, 2): [lambda: cond_low(0, 0, 0)], (6, 3): [lambda: cond_low(0, 0, 1)]}
            dve.wait_ge(sem("bw_zero"), 1)
            for b in range(B):
                dve.wait_ge(sem("ek_ready"), b + 1)
                chain(dve.tensor_tensor(ekk[:, 2 * b:2 * b + 2, 0, :], ekk[:, 2 * b:2 * b + 2, 1, :],
                                        kT[:, 2 * b:2 * b + 2, :], ALU.mult))
                if 0 < b < B - 1:
                    side_exp(b + 1)
                for n in (2 * b, 2 * b + 1):
                    wkv_kup(n, 0, n, n % 2)
                    for part in range(4):
                        wkv_scan(n, 0, n, n % 2, part)
                        if n and part == 1:
                            gain_max(n - 1, (n - 1) % 2)
                        if n and part == 2:
                            gain_reciprocal(n - 1, (n - 1) % 2)
                        if n and part == 3:
                            gain_out(n - 1, 0, n - 1, (n - 1) % 2)
                        for step in between.get((n, part), ()):
                            step()
            make_cond(0, 2)
            wkv_gain(NBLK - 1, 0, NBLK - 1, 1)
            xl_low(0)
            make_cond(0, 3)
            cond_low(0, 1, 0)
            cond_low(0, 1, 1)
            xl_low(1)

            def ranks(score, low, n, a, b, rank):
                four = dict(o=1)
                other = score.rearrange("p t (o g) -> p t o g", **four).to_broadcast([P, NT, n, n])
                own = score.rearrange("p t (g o) -> p t g o", **four).to_broadcast([P, NT, n, n])
                lowb = low[:].rearrange("p (o g) h -> p o g h", **four).to_broadcast([P, NT, n, n])
                dve.tensor_tensor(a, other, own, ALU.is_gt)
                chain(dve.tensor_tensor(b, other, own, ALU.is_equal))
                chain(dve.tensor_tensor(b, b, lowb, ALU.mult))
                chain(dve.tensor_tensor(a, a, b, ALU.add))
                chain(dve.tensor_reduce(rank, a, AX.X, ALU.add))

            def r(i, n=NT * E0):
                return rt[:, i, 0:n]

            def g8(i, w=8):
                return rt[:, i, 0:NT * G0 * w].rearrange("p (t w) -> p t w", w=w)

            dve.wait_ge(sem("score_ready"), 1)
            dve.wait_ge(sem("gbias_in"), 16)
            dve.wait_ge(sem("low_ready"), 2)
            chain(dve.tensor_tensor(r(1).rearrange("p (t e) -> p t e", e=E0), r(0).rearrange("p (t e) -> p t e", e=E0),
                                    gbias[:].rearrange("p (o e) -> p o e", o=1).to_broadcast([P, NT, E0]), ALU.add))
            sc = g8(1)
            hi4, lo4 = g8(2, 4), g8(3, 4)
            dve.tensor_tensor(hi4, sc[:, :, 0:4], sc[:, :, 4:8], ALU.max)
            chain(dve.tensor_tensor(lo4, sc[:, :, 0:4], sc[:, :, 4:8], ALU.min))
            hi, lo = hi4, lo4
            for lev, w in ((0, 2), (1, 1)):
                nh, nl, ml, ll = (g8(4 + 4 * lev + i, w) for i in range(4))
                dve.tensor_tensor(nh, hi[:, :, 0:w], hi[:, :, w:2 * w], ALU.max)
                dve.tensor_tensor(ml, hi[:, :, 0:w], hi[:, :, w:2 * w], ALU.min)
                chain(dve.tensor_tensor(ll, lo[:, :, 0:w], lo[:, :, w:2 * w], ALU.max))
                chain(dve.tensor_tensor(nl, ml, ll, ALU.max))
                hi, lo = nh, nl
            shared_h(4)
            gs = rt[:, 2, 0:NT * G0].rearrange("p (t g) -> p t g", g=G0)
            chain(dve.tensor_tensor(rt[:, 2, 0:NT * G0], rt[:, 8, 0:NT * G0], rt[:, 9, 0:NT * G0], ALU.add))
            sq = [rt[:, i, 0:NT * G0 * G0].rearrange("p (t g h) -> p t g h", g=G0, h=G0) for i in (3, 4)]
            ranks(gs, low4, G0, sq[0], sq[1], rt[:, 5, 0:NT * G0].rearrange("p (t g) -> p t g", g=G0))
            shared_h(5)
            shared_h(6)
            chain(dve.tensor_scalar(rt[:, 6, 0:NT * G0], rt[:, 5, 0:NT * G0], 2.0, None, ALU.is_lt))
            dve.tensor_scalar(rt[:, 7, 0:NT * G0], rt[:, 6, 0:NT * G0], -1.0, 3.0e38, ALU.add, ALU.mult)

            def over8(i):
                return rt[:, i, 0:NT * G0].rearrange("p (t o) -> p t o", o=1).to_broadcast([P, NT * G0, 8])

            chain(dve.tensor_tensor(g8(8), sc, over8(6), ALU.mult))
            chain(dve.tensor_tensor(g8(8), g8(8), over8(7), ALU.add))
            shared_h(7)
            for t in range(NT):
                ins = dve.max(top8[:, t, :], rt[:, 8, t * E0:t * E0 + E0])
            chain(ins)
            for t in range(NT):
                ins = dve.match_replace(rt[:, 9, t * E0:t * E0 + E0], top8[:, t, :], rt[:, 8, t * E0:t * E0 + E0], -3.3e38)
            chain(ins)
            chain(dve.tensor_tensor(r(10), r(9), r(8), ALU.not_equal))
            chain(dve.tensor_tensor(r(10), r(10), r(0), ALU.mult))
            chain(dve.tensor_reduce(rt[:, 11, 0:NT], r(10).rearrange("p (t e) -> p t e", e=E0), AX.X, ALU.add))
            chain(dve.reciprocal(rt[:, 11, NT:2 * NT], rt[:, 11, 0:NT]))
            chain(dve.tensor_scalar(rt[:, 11, 2 * NT:3 * NT], rt[:, 11, NT:2 * NT], ROUTED_SCALE, None, ALU.mult))
            dve.tensor_tensor(cw0[:], r(10).rearrange("p (t e) -> p t e", e=E0),
                              rt[:, 11, 2 * NT:3 * NT].rearrange("p (t o) -> p t o", o=1).to_broadcast([P, NT, E0]),
                              ALU.mult).then_inc(sem("cw0_ready"), 1)

            add_shared(0)
            add_shared(1)

            def weight_max(m):
                if m == 0:
                    dve.wait_ge(sem("q_in"), 32)
                dve.tensor_reduce(ws[:, m:m + 1], (q1raw, q2raw)[m][:].rearrange("p k n -> p (k n)"), AX.X, ALU.max,
                                  apply_absolute_value=True).then_inc(sem("wmax_part"), 1)

            def weight_scale():
                dve.wait_ge(sem("wmax_ready"), 1)
                chain(dve.reciprocal(ws[:, 4:6], ws[:, 2:4]))
                dve.tensor_scalar(ws[:, 6:8], ws[:, 4:6], Q, None, ALU.mult).then_inc(sem("wscale_ready"), 1)
                dve.wait_ge(sem("wscale_ready"), 1)
                chain(dve.tensor_scalar(ws[:, 4:6], ws[:, 2:4], 1.0 / (Q * Q), None, ALU.mult))

            def add_routed(v):
                dve.wait_ge(sem("fo_ready"), v + 1)
                dve.tensor_tensor(x[:, 2 * v:2 * v + 2, :], bank[v if v < 2 else 4 + v][:].rearrange("p (t c) -> p t c", t=2),
                                  x[:, 2 * v:2 * v + 2, :], ALU.add).then_inc(sem("x1_ready"), 1)

            def expert_h(q, o, j):
                wait(dve, sem("r_ready"), 4 * q + j + 1)
                dve.scalar_tensor_tensor(out=hx[:, o % 2, j, :], in0=bank[j][:], scalar=0.0, in1=rl[:, j % 2, :],
                                         op0=ALU.max, op1=ALU.mult).then_inc(sem("h0_ready"), 1)

            for j in range(4):
                expert_h(0, 0, j)
                if j % 2:
                    add_shared(2 + j // 2)
            expert_h(1, 1, 0)
            expert_h(1, 1, 1)
            dve.wait_ge(sem("G_turned"), 4)

            def expert_steps(i, last):
                for o in range(4):
                    q = 4 * i + o
                    n, l, blk, p = NBLK + q, 1 + o % 2, 2 * i + o // 2, o % 2
                    wkv_kup(n, l, blk, p)
                    for j in range(4):
                        if j < 2 and not (last and o == 3):
                            expert_h(q + 1, o + 1, j + 2)
                        if j >= 2 and not (last and o >= 2):
                            expert_h(q + 2, o + 2, j - 2)
                        wkv_scan(n, l, blk, p, j)
                        if last and o == 3 and j == 2:
                            add_routed(0)
                            add_routed(1)
                        if j == 2 and not (o == 0 and isinstance(i, int) and i == 0):
                            wkv_gain(n - 1, 1 + (o - 1) % 2, 2 * i + (o - 1) // 2, 1 - p)
                    if isinstance(i, int) and i == 0:
                        (lambda: weight_max(0), lambda: weight_max(1), weight_scale, lambda: None)[o]()

            expert_steps(0, False)
            with dve.Fori(1, EG // 2 - 1) as i:
                expert_steps(i, False)
            expert_steps(EG // 2 - 1, True)

            def row_scales(s):
                t = slice(TH * s, TH * s + TH)
                dve.wait_ge(sem("cond_ready"), 6 + 2 * s)
                chain(dve.tensor_reduce(st[:, 0, t], cond[:, t, :], AX.X, ALU.max, apply_absolute_value=True))
                chain(dve.reciprocal(st[:, 1, t], st[:, 0, t]))
                dve.tensor_scalar(st[:, 2, t], st[:, 1, t], Q, None, ALU.mult).then_inc(sem("row_scale"), 1)
                chain(dve.tensor_scalar(st[:, 3, t], st[:, 0, t], ws[:, 4:5], None, ALU.mult))

            def l1_pre(t):
                p = t % 2
                dve.wait_ge(sem("m1_ready"), t + 1)
                wait(dve, sem("gelu_ready"), t - 1)
                for h in range(2):
                    ins = dve.scalar_tensor_tensor(out=xp[:, p, 512 * h:512 * h + 512], in0=bank[2 * p + h][:],
                                                   scalar=st[:, 3, t:t + 1], in1=b1bc[:, 512 * h:512 * h + 512],
                                                   op0=ALU.mult, op1=ALU.add)
                ins.then_inc(sem("pre_ready"), 1)

            def l1_scales(t):
                p = t % 2
                wait(dve, sem("q2_ready"), t - 1)
                dve.wait_ge(sem("gelu_ready"), t + 1)
                chain(dve.tensor_reduce(pt[:, 0, p:p + 1], gl[:, p, :], AX.X, ALU.max, apply_absolute_value=True))
                chain(dve.reciprocal(pt[:, 1, p:p + 1], pt[:, 0, p:p + 1]))
                dve.tensor_scalar(pt[:, 3, p:p + 1], pt[:, 0, p:p + 1], ws[:, 5:6], None, ALU.mult)
                dve.tensor_scalar(pt[:, 2, p:p + 1], pt[:, 1, p:p + 1], Q, None, ALU.mult).then_inc(sem("q2_scale"), 1)

            def l1_out(t):
                dve.wait_ge(sem("m2_ready"), t + 1)
                dve.wait_ge(sem("xb_ready"), t + 1)
                dve.scalar_tensor_tensor(out=x[:, t, :], in0=bank[7][:, 0:C], scalar=pt[:, 3, t % 2:t % 2 + 1],
                                         in1=x[:, t, :], op0=ALU.mult, op1=ALU.add).then_inc(sem("x2_ready"), 1)

            dve.wait_ge(sem("qb_in"), 32)
            make_cond(1, 0)
            make_cond(1, 1)
            row_scales(0)
            for t in range(-3, NT + 1):
                if 0 <= t + 1 < NT and t != 0:
                    l1_pre(t + 1)
                if t == -2:
                    add_routed(2)
                    add_routed(3)
                if t == -1:
                    make_cond(1, 2)
                    make_cond(1, 3)
                if 0 <= t < NT:
                    l1_scales(t)
                if t == 0:
                    l1_pre(1)
                    row_scales(1)
                if t == 3:
                    dve.wait_ge(sem("rt_in"), 16)
                    chain(dve.tensor_copy(rthi[:], rtraw[:]))
                    dve.tensor_tensor(rtlo[:], rtraw[:], rthi[:].bitcast(F32), ALU.subtract).then_inc(sem("rt_split"), 1)
                if t == 2:
                    wkv_gain(3 * NBLK - 1, 2, NBLK - 1, 1)
                if t >= 1:
                    l1_out(t - 1)
                if t == NT - 1:
                    make_cond(2, 0)
                    make_cond(2, 1)

            cond_low(4, 0, 0)
            cond_low(4, 0, 1)
            make_cond(2, 2)
            make_cond(2, 3)
            cond_low(4, 1, 0)
            cond_low(4, 1, 1)
            lg = bank[4][:, 0:NT * E2].rearrange("p (t e) -> p t e", e=E2)

            def per_token(i):
                return r2[:, i, :, 0:1].to_broadcast([P, NT, E2])

            def shift_logits():
                dve.wait_ge(sem("logit_ready"), 1)
                chain(dve.tensor_reduce(r2[:, 0, :, 0:1], lg, AX.X, ALU.max))
                dve.tensor_tensor(r2[:, 1, :, :], lg, per_token(0), ALU.subtract).then_inc(sem("lsub_ready"), 1)

            sq = [r2c[:, i, :, :].rearrange("p t (g h) -> p t g h", g=E2) for i in range(2)]

            def top2_ranks():
                ranks(r2[:, 4, :, :], low8, E2, sq[0], sq[1], r2[:, 5, :, :])

            def top2_weights():
                chain(dve.tensor_scalar(r2[:, 5, :, :], r2[:, 5, :, :], 2.0, None, ALU.is_lt))
                chain(dve.tensor_tensor(r2[:, 6, :, :], r2[:, 5, :, :], r2[:, 4, :, :], ALU.mult))
                chain(dve.tensor_reduce(r2[:, 7, :, 0:1], r2[:, 6, :, :], AX.X, ALU.add))
                chain(dve.reciprocal(r2[:, 8, :, 0:1], r2[:, 7, :, 0:1]))
                chain(dve.tensor_tensor(cw2[:], r2[:, 6, :, :], per_token(8), ALU.mult))

            def softmax():
                dve.wait_ge(sem("lexp_ready"), 1)
                chain(dve.tensor_reduce(r2[:, 2, :, 0:1], r2[:, 1, :, :], AX.X, ALU.add))
                chain(dve.reciprocal(r2[:, 3, :, 0:1], r2[:, 2, :, 0:1]))
                chain(dve.tensor_tensor(r2[:, 4, :, :], r2[:, 1, :, :], per_token(3), ALU.mult))

            routing = {(0, 2): shift_logits, (1, 0): softmax, (1, 1): top2_ranks, (1, 2): top2_weights}

            def ternary_sum(m):
                dve.wait_ge(sem("t_in"), 16 * m + 16)
                dve.tensor_reduce(ws[:, 9 + m:10 + m], traw[:], AX.X, ALU.add, apply_absolute_value=True).then_inc(sem("tsum_part"), 1)

            def ternary_round(m):
                dve.wait_ge(sem("tsum_ready"), m + 1)
                chain(dve.tensor_scalar(ws[:, 15 + m:16 + m], ws[:, 12 + m:13 + m], 1.0 / (C * HID), 1e-5, ALU.mult, ALU.max))
                chain(dve.reciprocal(ws[:, 18 + m:19 + m], ws[:, 15 + m:16 + m]))
                dve.tensor_scalar(traw[:], traw[:], ws[:, 18 + m:19 + m], ROUND, ALU.mult, ALU.add).then_inc(sem("t_round"), 1)

            def ternary_clip(m):
                dve.wait_ge(sem("t_round"), m + 1)
                dve.tensor_scalar(traw[:], traw[:], ROUND + 1.0, ROUND - 1.0, ALU.min, ALU.max).then_inc(sem("t_clipped"), 1)

            def glu_h(e, s, j):
                u, p = 8 * e + 4 * s + j, j % 2
                wait(dve, sem("sl_ready"), u + 1)
                dve.tensor_tensor(hh[:, p, :], bank[2 * p + 1][:], sl[:, p, :], ALU.mult).then_inc(sem("hh_ready"), 1)
                wait(dve, sem("d_done"), 8 * e - 4 + 4 * s)
                wait(dve, sem("hh_ready"), u + 1)
                dve.tensor_copy(hhi[:, s, j, :], hh[:, p, :]).then_inc(sem("hhi_ready"), 1)
                wait(dve, sem("hhi_ready"), u + 1)
                dve.tensor_tensor(hlo[:, s, j, :], hh[:, p, :], hhi[:, s, j, :].bitcast(F32), ALU.subtract
                                  ).then_inc(sem("hlo_ready"), 1)

            cw2f = cw2[:].rearrange("p t e -> p (t e)")

            def glu_step(e, p, first=False):
                n = 3 * NBLK + e
                for s in range(2):
                    for j in range(4):
                        glu_h(e, s, j)
                        if s == 0 and j == 0:
                            wkv_kup(n, 3, e, p)
                        if first and (s, j) in routing:
                            routing[s, j]()
                        if j % 2 and not first:
                            wkv_scan(n, 3, e, p, 2 * s + j // 2)
                        if isinstance(e, int) and 1 <= e <= 3 and (s, j) == (0, 2):
                            ternary_round(e - 1)
                        if isinstance(e, int) and 1 <= e <= 3 and (s, j) == (1, 0):
                            ternary_clip(e - 1)
                for t in range(NT):
                    if t == TH and not first:
                        wkv_gain(n - 1, 3, e - 1, 1 - p)
                    v = 8 * e + t
                    wait(dve, sem("d_done"), v + 1)
                    dve.scalar_tensor_tensor(out=x[:, t, :], in0=bank[4 + t % 4][:, 0:C], scalar=col(cw2f, E2 * t + e),
                                             in1=x[:, t, :], op0=ALU.mult, op1=ALU.add).then_inc(sem("acc_ready"), 1)
                if first:
                    for part in range(4):
                        wkv_scan(n, 3, e, p, part)

            for e in range(4):
                glu_step(e, e % 2, e == 0)
                if e < 3:
                    ternary_sum(e)
            with dve.Fori(2, E2 // 2) as i:
                glu_step(2 * i, 0)
                glu_step(2 * i + 1, 1)

            def rms_max(s):
                t = slice(TH * s, TH * s + TH)
                dve.wait_ge(sem("cond_ready"), 14 + 2 * s)
                dve.tensor_reduce(st[:, 6, t], cond[:, t, :], AX.X, ALU.max, apply_absolute_value=True
                                  ).then_inc(sem("c3_max"), 1)

            def rms_scales(s):
                t = slice(TH * s, TH * s + TH)
                dve.wait_ge(sem("c3_stat"), s + 1)
                chain(dve.tensor_scalar(st[:, 7, t], st[:, 7, t], 1e-5, None, ALU.max))
                dve.tensor_scalar(st[:, 9, t], st[:, 7, t], ws[:, 21:22], None, ALU.mult)
                dve.tensor_scalar(st[:, 10, t], st[:, 7, t], ws[:, 22:23], None, ALU.mult)
                chain(dve.reciprocal(st[:, 8, t], st[:, 7, t]))
                dve.scalar_tensor_tensor(out=st[:, 8, t], in0=st[:, 8, t], scalar=Q, in1=st[:, 5, t],
                                         op0=ALU.mult, op1=ALU.mult).then_inc(sem("c3_scale"), 1)

            make_cond(3, 0)
            make_cond(3, 1)
            rms_max(0)
            chain(dve.tensor_scalar(ws[:, 21:24], ws[:, 15:18], 1.0 / Q, None, ALU.mult))
            wkv_gain(4 * NBLK - 1, 3, NBLK - 1, 1)
            rms_scales(0)
            make_cond(3, 2)
            make_cond(3, 3)
            rms_max(1)

            def l3_h(t):
                p = t % 2
                wait(dve, sem("q2t_ready3"), 2 * t - 4)
                dve.wait_ge(sem("c3_scale"), t // TH + 1)
                for h in range(2):
                    dve.wait_ge(sem("silu3_ready"), 2 * t + h + 1)
                    dve.scalar_tensor_tensor(out=gl[:, t % 3, 512 * h:512 * h + 512], in0=bank[2 + h][:],
                                                   scalar=st[:, 10, t:t + 1], in1=xp[:, p, 512 * h:512 * h + 512],
                                                   op0=ALU.mult, op1=ALU.mult).then_inc(sem("h3_ready"), 1)

            def l3_max(t):
                p = t % 2
                dve.wait_ge(sem("h3_ready"), 2 * t + 2)
                dve.tensor_reduce(pt[:, 6, p:p + 1], gl[:, t % 3, :], AX.X, ALU.max, apply_absolute_value=True
                                  ).then_inc(sem("h3_max"), 1)

            def l3_quant(t):
                p = t % 2
                dve.wait_ge(sem("h3_stat"), t + 1)
                chain(dve.reciprocal(pt[:, 1, p:p + 1], st[:, 0, t:t + 1]))
                chain(dve.tensor_scalar(pt[:, 2, p:p + 1], pt[:, 1, p:p + 1], pt[:, 5, p:p + 1], Q, ALU.mult, ALU.mult))
                dve.tensor_scalar(gl[:, t % 3, :], gl[:, t % 3, :], pt[:, 2, p:p + 1], ROUND, ALU.mult, ALU.add
                                  ).then_inc(sem("q23_ready"), 1)

            def l3_out(t):
                dve.wait_ge(sem("m2_ready3"), t + 1)
                dve.wait_ge(sem("h3_scale"), t + 1)
                dve.scalar_tensor_tensor(out=x[:, t, :], in0=bank[7][:, 0:C], scalar=st[:, 1, t:t + 1],
                                         in1=x[:, t, :], op0=ALU.mult, op1=ALU.add).then_inc(sem("x4_ready"), 1)

            for t in range(-1, NT + 1):
                if 0 <= t + 1 < NT:
                    l3_h(t + 1)
                    l3_max(t + 1)
                if t == -1:
                    rms_scales(1)
                if 0 <= t < NT:
                    l3_quant(t)
                if t >= 1:
                    l3_out(t - 1)

        @block.tensor
        def _(pe):
            def mm3(out, lhs, rhs, start, stop):
                pe.matmul(out, lhs[0], rhs[0], start=start, stop=False)
                pe.matmul(out, lhs[0], rhs[1], start=False, stop=False)
                return pe.matmul(out, lhs[1], rhs[0], start=False, stop=stop)

            def turn_gain(l, b):
                units = {0: 2 * b + 2, 1: 2 * NBLK if b < 2 else 3 * NBLK - 1, 3: 3 * NBLK + 2 * b + 2}
                pe.wait_ge(sem("G_ready"), units.get(l, DONE[l]))
                if b >= 2:
                    pe.wait_ge(sem("cond_ready"), 4 * l + b - 1)
                for u in range(2):
                    for k in range(KC):
                        ins = pe.transpose(gain_bank(l, b)[:, u * C + k * P:u * C + k * P + P],
                                           GT[:, l % 2, 2 * b + k, u * P:u * P + P], ident[:])
                ins.then_inc(sem("G_turned"), 1)

            def turn_cond(l, n0, s):
                pe.wait_ge(sem("cond_ready"), 4 * l + 2 * s + 2)
                for k in range(KC):
                    n = n0 + 2 * s + k
                    wait(pe, sem("cT_low"), n - 1)
                    for j in range(TH):
                        ins = pe.transpose(cond_bank(n)[:, j * P:j * P + P], cond[:, TH * s + j, k * P:k * P + P], ident[:])
                    ins.then_inc(sem("cT_ready"), 1)

            def cT(k, a, b):
                return cThi[:, k, a:b], cTlo[:, k, a:b]

            pe.wait_ge(sem("ident_ready"), 1)
            ins_back = [None]

            def scores_up(out, n, high, low, s):
                for k in range(KC):
                    ins = mm3(out[0:n, :], (high[:, k, 0:n], low[:, k, 0:n]), cT(k, HALF * s, HALF * s + HALF),
                              k == 0, k == KC - 1)
                ins.then_inc(sem("sT_ready"), 1)

            def scores_back(out, n, done):
                pe.wait_ge(sem("sT_copied"), done)
                for t in range(NT):
                    ins_back[0] = pe.transpose(out[:, t * n:t * n + n], sT(n)[:, t * P:t * P + P], ident[0:n, 0:n])

            def shared_up(u):
                s, j = u // 4, u % 4
                wait(pe, sem("sh_ready"), u - 3)
                for k in range(KC):
                    w = slice(E0 + LAT + j * P, E0 + LAT + j * P + P)
                    ins = mm3(bank[u % 4][:], (sm_hi[:, k, w], sm_lo[:, k, w]), cT(k, HALF * s, HALF * s + HALF),
                              k == 0, k == KC - 1)
                ins.then_inc(sem("sz_ready"), 1)

            def latent(s):
                for k in range(KC):
                    w = slice(E0, E0 + LAT)
                    ins = mm3(bank[5 + 2 * s][:], (sm_hi[:, k, w], sm_lo[:, k, w]), cT(k, HALF * s, HALF * s + HALF),
                              k == 0, k == KC - 1)
                ins.then_inc(sem("xl_ready"), 1)

            def shared_down(v):
                if v == 0:
                    pe.wait_ge(sem("down_in"), 16)
                for half in range(2):
                    t = 2 * (v % 2) + half
                    for j in range(4):
                        ins = pe.matmul(down_bank(v)[:, half * C:half * C + C], hx[:, v // 2, j, t * P:t * P + P],
                                        downw[:, j, :], start=(j == 0), stop=(j == 3))
                ins.then_inc(sem("sd_ready"), 1)

            turn_gain(0, 0)
            turn_gain(0, 1)
            turn_cond(0, 0, 0)
            pe.wait_ge(sem("sm_low"), 1)
            pe.wait_ge(sem("cT_low"), 2)
            turn_gain(0, 2)
            scores_up(bank[6], E0, sm_hi, sm_lo, 0)
            latent(0)
            shared_up(0)
            turn_gain(0, 3)
            shared_up(1)
            pe.wait_ge(sem("sT_copied"), 1)
            pe.wait_ge(sem("xl_low"), 1)
            turn_cond(0, 0, 1)
            shared_up(2)
            pe.wait_ge(sem("cT_low"), 4)
            scores_up(bank[4], E0, sm_hi, sm_lo, 1)
            latent(1)
            shared_up(3)
            shared_up(4)
            scores_back(bank[4], E0, 2)
            ins_back[0].then_inc(sem("gate_ready"), 1)
            for u in range(5, 8):
                shared_up(u)
            shared_down(0)
            shared_down(1)

            def expert_z(q, i, o, j):
                slot, t = (o // 2) % 2, TH * (o % 2) + j
                wait(pe, sem("h0_ready"), 4 * q - 3 + j)
                if j == 0 and o % 2 == 0:
                    wait(pe, sem("w1_split"), 2 * i + o // 2 + 1)
                w = (w1hi[:, slot, :], w1lo[:, slot, :])
                mm3(bank[j][:], (xlhi[:, t * P:t * P + P], xllo[:, t * P:t * P + P]), w, True, True).then_inc(sem("z_ready"), 1)

            def expert_turn(q, o, e):
                if e == 0:
                    wait(pe, sem("h0_ready"), 4 * q + 4)
                wait(pe, sem("hT_ready"), 4 * q + e - 1)
                for j in range(4):
                    ins = pe.transpose(bank[6 + e % 2][:, j * P:j * P + P], hx[:, o % 2, j, e * P:e * P + P], ident[:])
                ins.then_inc(sem("t_ready"), 1)

            def expert_y(q, i, o, e):
                slot = o // 2
                if o % 2 == 0 and e == 0:
                    pe.wait_ge(sem(f"w2_in{slot}"), 16 * (i + 1))
                wait(pe, sem("hT_ready"), 4 * q + e + 1)
                start = isinstance(i, int) and i == 0 and o < 2 and e == 0
                stop = isinstance(i, int) and i == EG // 2 - 1 and o >= 2 and e == 3
                pe.matmul(bank[4 + o % 2][:], w2raw[:, slot, e, :], hT[:, e % 2, :], start=start, stop=stop,
                          skip_group_check=True).then_inc(sem("y_done"), 1)

            pe.wait_ge(sem("sh_ready"), 8)
            pe.wait_ge(sem("xl_low"), 2)
            for j in range(4):
                expert_z(0, 0, 0, j)
            pe.wait_ge(sem("score_ready"), 1)
            shared_down(2)
            shared_down(3)
            expert_z(1, 0, 1, 0)
            expert_z(1, 0, 1, 1)
            pe.wait_ge(sem("sx_done"), 4)

            def expert_steps(i, last):
                for o in range(4):
                    q = 4 * i + o
                    z = (lambda j: None) if last and o == 3 else (lambda j: expert_z(q + 1, i, o + 1, j))
                    zz = (lambda j: None) if last and o >= 2 else (lambda j: expert_z(q + 2, i, o + 2, j))
                    expert_turn(q, o, 0)
                    z(2)
                    expert_turn(q, o, 1)
                    expert_y(q, i, o, 0)
                    z(3)
                    expert_turn(q, o, 2)
                    expert_y(q, i, o, 1)
                    if last and o == 3:
                        latent_out(0)
                        turn_gain(1, 0)
                        turn_gain(1, 1)
                    expert_turn(q, o, 3)
                    zz(0)
                    expert_y(q, i, o, 2)
                    zz(1)
                    expert_y(q, i, o, 3)

            def latent_out(s):
                if s == 0:
                    pe.wait_ge(sem("fc2_in"), 16)
                    pe.wait_ge(sem("h0_ready"), 4 * 2 * EG)
                pe.wait_ge(sem("ylat_ready"), s + 1)
                for v in range(2 * s, 2 * s + 2):
                    for half in range(2):
                        t = 2 * (v % 2) + half
                        ins = pe.matmul(bank[v if v < 2 else 4 + v][:, half * C:half * C + C],
                                        ylat[:, s, t * P:t * P + P], fc2w[:], start=True, stop=True)
                    ins.then_inc(sem("fo_ready"), 1)

            expert_steps(0, False)
            with pe.Fori(1, EG // 2 - 1) as i:
                expert_steps(i, False)
            expert_steps(EG // 2 - 1, True)
            latent_out(1)

            turn_gain(1, 2)
            pe.wait_ge(sem("x1_ready"), 3)
            turn_gain(1, 3)
            pe.wait_ge(sem("q_quant"), 2)

            def turn_rows(t, tag, quant):
                pe.wait_ge(sem(quant), t + 1)
                wait(pe, sem("q1T" + tag + "_ready"), t)
                for k in range(KC):
                    ins = pe.transpose(bank[4][:, k * P:k * P + P], qf[:, t % 2, k * P:k * P + P], ident[:])
                ins.then_inc(sem("q1t" + tag + "_ready"), 1)

            def first(t, tag, weights, banks):
                p = t % 2
                pe.wait_ge(sem("q1T" + tag + "_ready"), t + 1)
                if not tag:
                    wait(pe, sem("pre_ready"), t - 1)
                for n, (b, w) in enumerate(zip(banks(p), weights)):
                    if tag and n % 2 == 0:
                        wait(pe, sem("h3_ready"), 2 * t + n // 2 - 1)
                    for k in range(KC):
                        ins = pe.matmul(bank[b][:], qT[:, p, k, :], w(k), start=(k == 0), stop=(k == KC - 1))
                    if n % 2:
                        ins.then_inc(sem("m1" + tag + "_ready"), 1)

            def turn_hidden(t, tag, quant):
                pe.wait_ge(sem(quant), t + 1)
                for h in range(2):
                    wait(pe, sem("q2T_ready" + tag), 2 * t - 1 + h)
                    for j in range(4):
                        c = 4 * h + j
                        ins = pe.transpose(bank[5 + h][:, j * P:j * P + P],
                                           gl[:, t % (3 if tag else 2), c * P:c * P + P], ident[:])
                    ins.then_inc(sem("q2t_ready" + tag), 1)

            def second(t, tag, out_ready, weight):
                wait(pe, sem(out_ready), t)
                for c in range(8):
                    if c % 4 == 0:
                        pe.wait_ge(sem("q2T_ready" + tag), 2 * t + c // 4 + 1)
                    ins = pe.matmul(bank[7][:, 0:C], q2T[:, t % 2, c, :], weight(c), start=(c == 0), stop=(c == 7))
                ins.then_inc(sem("m2_ready" + tag), 1)

            w_first = [lambda k, h=h: q1w[:, k, 512 * h:512 * h + 512] for h in range(2)]
            turn_rows(0, "", "q1_ready")
            for t in range(-2, NT):
                if t + 2 < NT:
                    first(t + 2, "", w_first, lambda p: (2 * p, 2 * p + 1))
                if t == 0:
                    pe.wait_ge(sem("cond_ready"), 8)
                    pe.wait_ge(sem("x1_ready"), 4)
                if t == NT - 2:
                    pe.wait_ge(sem("pre_ready"), NT)
                    turn_gain(2, 0)
                    turn_gain(2, 1)
                if t >= 0:
                    turn_hidden(t, "", "q2_ready")
                if t + 3 < NT:
                    turn_rows(t + 3, "", "q1_ready")
                if t >= 0:
                    second(t, "", "x2_ready", lambda c: q2w[:, c, :])

            turn_cond(2, 4, 0)
            def glu_up(e, s, j):
                u, p = 8 * e + 4 * s + j, j % 2
                wait(pe, sem("hh_ready"), u - 1)
                for up in range(2):
                    for k in range(KC):
                        w = slice(up * I2 + j * P, up * I2 + j * P + P)
                        ins = mm3(bank[2 * p + up][:], (guhi[:, k, w], gulo[:, k, w]),
                                  cT(k, HALF * s, HALF * s + HALF), k == 0, k == KC - 1)
                ins.then_inc(sem("gu_done"), 1)

            def glu_down(e):
                pe.wait_ge(sem("dn_split"), e + 1)
                for s in range(2):
                    wait(pe, sem("hlo_ready"), 8 * e + 4 * s + 4)
                    for t in range(TH):
                        v = 8 * e + 4 * s + t
                        wait(pe, sem("acc_ready"), v - 3)
                        for j in range(4):
                            ins = mm3(bank[4 + t][:, 0:C], (hhi[:, s, j, t * P:t * P + P], hlo[:, s, j, t * P:t * P + P]),
                                      (dnhi[:, j, :], dnlo[:, j, :]), j == 0, j == 3)
                        ins.then_inc(sem("d_done"), 1)

            pe.wait_ge(sem("q1T_ready"), NT)
            turn_gain(2, 2)
            pe.wait_ge(sem("rt_split"), 1)
            pe.wait_ge(sem("cT_low"), 6)
            scores_up(bank[0], E2, rthi, rtlo, 0)
            pe.wait_ge(sem("x2_ready"), NT)
            turn_gain(2, 3)
            pe.wait_ge(sem("gu_split"), 1)
            pe.wait_ge(sem("sT_copied"), 3)
            glu_up(0, 0, 0)
            pe.wait_ge(sem("q2T_ready"), 2 * NT)
            turn_cond(2, 4, 1)
            glu_up(0, 0, 1)
            pe.wait_ge(sem("cT_low"), 8)
            scores_up(bank[5], E2, rthi, rtlo, 1)
            glu_up(0, 0, 2)
            scores_back(bank[4], E2, 4)
            ins_back[0].then_inc(sem("logit_ready"), 1)
            glu_up(0, 0, 3)
            for j in range(4):
                glu_up(0, 1, j)
            pe.wait_ge(sem("lsub_ready"), 1)
            glu_down(0)
            with pe.Fori(1, E2) as e:
                pe.wait_ge(sem("gu_split"), e + 1)
                for s in range(2):
                    for j in range(4):
                        glu_up(e, s, j)
                glu_down(e)

            for b in range(B):
                turn_gain(3, b)
            pe.wait_ge(sem("t_quant"), 3)
            w_first = [lambda k, m=m, h=h: tw[:, m, HID * k + 512 * h:HID * k + 512 * h + 512]
                       for h in range(2) for m in range(2)]
            turn_rows(0, "3", "q13_ready")
            for t in range(-2, NT):
                if t + 2 < NT:
                    first(t + 2, "3", w_first, lambda p: (0, 2, 1, 3))
                if t == 0:
                    pe.wait_ge(sem("cond_ready"), 16)
                if t >= 0:
                    turn_hidden(t, "3", "q23_ready")
                if t + 3 < NT:
                    turn_rows(t + 3, "3", "q13_ready")
                if t >= 0:
                    second(t, "3", "x4_ready", lambda c: tw[:, 2, C * c:C * c + C])


def kernel(x, fside_BxSxS_0, cond_512, L0_cond_w, L0_cond_u, L0_ffn_gate_w, L0_ffn_gate_bias, L0_ffn_fc1_w,
           L0_ffn_fc2_w, L0_ffn_w1, L0_ffn_w2, L0_ffn_shared_up_w, L0_ffn_shared_down_w, L1_cond_w, L1_cond_u,
           L1_ffn_W1, L1_ffn_B1, L1_ffn_W2, L1_ffn_B2, L2_cond_w, L2_cond_u, L2_ffn_gate_weight,
           L2_ffn_gate_up_proj, L2_ffn_down_proj, L3_cond_w, L3_cond_u, L3_ffn_w1, L3_ffn_w2, L3_ffn_w3):
    import numpy as np
    import concourse.bacc as bacc
    from concourse.bass_utils import run_bass_kernel_spmd

    def rows(w, inner):
        w = np.asarray(w).T
        return w.reshape(inner // P, P, w.shape[1]).transpose(1, 0, 2)

    def spread(v):
        v = np.asarray(v).reshape(1, -1)
        return np.broadcast_to(v, (P, v.shape[1]))

    def channels(*vs):
        return np.stack([np.asarray(v).reshape(KC, P).T for v in vs], axis=1)

    xs = np.asarray(x)
    small = np.concatenate([rows(L0_ffn_gate_w, C), rows(L0_ffn_fc1_w, C), rows(L0_ffn_shared_up_w, C)], axis=2)
    gu = np.asarray(L2_ffn_gate_up_proj).transpose(0, 2, 1).reshape(E2, KC, P, 2 * I2).transpose(0, 2, 1, 3)
    dn = np.asarray(L2_ffn_down_proj).transpose(0, 2, 1).reshape(E2, I2 // P, P, C).transpose(0, 2, 1, 3)
    ins = {
        "x": xs.reshape(NT, P, C).transpose(1, 0, 2),
        "kt": np.asarray(fside_BxSxS_0).reshape(B, S, KC, P).transpose(3, 0, 2, 1).reshape(P, NBLK, S),
        "te": spread(cond_512).reshape(P, B, 64),
        "w": channels(L0_cond_w, L1_cond_w, L2_cond_w, L3_cond_w),
        "u": channels(L0_cond_u, L1_cond_u, L2_cond_u, L3_cond_u),
        "sm": small,
        "gbias": spread(L0_ffn_gate_bias),
        "down": rows(L0_ffn_shared_down_w, SH),
        "fc2": np.asarray(L0_ffn_fc2_w).T,
        "w1": np.asarray(L0_ffn_w1).transpose(2, 0, 1).reshape(P, EG, 4 * INTER),
        "w2": np.asarray(L0_ffn_w2).transpose(2, 0, 1).reshape(P, EG, 4, LAT),
        "q1": rows(L1_ffn_W1, C), "q1b": spread(L1_ffn_B1),
        "q2": rows(L1_ffn_W2, HID), "q2b": spread(L1_ffn_B2),
        "rt": rows(L2_ffn_gate_weight, C),
        "gu": gu, "dn": dn,
        "t1": rows(L3_ffn_w1, C).reshape(P, -1), "t2": rows(L3_ffn_w2, C).reshape(P, -1),
        "t3": rows(L3_ffn_w3, HID).reshape(P, -1),
    }
    nc = bacc.Bacc("TRN2", target_bir_lowering=False, num_devices=1)
    arrays, args = {}, []
    for name, a in ins.items():
        a = np.ascontiguousarray(a)
        arrays["in_" + name] = a
        args.append(nc.dram_tensor("in_" + name, a.shape, mybir.dt.from_np(a.dtype), kind="ExternalInput").ap())
    out = nc.dram_tensor("out_x", (P, NT, C), F32, kind="ExternalOutput").ap()
    build(nc, *args, out)
    got = run_bass_kernel_spmd(nc, [arrays], core_ids=[0]).results[0]["out_x"]
    return np.ascontiguousarray(got.transpose(1, 0, 2)).reshape(xs.shape)
```
